# Optimizing a Trainium2 kernel written in Bass

```python
import numpy as np
import jax
import jax.numpy as jnp

def _softmax(x, axis=-1):
    return jax.nn.softmax(x, axis=axis)

def _gelu(x):
    return jax.nn.gelu(x, approximate=True)

def _silu(x):
    return jax.nn.silu(x)

def _sigmoid(x):
    return jax.nn.sigmoid(x)

def _layernorm(x, axis=-1, eps=1e-05):
    m = jnp.mean(x, axis=axis, keepdims=True)
    v = jnp.var(x, axis=axis, keepdims=True)
    return (x - m) / jnp.sqrt(v + eps)

def _scatter_add(tgt, idx, src, axis=0):
    return tgt.at[idx].add(src)

def _segment_sum(src, seg, n):
    return jax.ops.segment_sum(src, seg, n)
kernel_name = 'mk_gps_d1_gnn_r8_4be70e'

def setup_inputs(seed: int=0):
    np.random.seed(seed)
    _w = jnp.asarray

    def _rec_inputs():
        import jax
        import jax.numpy as jnp
        _gk = jax.random.key(seed)
        x = -8.776e-05 + 1 * jax.random.normal(jax.random.fold_in(_gk, 1), (6250, 256), jnp.float32)
        _s = jax.random.randint(jax.random.fold_in(_gk, 2), (100000,), 0, 6250, jnp.int32)
        _d = jax.random.randint(jax.random.fold_in(_gk, 3), (100000,), 0, 6250, jnp.int32)
        _loop = jnp.arange(6250, dtype=jnp.int32)
        src = jnp.concatenate([_s, _d, _loop])
        dst = jnp.concatenate([_d, _s, _loop])
        _o = jnp.argsort(dst, stable=True)
        src = src[_o]
        dst = dst[_o]
        edge_attr_4 = 0.000126197 + 0.999763 * jax.random.normal(jax.random.fold_in(_gk, 11), (206250, 4), jnp.float32)
        edge_attr_8 = jax.random.uniform(jax.random.fold_in(_gk, 12), (206250, 8), jnp.float32, 0.0, 1)
        return (x, src, dst, edge_attr_4, edge_attr_8)
    x, src, dst, edge_attr_4, edge_attr_8 = _rec_inputs()

    def _L0_gnn_setup():
        import jax, jax.numpy as jnp
        import numpy as np
        N_NODES = 2500
        N_EDGES = 40000
        MUL = 64
        NUM_BASIS = 8
        INV_SQRT3 = 0.5773502691896258
        EPS = 1e-05
        key = jax.random.key(seed)
        k = jax.random.split(key, 16)
        return {'node_hiddens': jax.random.normal(k[0], (N_NODES, 4 * MUL), dtype=jnp.float32), 'edge_attr': jax.random.uniform(k[1], (N_EDGES, NUM_BASIS), dtype=jnp.float32), 'edge_sh': jax.random.normal(k[2], (N_EDGES, 4), dtype=jnp.float32), 'w1_s': jax.random.normal(k[3], (MUL, MUL), dtype=jnp.float32), 'w1_v': jax.random.normal(k[4], (MUL, MUL), dtype=jnp.float32), 'wsc_s': jax.random.normal(k[5], (MUL, MUL), dtype=jnp.float32), 'wsc_v': jax.random.normal(k[6], (MUL, MUL), dtype=jnp.float32), 'w2_s': jax.random.normal(k[7], (2 * MUL, MUL), dtype=jnp.float32), 'w2_v': jax.random.normal(k[8], (2 * MUL, MUL), dtype=jnp.float32), 'fc_w1': jax.random.normal(k[9], (NUM_BASIS, 64), dtype=jnp.float32), 'fc_w2': jax.random.normal(k[10], (64, 64), dtype=jnp.float32), 'fc_w3': jax.random.normal(k[11], (64, 4 * MUL), dtype=jnp.float32), 'g_s': jnp.ones((MUL,), dtype=jnp.float32), 'g_v': jnp.ones((MUL,), dtype=jnp.float32), 'edge_index': jax.random.randint(k[12], (2, N_EDGES), 0, N_NODES)}
    _L0_gnn_all = _L0_gnn_setup()
    _L0_gnn_in = {k: v for k, v in _L0_gnn_all.items() if k in ('w1_s', 'w1_v', 'wsc_s', 'wsc_v', 'w2_s', 'w2_v', 'fc_w1', 'fc_w2', 'fc_w3', 'g_s', 'g_v')}
    del _L0_gnn_all

    def _L0_mix_setup():
        import jax, jax.numpy as jnp
        import numpy as np
        C_CURV = 1.0
        MIN_NORM = 1e-15
        BALL_EPS = 1e-05
        ATT_EPS = 1e-15
        DIM = 32

        def _norm(x):
            return jnp.clip(jnp.linalg.norm(x, axis=-1, keepdims=True), MIN_NORM)

        def proj(x, c):
            maxnorm = (1.0 - BALL_EPS) / jnp.sqrt(c)
            n = _norm(x)
            return jnp.where(n > maxnorm, x / n * maxnorm, x)

        def expmap0(u, c):
            sc = jnp.sqrt(c)
            n = _norm(u)
            return jnp.tanh(sc * n) * u / (sc * n)

        def logmap0(p, c):
            sc = jnp.sqrt(c)
            n = _norm(p)
            return jnp.arctanh(jnp.clip(sc * n, -1.0 + 1e-07, 1.0 - 1e-07)) * p / (sc * n)

        def mobius_add(x, y, c):
            x2 = jnp.sum(x * x, -1, keepdims=True)
            y2 = jnp.sum(y * y, -1, keepdims=True)
            xy = jnp.sum(x * y, -1, keepdims=True)
            num = (1 + 2 * c * xy + c * y2) * x + (1 - c * x2) * y
            den = 1 + 2 * c * xy + c * c * x2 * y2
            return num / jnp.clip(den, MIN_NORM)

        def conv1d(x, w, pad, groups=1):
            return jax.lax.conv_general_dilated(x, w, (1,), [(pad, pad)], dimension_numbers=('NCH', 'OIH', 'NCH'), feature_group_count=groups)

        def batchnorm(x, gamma, beta):
            mean = jnp.mean(x, axis=(0, 2), keepdims=True)
            var = jnp.var(x, axis=(0, 2), keepdims=True)
            xn = (x - mean) * jax.lax.rsqrt(var + 1e-05)
            return gamma[None, :, None] * xn + beta[None, :, None]

        def _reference_tuple_inner(x, w_qkv, bn_gamma, bn_beta, w_dw, w_pw, w_res, b_res):
            c = C_CURV
            h = logmap0(proj(x, c), c)
            h = jnp.transpose(h, (1, 2, 0))
            h = conv1d(h, w_qkv, pad=2)
            h = batchnorm(h, bn_gamma, bn_beta)
            h = jax.nn.relu(jnp.transpose(h, (2, 0, 1)))
            qkv = proj(expmap0(h, c), c)
            t = jnp.transpose(logmap0(proj(qkv, c), c), (1, 2, 0))
            s = conv1d(t, w_dw, pad=2, groups=t.shape[1])
            s = conv1d(s, w_pw, pad=0, groups=t.shape[1] // DIM)
            cat = jnp.concatenate([t, s], axis=1)
            ai = proj(expmap0(jnp.transpose(cat, (2, 0, 1)), c), c)
            t2 = logmap0(proj(ai, c), c)
            L, N, C2 = t2.shape
            g = C2 // (3 * DIM)
            qkv3 = jnp.transpose(t2, (1, 2, 0)).reshape(N, g, 3 * DIM, L)
            q, k, v = jnp.split(qkv3, 3, axis=2)
            q = jax.nn.relu(q)
            k = jax.nn.relu(k)
            vk = jnp.einsum('ngdl,ngel->ngde', v, k)
            out = jnp.einsum('ngde,ngdl->ngdl', vk, q)
            out = out / (jnp.sum(v, -1, keepdims=True) + ATT_EPS)
            out = jnp.transpose(out.reshape(N, g * DIM, L), (2, 0, 1))
            fx_h = proj(expmap0(out, c), c)
            ft = jnp.transpose(logmap0(proj(fx_h, c), c), (1, 2, 0))
            ft = conv1d(ft, w_res, pad=0) + b_res[None, :, None]
            fx = proj(expmap0(jnp.transpose(ft, (2, 0, 1)), c), c)
            residual = mobius_add(fx, x, c)
            return (fx, residual)
        key = jax.random.key(seed)
        ks = jax.random.split(key, 6)
        L, N, C, TD = (256, 16, 256, 256)
        x = jax.random.normal(ks[0], (L, N, C), jnp.float32) * 0.05
        w_qkv = jax.random.normal(ks[1], (3 * TD, C, 5), jnp.float32) / np.sqrt(C * 5)
        bn_gamma = jnp.ones((3 * TD,), jnp.float32)
        bn_beta = jnp.zeros((3 * TD,), jnp.float32)
        w_dw = jax.random.normal(ks[2], (3 * TD, 1, 5), jnp.float32) / np.sqrt(5.0)
        w_pw = jax.random.normal(ks[3], (3 * TD, DIM, 1), jnp.float32) / np.sqrt(DIM)
        w_res = jax.random.normal(ks[4], (C, 2 * TD, 1), jnp.float32) / np.sqrt(2 * TD)
        b_res = jnp.zeros((C,), jnp.float32)
        return {'x': x, 'w_qkv': w_qkv, 'bn_gamma': bn_gamma, 'bn_beta': bn_beta, 'w_dw': w_dw, 'w_pw': w_pw, 'w_res': w_res, 'b_res': b_res}
    _L0_mix_all = _L0_mix_setup()
    _L0_mix_in = {k: v for k, v in _L0_mix_all.items() if k in ('w_qkv', 'bn_gamma', 'bn_beta', 'w_dw', 'w_pw', 'w_res', 'b_res')}
    del _L0_mix_all

    def _L0_ffn_setup():
        import math
        import jax, jax.numpy as jnp
        import numpy as np
        CAPACITY_FACTOR = 1.25
        TOP_K = 2
        LN_EPS = 1e-05

        def _layer_norm(x, gamma, beta):
            mu = jnp.mean(x, axis=-1, keepdims=True)
            var = jnp.var(x, axis=-1, keepdims=True)
            return (x - mu) * jax.lax.rsqrt(var + LN_EPS) * gamma + beta
        key = jax.random.key(seed)
        ks = jax.random.split(key, 4)
        B, S, D, F, E = (8, 512, 256, 512, 8)
        x = jax.random.normal(ks[0], (B, S, D), dtype=jnp.float32)
        Wr = jax.random.normal(ks[1], (D, E), dtype=jnp.float32) / np.sqrt(D)
        br = jnp.zeros((E,), jnp.float32)
        W1 = jax.random.normal(ks[2], (E, D, F), dtype=jnp.float32) / np.sqrt(D)
        b1 = jnp.zeros((E, F), jnp.float32)
        W2 = jax.random.normal(ks[3], (E, F, D), dtype=jnp.float32) / np.sqrt(F)
        b2 = jnp.zeros((E, D), jnp.float32)
        gamma = jnp.ones((D,), jnp.float32)
        beta = jnp.zeros((D,), jnp.float32)
        return {'x': x, 'Wr': Wr, 'br': br, 'W1': W1, 'b1': b1, 'W2': W2, 'b2': b2, 'gamma': gamma, 'beta': beta}
    _L0_ffn_all = _L0_ffn_setup()
    _L0_ffn_in = {k: v for k, v in _L0_ffn_all.items() if k in ('Wr', 'br', 'W1', 'b1', 'W2', 'b2', 'gamma', 'beta')}
    del _L0_ffn_all
    return {'x': x, 'src': src, 'dst': dst, 'edge_attr_4': edge_attr_4, 'edge_attr_8': edge_attr_8, 'L0_gnn_w1_s': _L0_gnn_in['w1_s'], 'L0_gnn_w1_v': _L0_gnn_in['w1_v'], 'L0_gnn_wsc_s': _L0_gnn_in['wsc_s'], 'L0_gnn_wsc_v': _L0_gnn_in['wsc_v'], 'L0_gnn_w2_s': _L0_gnn_in['w2_s'], 'L0_gnn_w2_v': _L0_gnn_in['w2_v'], 'L0_gnn_fc_w1': _L0_gnn_in['fc_w1'], 'L0_gnn_fc_w2': _L0_gnn_in['fc_w2'], 'L0_gnn_fc_w3': _L0_gnn_in['fc_w3'], 'L0_gnn_g_s': _L0_gnn_in['g_s'], 'L0_gnn_g_v': _L0_gnn_in['g_v'], 'L0_mix_w_qkv': _L0_mix_in['w_qkv'], 'L0_mix_bn_gamma': _L0_mix_in['bn_gamma'], 'L0_mix_bn_beta': _L0_mix_in['bn_beta'], 'L0_mix_w_dw': _L0_mix_in['w_dw'], 'L0_mix_w_pw': _L0_mix_in['w_pw'], 'L0_mix_w_res': _L0_mix_in['w_res'], 'L0_mix_b_res': _L0_mix_in['b_res'], 'L0_ffn_Wr': _L0_ffn_in['Wr'], 'L0_ffn_br': _L0_ffn_in['br'], 'L0_ffn_W1': _L0_ffn_in['W1'], 'L0_ffn_b1': _L0_ffn_in['b1'], 'L0_ffn_W2': _L0_ffn_in['W2'], 'L0_ffn_b2': _L0_ffn_in['b2'], 'L0_ffn_gamma': _L0_ffn_in['gamma'], 'L0_ffn_beta': _L0_ffn_in['beta']}

def reference(x, src, dst, edge_attr_4, edge_attr_8, L0_gnn_w1_s, L0_gnn_w1_v, L0_gnn_wsc_s, L0_gnn_wsc_v, L0_gnn_w2_s, L0_gnn_w2_v, L0_gnn_fc_w1, L0_gnn_fc_w2, L0_gnn_fc_w3, L0_gnn_g_s, L0_gnn_g_v, L0_mix_w_qkv, L0_mix_bn_gamma, L0_mix_bn_beta, L0_mix_w_dw, L0_mix_w_pw, L0_mix_w_res, L0_mix_b_res, L0_ffn_Wr, L0_ffn_br, L0_ffn_W1, L0_ffn_b1, L0_ffn_W2, L0_ffn_b2, L0_ffn_gamma, L0_ffn_beta):
    import jax
    import jax.numpy as jnp

    def _L0_gnn_ref(node_hiddens, edge_attr, edge_sh, w1_s, w1_v, wsc_s, wsc_v, w2_s, w2_v, fc_w1, fc_w2, fc_w3, g_s, g_v, edge_index):
        import jax, jax.numpy as jnp
        import numpy as np
        N_NODES = 2500
        N_EDGES = 40000
        MUL = 64
        NUM_BASIS = 8
        INV_SQRT3 = 0.5773502691896258
        EPS = 1e-05
        N = node_hiddens.shape[0]
        xs = node_hiddens[:, :MUL]
        xv = node_hiddens[:, MUL:].reshape(N, MUL, 3)
        h = jax.nn.silu(edge_attr @ fc_w1 * (1.0 / np.sqrt(float(NUM_BASIS))))
        h = jax.nn.silu(h @ fc_w2 * (1.0 / np.sqrt(64.0)))
        w = h @ fc_w3 * (1.0 / np.sqrt(64.0))
        wA, wB, wC, wD = jnp.split(w, 4, axis=1)
        inv = 1.0 / np.sqrt(float(MUL))
        sc_s = xs @ wsc_s * inv
        sc_v = jnp.einsum('nud,uv->nvd', xv, wsc_v) * inv
        ys = xs @ w1_s * inv
        yv = jnp.einsum('nud,uv->nvd', xv, w1_v) * inv
        src = edge_index[0]
        dst = edge_index[1]
        es = ys[dst]
        ev = yv[dst]
        sh0 = edge_sh[:, :1]
        sh1 = edge_sh[:, 1:]
        m0a = wA * es * sh0
        m0b = wD * jnp.einsum('eud,ed->eu', ev, sh1) * INV_SQRT3
        m1a = wB[:, :, None] * es[:, :, None] * sh1[:, None, :]
        m1b = wC[:, :, None] * ev * sh0[:, :, None]
        mid_s = jnp.concatenate([m0a, m0b], axis=1)
        mid_v = jnp.concatenate([m1a, m1b], axis=1)
        ns = jax.ops.segment_sum(mid_s, src, num_segments=N)
        nv = jax.ops.segment_sum(mid_v, src, num_segments=N)
        deg = jax.ops.segment_sum(jnp.ones((src.shape[0],), node_hiddens.dtype), src, num_segments=N)
        dn = jax.lax.rsqrt(jnp.maximum(deg, 1.0))
        ns = ns * dn[:, None]
        nv = nv * dn[:, None, None]
        inv2 = 1.0 / np.sqrt(2.0 * MUL)
        os_ = ns @ w2_s * inv2 + sc_s
        ov = jnp.einsum('nud,uv->nvd', nv, w2_v) * inv2 + sc_v
        os_ = os_ * jax.lax.rsqrt(jnp.mean(os_ * os_, axis=1, keepdims=True) + EPS) * g_s
        rms_v = jax.lax.rsqrt(jnp.mean(ov * ov, axis=(1, 2))[:, None, None] + EPS)
        ov = ov * rms_v * g_v[None, :, None]
        return jnp.concatenate([os_, ov.reshape(N, 3 * MUL)], axis=1)

    def _L0_mix_ref(x, w_qkv, bn_gamma, bn_beta, w_dw, w_pw, w_res, b_res):
        import jax, jax.numpy as jnp
        import numpy as np
        C_CURV = 1.0
        MIN_NORM = 1e-15
        BALL_EPS = 1e-05
        ATT_EPS = 1e-15
        DIM = 32

        def _norm(x):
            return jnp.clip(jnp.linalg.norm(x, axis=-1, keepdims=True), MIN_NORM)

        def proj(x, c):
            maxnorm = (1.0 - BALL_EPS) / jnp.sqrt(c)
            n = _norm(x)
            return jnp.where(n > maxnorm, x / n * maxnorm, x)

        def expmap0(u, c):
            sc = jnp.sqrt(c)
            n = _norm(u)
            return jnp.tanh(sc * n) * u / (sc * n)

        def logmap0(p, c):
            sc = jnp.sqrt(c)
            n = _norm(p)
            return jnp.arctanh(jnp.clip(sc * n, -1.0 + 1e-07, 1.0 - 1e-07)) * p / (sc * n)

        def mobius_add(x, y, c):
            x2 = jnp.sum(x * x, -1, keepdims=True)
            y2 = jnp.sum(y * y, -1, keepdims=True)
            xy = jnp.sum(x * y, -1, keepdims=True)
            num = (1 + 2 * c * xy + c * y2) * x + (1 - c * x2) * y
            den = 1 + 2 * c * xy + c * c * x2 * y2
            return num / jnp.clip(den, MIN_NORM)

        def conv1d(x, w, pad, groups=1):
            return jax.lax.conv_general_dilated(x, w, (1,), [(pad, pad)], dimension_numbers=('NCH', 'OIH', 'NCH'), feature_group_count=groups)

        def batchnorm(x, gamma, beta):
            mean = jnp.mean(x, axis=(0, 2), keepdims=True)
            var = jnp.var(x, axis=(0, 2), keepdims=True)
            xn = (x - mean) * jax.lax.rsqrt(var + 1e-05)
            return gamma[None, :, None] * xn + beta[None, :, None]

        def _reference_tuple_inner(x, w_qkv, bn_gamma, bn_beta, w_dw, w_pw, w_res, b_res):
            c = C_CURV
            h = logmap0(proj(x, c), c)
            h = jnp.transpose(h, (1, 2, 0))
            h = conv1d(h, w_qkv, pad=2)
            h = batchnorm(h, bn_gamma, bn_beta)
            h = jax.nn.relu(jnp.transpose(h, (2, 0, 1)))
            qkv = proj(expmap0(h, c), c)
            t = jnp.transpose(logmap0(proj(qkv, c), c), (1, 2, 0))
            s = conv1d(t, w_dw, pad=2, groups=t.shape[1])
            s = conv1d(s, w_pw, pad=0, groups=t.shape[1] // DIM)
            cat = jnp.concatenate([t, s], axis=1)
            ai = proj(expmap0(jnp.transpose(cat, (2, 0, 1)), c), c)
            t2 = logmap0(proj(ai, c), c)
            L, N, C2 = t2.shape
            g = C2 // (3 * DIM)
            qkv3 = jnp.transpose(t2, (1, 2, 0)).reshape(N, g, 3 * DIM, L)
            q, k, v = jnp.split(qkv3, 3, axis=2)
            q = jax.nn.relu(q)
            k = jax.nn.relu(k)
            vk = jnp.einsum('ngdl,ngel->ngde', v, k)
            out = jnp.einsum('ngde,ngdl->ngdl', vk, q)
            out = out / (jnp.sum(v, -1, keepdims=True) + ATT_EPS)
            out = jnp.transpose(out.reshape(N, g * DIM, L), (2, 0, 1))
            fx_h = proj(expmap0(out, c), c)
            ft = jnp.transpose(logmap0(proj(fx_h, c), c), (1, 2, 0))
            ft = conv1d(ft, w_res, pad=0) + b_res[None, :, None]
            fx = proj(expmap0(jnp.transpose(ft, (2, 0, 1)), c), c)
            residual = mobius_add(fx, x, c)
            return (fx, residual)
        return _reference_tuple_inner(x, w_qkv, bn_gamma, bn_beta, w_dw, w_pw, w_res, b_res)[0]

    def _L0_ffn_ref(x, Wr, br, W1, b1, W2, b2, gamma, beta):
        import math
        import jax, jax.numpy as jnp
        import numpy as np
        CAPACITY_FACTOR = 1.25
        TOP_K = 2
        LN_EPS = 1e-05

        def _layer_norm(x, gamma, beta):
            mu = jnp.mean(x, axis=-1, keepdims=True)
            var = jnp.var(x, axis=-1, keepdims=True)
            return (x - mu) * jax.lax.rsqrt(var + LN_EPS) * gamma + beta
        B, S, D = x.shape
        E = Wr.shape[1]
        N = B * S
        K = TOP_K
        logits = jnp.mean(x, axis=1) @ Wr + br
        routing_weights = jax.nn.softmax(logits, axis=-1)
        capacity = float(math.ceil(N * CAPACITY_FACTOR / E))
        expected_loads = routing_weights.sum(axis=0) * (N / B)
        scale = jnp.where(expected_loads > capacity, capacity / expected_loads, 1.0)
        routing_weights = jax.nn.softmax(routing_weights * scale, axis=-1)
        rw_tok = jnp.broadcast_to(routing_weights[:, None, :], (B, S, E)).reshape(N, E)
        top_w, top_i = jax.lax.top_k(rw_tok, K)
        top_w = jax.nn.softmax(top_w, axis=-1)
        xf = x.reshape(N, D)
        h = jax.nn.gelu(jnp.einsum('nd,edf->enf', xf, W1) + b1[:, None, :], approximate=False)
        y = jnp.einsum('enf,efd->end', h, W2) + b2[:, None, :]
        w_dense = jnp.zeros((N, E), x.dtype).at[jnp.arange(N)[:, None], top_i].add(top_w)
        out = jnp.einsum('ne,end->nd', w_dense, y).reshape(B, S, D)
        out = _layer_norm(out + x, gamma, beta)
        return out
    edge_index = jnp.stack([src, dst])
    xn = _layernorm(x, axis=-1)
    x = x + _L0_gnn_ref(xn, edge_attr_8, edge_attr_4, L0_gnn_w1_s, L0_gnn_w1_v, L0_gnn_wsc_s, L0_gnn_wsc_v, L0_gnn_w2_s, L0_gnn_w2_v, L0_gnn_fc_w1, L0_gnn_fc_w2, L0_gnn_fc_w3, L0_gnn_g_s, L0_gnn_g_v, edge_index) + _L0_mix_ref(xn[None], L0_mix_w_qkv, L0_mix_bn_gamma, L0_mix_bn_beta, L0_mix_w_dw, L0_mix_w_pw, L0_mix_w_res, L0_mix_b_res)[0]
    x = x + _L0_ffn_ref(_layernorm(x, axis=-1)[None], L0_ffn_Wr, L0_ffn_br, L0_ffn_W1, L0_ffn_b1, L0_ffn_W2, L0_ffn_b2, L0_ffn_gamma, L0_ffn_beta)[0]
    return x

_drawn_inputs = setup_inputs


def setup_inputs(seed=0):
    import zlib

    import numpy as np

    out = dict(_drawn_inputs(seed))
    spreads = {'L0_gnn_g_s': (1.0, 0.2),
     'L0_gnn_g_v': (1.0, 0.2),
     'L0_mix_bn_gamma': (1.0, 0.6),
     'L0_mix_bn_beta': (0.0, 0.698),
     'L0_mix_b_res': (0.0, 0.547),
     'L0_ffn_br': (0.0, 0.1),
     'L0_ffn_b1': (0.0, 0.455),
     'L0_ffn_b2': (0.0, 0.306),
     'L0_ffn_gamma': (1.0, 0.2),
     'L0_ffn_beta': (0.0, 0.1)}
    factors = {'L0_mix_w_dw': 8.0, 'L0_mix_w_pw': 8.0, 'L0_ffn_Wr': 8.0}
    for name, (base, spread) in spreads.items():
        noise = np.random.default_rng([zlib.crc32(name.encode()), seed]).standard_normal(out[name].shape)
        drawn = base * np.exp(spread * noise) if base else spread * noise
        out[name] = jnp.asarray(drawn.astype(out[name].dtype))
    for name, factor in factors.items():
        out[name] = (out[name] * factor).astype(out[name].dtype)
    return out
```

```python
from contextlib import ExitStack

import numpy as np

import concourse.bass as bass
from concourse import mybir

F32 = mybir.dt.float32
BF16 = mybir.dt.bfloat16
I32 = mybir.dt.int32
U32 = mybir.dt.uint32
ALU = mybir.AluOpType
ACT = mybir.ActivationFunctionType
AX = mybir.AxisListType

P = 128
N = 6250
D = 256
MUL = 64
E = 206250
NT = -(-N // P)
NP = NT * P
LAST = N - (NT - 1) * P
G7 = 7
HALF = 8
STEP = 2 * HALF
NH = 2 * (-(-E // (STEP * P)))
NI = NH // 2
TABLES = 2
ROW = 516
TRASH = NP
TROWS = NP + P
CH = 768
NCH = CH // P
GROUPS = 16
DIM = 32
FF = 512
NE = 8
EPS = 1e-5
MIN_NORM = 1e-15
MAXN = float(np.float32(1.0 - 1e-5))
ATANH_MAXN = float(np.arctanh(np.float64(np.float32(1.0 - 1e-5))))
INV_SQRT3 = 0.5773502691896258
CAPACITY = float(-(-int(N * 1.25) // NE)) if (N * 1.25) == int(N * 1.25) else float(int(N * 1.25 / NE) + 1)


class Arena:

    def __init__(self, tensor, size):
        self.tensor, self.size, self.at = tensor, size, 0

    def reset(self):
        self.at = 0

    def take(self, *shape):
        n = int(np.prod(shape))
        ap = self.tensor[:, self.at:self.at + n]
        self.at += n
        assert self.at <= self.size, (self.at, self.size)
        if len(shape) == 1:
            return ap
        names = "abcd"[:len(shape)]
        spec = f"p ({' '.join(names)}) -> p {' '.join(names)}"
        return ap.rearrange(spec, **{names[i]: shape[i] for i in range(1, len(shape))})


class Env:
    pass


def col(ap, i, n=1):
    return ap[:, bass.ds(i, n)]


def setup(nc, ctx, io):
    e = Env()
    e.io = io
    e.sb = lambda n, s, d=F32: ctx.enter_context(nc.sbuf_tensor(n, s, d))
    e.ps = lambda n, s, d=F32: ctx.enter_context(nc.psum_tensor(n, s, d))
    e.sem = lambda n: ctx.enter_context(nc.semaphore(n))
    e.dram = lambda n, s: nc.dram_tensor(n, s, F32).ap()
    e.A = e.sb("region_a", [P, NT * D])
    e.B = e.sb("region_b", [P, 2 * NP])
    e.C = e.sb("region_c", [P, 2 * NP])
    e.arena = Arena(e.sb("scratch", [P, 14100]), 14100)
    e.ident = e.sb("ident", [P, P])
    e.pick = e.sb("picked_experts", [1, 2], I32)
    e.weight = e.sb("expert_weights", [P, 2])
    e.bn = e.sb("bn_scale_shift", [P, 2, NCH])
    e.eq = e.sb("equal_src", [P, 2, 2, P], BF16)
    e.row1 = e.sb("row_index", [P, P], BF16)[:, :]
    e.ones_b = e.sb("ones_bf16", [P, 1], BF16)
    e.junk = e.sb("junk", [P, 2, P], BF16)
    e.stat = e.sb("stat", [P, 12, NT])
    e.banks = [e.ps(f"bank{i}", [P, 512]) for i in range(8)]
    e.y_d = e.dram("y_d", [NP, D])
    e.sc_d = e.dram("sc_d", [NP, D])
    e.conv_d = e.dram("conv_d", [NCH, P, NP])
    e.agg_d = [e.dram(f"agg{r}_d", [TROWS, ROW]) for r in range(TABLES)]
    return e


def linker(eng, sem):
    n = [0]

    def link(ins):
        n[0] += 1
        ins.then_inc(sem, 1)
        eng.wait_ge(sem, n[0])
    return link


def row_moments(link, dve, bst, mean, var, tmp):
    link(dve.tensor_tensor(mean, bst[:, :, 1], bst[:, :, 4], ALU.add))
    link(dve.tensor_scalar(mean, mean, 0.5, None, ALU.mult))
    link(dve.tensor_tensor(tmp, mean, bst[:, :, 1], ALU.subtract))
    link(dve.tensor_tensor(tmp, tmp, tmp, ALU.mult))
    link(dve.tensor_tensor(var, bst[:, :, 2], bst[:, :, 5], ALU.add))
    link(dve.tensor_scalar(var, var, 1.0 / D, None, ALU.mult))
    link(dve.tensor_tensor(var, var, tmp, ALU.add))


MOMENTS = 7


def phase_nodes(nc, e):
    io, ar, st = e.io, e.arena, e.stat
    ar.reset()
    wy = ar.take(2, D)
    xn = ar.take(G7, D)
    hin = ar.take(G7, D)
    xnT = ar.take(2, 2, P)
    ysc = ar.take(G7, 2, D)
    bst = ar.take(NT, 6)
    mean, var = ar.take(NT), ar.take(NT)
    s1, s2, q, l1, l2, sq, ser, msk, e2 = (ar.take(NT) for _ in range(9))
    zero = e.C[:, 0:5 * ROW]
    rstd, ascale, norm = st[:, 0], st[:, 1], st[:, 2]
    ident = e.ident
    x_v = io["x"].rearrange("(t p) d -> p t d", p=P)
    x_ld, w_ld, z_ld = e.sem("x_ld"), e.sem("wy_ld"), e.sem("table_zeroed")
    w_zero, z_zero, id0, id1 = e.sem("wy_zero"), e.sem("zero_tile"), e.sem("ident0"), e.sem("ident_ready")
    bs_done, v, a = e.sem("bn_done"), e.sem("nodes_vec"), e.sem("nodes_act")
    xn_rdy, hin_rdy, t_done, xnT_rdy, hT_rdy = (e.sem(n) for n in (
        "xn_ready", "hin_ready", "node_transposed", "xnT_ready", "hinT_ready"))
    y_done, ysc_rdy = e.sem("y_done"), e.sem("ysc_ready")
    st_y = [e.sem(f"ysc_stored{k}") for k in range(G7)]
    e.v_total = 0

    with nc.Block() as block:
        @block.sync
        def _(sp):
            for g in range(NT // G7):
                sp.dma_start(e.A[:, g * G7 * D:(g + 1) * G7 * D].rearrange("p (t d) -> p t d", d=D),
                             x_v[:, g * G7:(g + 1) * G7, :]).then_inc(x_ld, 16)
            sp.wait_ge(w_zero, 1)
            for c, top in ((0, "s"), (1, "v")):
                for h, name in ((0, "w1"), (1, "wsc")):
                    sp.dma_start(wy[0:64, c, h * P:h * P + 64], io[f"{name}_{top}"]).then_inc(w_ld, 16)
                    sp.dma_start(wy[64:128, c, h * P + 64:h * P + 128], io[f"{name}_v"]).then_inc(w_ld, 16)
            sp.wait_ge(z_zero, 1)
            for r in range(TABLES):
                sp.dma_start(e.agg_d[r].rearrange("(p a b) c -> p a (b c)", p=P, b=5),
                             zero.rearrange("p (a n) -> p a n", a=1).broadcast_to([P, TROWS // P // 5, 5 * ROW])
                             ).then_inc(z_ld, 16)

            with sp.Fori(0, NT // G7) as it:
                for k in range(G7):
                    sp.wait_ge(ysc_rdy, G7 * it + (k + 1))
                    sp.dma_start(e.y_d[bass.ds(it * (G7 * P) + k * P, P), :], ysc[:, k, 0]).then_inc(st_y[k], 16)
                    sp.dma_start(e.sc_d[bass.ds(it * (G7 * P) + k * P, P), :], ysc[:, k, 1]).then_inc(st_y[k], 16)
            for k in range(G7):
                sp.wait_ge(st_y[k], 32 * (NT // G7))
            sp.wait_ge(z_ld, 16 * TABLES)

        @block.gpsimd
        def _(pool):
            pool.memset(ident[:], 0.0).then_inc(id0, 1)
            pool.memset(wy, 0.0).then_inc(w_zero, 1)
            pool.memset(zero, 0.0).then_inc(z_zero, 1)
            pool.wait_ge(id0, 1)
            pool.affine_select(out=ident[:], in_=ident[:], compare_op=ALU.not_equal, fill=1.0, base=0,
                               pattern=[[-1, P]], channel_multiplier=1).then_inc(id1, 1)

        def evac(dve, it, k):
            i = it * G7 + k
            dve.wait_ge(t_done, i + 1)
            dve.wait_ge(y_done, i - 1 if k else it * G7)
            dve.tensor_copy(xnT[:, k % 2], e.banks[k % 2][:, 0:D].rearrange("p (c n) -> p c n", c=2)).then_inc(xnT_rdy, 1)

        @block.vector
        def _(dve):
            link = linker(dve, v)
            dve.wait_ge(x_ld, 16 * (NT // G7))
            with dve.Fori(0, NT) as i:
                dve.bn_stats(col(bst.rearrange("p a b -> p (a b)"), 6 * i, 6),
                             col(e.A, i * D, D)).then_inc(bs_done, 1)
            dve.wait_ge(bs_done, NT)
            row_moments(link, dve, bst, mean, var, q)
            link(dve.tensor_scalar(s1, var, EPS, None, ALU.add))
            dve.wait_ge(a, 2)
            link(dve.reciprocal(rstd, s1))
            link(dve.tensor_tensor(norm, s2, rstd, ALU.mult))
            link(dve.tensor_scalar(norm, norm, MIN_NORM, None, ALU.max))
            link(dve.tensor_scalar(q, norm, MAXN, None, ALU.min))
            dve.wait_ge(a, 4)
            link(dve.tensor_tensor(l1, l1, l2, ALU.subtract))
            link(dve.tensor_scalar(l1, l1, 0.5, None, ALU.mult))
            link(dve.tensor_tensor(sq, q, q, ALU.mult))
            link(dve.tensor_scalar(ser, sq, 0.2, 1.0 / 3.0, ALU.mult, ALU.add))
            link(dve.tensor_tensor(ser, ser, sq, ALU.mult))
            link(dve.tensor_scalar(ser, ser, 1.0, None, ALU.add))
            link(dve.tensor_tensor(ser, ser, q, ALU.mult))
            link(dve.tensor_scalar(msk, q, 0.03, None, ALU.is_lt))
            link(dve.tensor_tensor(ser, ser, l1, ALU.subtract))
            link(dve.tensor_tensor(ser, ser, msk, ALU.mult))
            link(dve.tensor_tensor(l1, l1, ser, ALU.add))
            link(dve.reciprocal(e2, norm))
            link(dve.tensor_tensor(ascale, l1, e2, ALU.mult))

            with dve.Fori(0, NT // G7) as it:
                for k in range(G7):
                    i = it * G7 + k
                    dve.wait_ge(t_done, it * G7)
                    dve.wait_ge(hin_rdy, it * G7)
                    dve.tensor_scalar(xn[:, k], col(e.A, i * D, D), col(mean, i), col(rstd, i),
                                      ALU.subtract, ALU.mult).then_inc(xn_rdy, 1)
                    if k:
                        evac(dve, it, k - 1)
                evac(dve, it, G7 - 1)

        @block.scalar
        def _(act):
            act.wait_ge(v, MOMENTS + 1)
            act.activation(s1, s1, ACT.Sqrt).then_inc(a, 1)
            act.activation(s2, var, ACT.Sqrt, scale=float(D)).then_inc(a, 1)
            act.wait_ge(v, MOMENTS + 5)
            act.activation(l1, q, ACT.Ln, bias=1.0).then_inc(a, 1)
            act.activation(l2, q, ACT.Ln, bias=1.0, scale=-1.0).then_inc(a, 1)
            act.wait_ge(v, MOMENTS + 18)
            hT = e.B[:, :].rearrange("p (c n) -> p c n", c=2)

            def out(it, k):
                i = it * G7 + k
                act.wait_ge(t_done, i + 1)
                act.activation(hT[:, :, bass.ds(i * P, P)],
                               e.banks[4 + k % 2][:, 0:D].rearrange("p (c n) -> p c n", c=2),
                               ACT.Copy).then_inc(hT_rdy, 1)
                act.wait_ge(y_done, i + 1)
                act.wait_ge(st_y[k], 32 * it)
                act.activation(ysc[:, k].rearrange("p h (c n) -> p c h n", c=2),
                               e.banks[2 + k % 2][:, :].rearrange("p (c h n) -> p c h n", c=2, h=2),
                               ACT.Copy, scale=0.125).then_inc(ysc_rdy, 1)

            with act.Fori(0, NT // G7) as it:
                for k in range(G7):
                    i = it * G7 + k
                    act.wait_ge(xn_rdy, i + 1)
                    act.activation(hin[:, k], xn[:, k], ACT.Copy, scale=col(ascale, i)).then_inc(hin_rdy, 1)
                    if k:
                        out(it, k - 1)
                out(it, G7 - 1)

        @block.tensor
        def _(pe):
            pe.wait_ge(id1, 1)
            pe.wait_ge(w_ld, 16 * 8)

            def project(it, k):
                i = it * G7 + k
                pe.wait_ge(xnT_rdy, i + 1)
                pe.wait_ge(ysc_rdy, i - 1 if k else it * G7)
                for c in range(2):
                    mm = pe.matmul(e.banks[2 + k % 2][:, c * D:(c + 1) * D], xnT[:, k % 2, c], wy[:, c],
                                   start=True, stop=True)
                mm.then_inc(y_done, 1)

            with pe.Fori(0, NT // G7) as it:
                for k in range(G7):
                    i = it * G7 + k
                    pe.wait_ge(xn_rdy, i + 1)
                    pe.wait_ge(hin_rdy, i + 1)
                    pe.wait_ge(xnT_rdy, i - 1 if k else it * G7)
                    pe.wait_ge(hT_rdy, i - 1 if k else it * G7)
                    for c in range(4):
                        src = (xn if c < 2 else hin)[:, k, (c % 2) * P:(c % 2 + 1) * P]
                        mm = pe.transpose(e.banks[c // 2 * 4 + k % 2][:, c % 2 * P:(c % 2 + 1) * P], src, ident[:])
                    mm.then_inc(t_done, 1)
                    if k:
                        project(it, k - 1)
                project(it, G7 - 1)


def phase_convolve(nc, e):
    io, ar, S = e.io, e.arena, e.sem
    ar.reset()
    wq = ar.take(2, CH)
    stage = ar.take(NCH, 512)
    full = N // 512
    tail, tail_w = N - full * 512, NP - full * 512
    bst = ar.take(NCH, full + 1, 6)
    bstf = bst.rearrange("p a b c -> p (a b c)")
    mv = ar.take(NCH, 2)
    gb = ar.take(2, NCH)
    t1 = ar.take(NCH)
    hT = e.B[:, :].rearrange("p (c n) -> p c n", c=2)
    w_ld, conv, out, bs, v, a = S("wq_ld"), S("conv_done"), S("conv_out"), S("conv_stats"), S("bn_vec"), S("bn_act")
    stored = [S(f"conv_stored{c}") for c in range(NCH)]

    with nc.Block() as block:
        @block.sync
        def _(sp):
            sp.dma_start(wq, io["w_qkv"][2].rearrange("(k p) c -> p k c", p=P)).then_inc(w_ld, 16)
            sp.dma_start(gb[:, 0], io["bn_g"]).then_inc(w_ld, 16)
            sp.dma_start(gb[:, 1], io["bn_b"]).then_inc(w_ld, 16)

            def store(n, w):
                for c in range(NCH):
                    sp.wait_ge(out, NCH * n + (c + 1))
                    sp.dma_start(e.conv_d[c][:, bass.ds(n * 512, w)], stage[:, c, 0:w]).then_inc(stored[c], 16)

            with sp.Fori(0, full) as n:
                store(n, 512)
            store(full, tail_w)
            for c in range(NCH):
                sp.wait_ge(stored[c], 16 * (full + 1))

        @block.tensor
        def _(pe):
            pe.wait_ge(w_ld, 48)

            def chunk(n, w):
                for c in range(NCH):
                    pe.wait_ge(out, NCH * n)
                    for k in range(2):
                        mm = pe.matmul(e.banks[c][:, 0:w], wq[:, k, c * P:(c + 1) * P],
                                       hT[:, k, bass.ds(n * 512, w)], start=(k == 0), stop=(k == 1))
                    mm.then_inc(conv, 1)

            with pe.Fori(0, full) as n:
                chunk(n, 512)
            chunk(full, tail_w)

        @block.scalar
        def _(act):
            def chunk(n, w):
                for c in range(NCH):
                    act.wait_ge(conv, NCH * n + (c + 1))
                    act.wait_ge(stored[c], 16 * n)
                    act.wait_ge(bs, NCH * n)
                    act.activation(stage[:, c, 0:w], e.banks[c][:, 0:w], ACT.Copy).then_inc(out, 1)

            with act.Fori(0, full) as n:
                chunk(n, 512)
            chunk(full, tail_w)
            act.wait_ge(v, 1)
            act.activation(t1, t1, ACT.Sqrt).then_inc(a, 1)

        @block.vector
        def _(dve):
            def chunk(n, w):
                for c in range(NCH):
                    dve.wait_ge(out, NCH * n + (c + 1))
                    dve.bn_stats(col(bstf, (n + c * (full + 1)) * 6, 6), stage[:, c, 0:w]).then_inc(bs, 1)

            with dve.Fori(0, full) as n:
                chunk(n, 512)
            chunk(full, tail)
            dve.wait_ge(bs, NCH * (full + 1))
            for c in range(NCH):
                dve.bn_aggr(mv[:, c], bst[:, c].rearrange("p a b -> p (a b)")).then_inc(bs, 1)
            dve.wait_ge(bs, NCH * (full + 2))
            n = [0]

            def link(ins):
                n[0] += 1
                ins.then_inc(v, 1)
                dve.wait_ge(v, n[0])

            link(dve.tensor_scalar(t1, mv[:, :, 1], EPS, None, ALU.add))
            dve.wait_ge(a, 1)
            dve.wait_ge(w_ld, 48)
            link(dve.reciprocal(t1, t1))
            link(dve.tensor_tensor(e.bn[:, 0], t1, gb[:, 0], ALU.mult))
            link(dve.tensor_tensor(t1, mv[:, :, 0], e.bn[:, 0], ALU.mult))
            link(dve.tensor_tensor(e.bn[:, 1], gb[:, 1], t1, ALU.subtract))


def phase_mix(nc, e):
    io, ar, S = e.io, e.arena, e.sem
    ar.reset()
    hb = [e.B[:, c * 3072:(c + 1) * 3072].rearrange("p (c n) -> p c n", c=NCH) for c in range(2)]
    wbd = ar.take(NCH, P)
    wres = ar.take(4, D)
    bres = ar.take(D)
    dw = ar.take(NCH)
    cat = ar.take(2, 2 * CH)
    kr = ar.take(GROUPS, DIM)
    qv = ar.take(GROUPS, DIM)
    den = ar.take(GROUPS, DIM)
    rat = ar.take(GROUPS, DIM)
    att = ar.take(2, GROUPS * DIM)
    attT = ar.take(4, P)
    junk = ar.take(2, CH)
    junk3 = ar.take(D)
    n2, r2, kap = ar.take(2, 2), ar.take(2, 2), ar.take(2, 1)
    ks = ar.take(GROUPS)
    o2, gam, o2a = ar.take(2, 1), ar.take(2, 1), ar.take(2, 1)
    junk2 = ar.take(512)
    nf2 = e.stat[:, 3]
    ident = e.ident
    b_h, b_s, b_t, b_r = e.banks[0:2], e.banks[2:4], e.banks[4], e.banks[5]
    STEPS, J = 6, 8
    w_zero, w_ld, w_rdy = S("mix_zero"), S("mix_w_ld"), S("mix_w_ready")
    c_in = [S(f"conv_in{c}") for c in range(2)]
    h_rdy, a_done, ea, nrm = S("h_ready"), S("mix_a_done"), S("cat_ready"), S("norm_ready")
    v, att_rdy, so, t_done, eo, res, ft, sf = (S(n) for n in (
        "mix_vec", "att_ready", "att_norm", "att_transposed", "attT_ready", "res_done", "ft_ready", "ft_square"))
    sq, sq2, v2 = S("mix_squares"), S("att_square"), S("mix_scale")

    with nc.Block() as block:
        @block.gpsimd
        def _(pool):
            pool.memset(wbd, 0.0).then_inc(w_zero, 1)

        @block.sync
        def _(sp):
            def load(n, w, b):
                sp.dma_start(hb[b][:, :, 0:w], e.conv_d[:, :, bass.ds(n * 512, w)].rearrange("c p n -> p c n")
                             ).then_inc(c_in[b], 16)

            load(0, 512, 0)
            load(1, 512, 1)
            sp.wait_ge(w_zero, 1)
            for b in range(4):
                sp.dma_start(wbd[32 * b:32 * b + 32, :, 32 * b:32 * b + 32], io["w_pw"][b]).then_inc(w_ld, 16)
            sp.dma_start(dw, io["w_dw"][2]).then_inc(w_ld, 16)
            sp.dma_start(wres, io["w_res"].rearrange("(k p) c -> p k c", p=P)).then_inc(w_ld, 16)
            sp.dma_start(bres, io["b_res"].broadcast_to([P, D])).then_inc(w_ld, 16)
            with sp.Fori(0, STEPS - 1) as s:
                for b in range(2):
                    sp.wait_ge(a_done, 8 * s + 4 * (b + 1))
                    load(2 * s + (2 + b), 512, b)
            sp.wait_ge(a_done, 8 * (STEPS - 1) + 4)
            load(2 * STEPS, NP - 1024 * STEPS, 0)

        @block.vector
        def _(dve):
            n = [0]
            dve.wait_ge(w_ld, 16 * 7)
            for c in range(NCH):
                dve.tensor_scalar(wbd[:, c], wbd[:, c], dw[:, c:c + 1], None, ALU.mult).then_inc(w_rdy, 1)

            LINKS = 8

            def attention(t, j):
                s = j % 2
                m = [0]

                def link(ins):
                    m[0] += 1
                    ins.then_inc(v, 1)
                    dve.wait_ge(v, LINKS * t + m[0])

                x = cat[:, s].rearrange("p (g c d) -> p g c d", g=GROUPS, c=3)
                dve.wait_ge(nrm, t + 1)
                link(dve.tensor_scalar(r2[:, s], r2[:, s], MIN_NORM, None, ALU.max))
                link(dve.reciprocal(r2[:, s], r2[:, s]))
                link(dve.tensor_scalar(r2[:, s], r2[:, s], ATANH_MAXN, 1.0, ALU.mult, ALU.min))
                link(dve.tensor_tensor(kap[:, s], r2[:, s, 0:1], r2[:, s, 1:2], ALU.min))
                dve.tensor_scalar(kr, x[:, :, 1], 0.0, None, ALU.max)
                link(dve.tensor_scalar(den, x[:, :, 2], kap[:, s], MIN_NORM, ALU.mult, ALU.add))
                dve.scalar_tensor_tensor(out=qv, in0=x[:, :, 0], scalar=0.0, in1=x[:, :, 2], op0=ALU.max, op1=ALU.mult)
                link(dve.reciprocal(den, den))
                dve.tensor_reduce(ks, kr, AX.X, ALU.add)
                link(dve.scalar_tensor_tensor(out=rat, in0=qv, scalar=kap[:, s], in1=den,
                                              op0=ALU.mult, op1=ALU.mult))
                link(dve.tensor_scalar(ks, ks, kap[:, s], kap[:, s], ALU.mult, ALU.mult))
                dve.wait_ge(t_done, t - 1 if not isinstance(t, int) else max(t - 1, 0))
                dve.tensor_tensor(att[:, s].rearrange("p (g d) -> p g d", g=GROUPS), rat,
                                  ks.rearrange("p (g o) -> p g o", o=1).broadcast_to([P, GROUPS, DIM]),
                                  ALU.mult).then_inc(att_rdy, 1)

            def finish(t, j):
                s = j % 2
                dve.wait_ge(so, t + 1)
                dve.tensor_scalar(o2[:, s], o2[:, s], MIN_NORM, None, ALU.max).then_inc(v2, 1)
                dve.wait_ge(v2, 3 * t + 1)
                dve.reciprocal(gam[:, s], o2[:, s]).then_inc(v2, 1)
                dve.wait_ge(v2, 3 * t + 2)
                dve.tensor_scalar(gam[:, s], gam[:, s], ATANH_MAXN, 1.0, ALU.mult, ALU.min).then_inc(v2, 1)
                dve.wait_ge(v2, 3 * t + 3)
                dve.wait_ge(res, t + 1)
                dve.scalar_tensor_tensor(out=col(e.C, t * D, D), in0=b_r[:, 0:D], scalar=gam[:, s], in1=bres,
                                         op0=ALU.mult, op1=ALU.add).then_inc(ft, 1)

            def step(s, first=False):
                for j in range(J):
                    attention(J * s + j, j)
                    if not (first and j == 0):
                        finish(J * s + (j - 1), (j - 1) % J)

            step(0, True)
            with dve.Fori(1, STEPS) as s:
                step(s)
            attention(NT - 1, 0)
            finish(NT - 2, 7)
            finish(NT - 1, 0)

        @block.scalar
        def _(act):
            def relu(b, w):
                for c in range(NCH):
                    last = act.activation(hb[b][:, c, 0:w], hb[b][:, c, 0:w], ACT.Relu, scale=e.bn[:, 0, c:c + 1],
                                          bias=e.bn[:, 1, c:c + 1])
                last.then_inc(h_rdy, 1)

            def cat_out(t, j):
                s = j % 2
                act.wait_ge(a_done, t + 1)
                if not (isinstance(t, int) and t < 2):
                    act.wait_ge(att_rdy, t - 1)
                for b, (o, w) in zip((*b_h, *b_s), ((0, 512), (512, 256), (768, 512), (1280, 256))):
                    last = act.activation(cat[:, s, o:o + w], b[:, 0:w], ACT.Copy)
                last.then_inc(ea, 1)
                act.wait_ge(ea, t + 1)
                for h in range(2):
                    last = act.activation(junk[:, h], cat[:, s, h * CH:(h + 1) * CH], ACT.Square,
                                          accum_out=n2[:, s, h:h + 1])
                last.then_inc(sq, 1)
                act.wait_ge(sq, t + 1)
                act.activation(r2[:, s, 1:2], n2[:, s, 0:1], ACT.Sqrt, bias=n2[:, s, 1:2])
                act.activation(r2[:, s, 0:1], n2[:, s, 0:1], ACT.Sqrt).then_inc(nrm, 1)

            def att_norm(t, j):
                s = j % 2
                act.wait_ge(att_rdy, t + 1)
                act.activation(junk2, att[:, s], ACT.Square, accum_out=o2a[:, s]).then_inc(sq2, 1)
                act.wait_ge(sq2, t + 1)
                act.activation(o2[:, s], o2a[:, s], ACT.Sqrt).then_inc(so, 1)
                act.wait_ge(t_done, t + 1)
                act.wait_ge(res, t)
                act.activation(attT.rearrange("p a b -> p (a b)"), b_t[:, :], ACT.Copy).then_inc(eo, 1)

            def ft_square(t):
                act.wait_ge(ft, t + 1)
                act.wait_ge(sf, t)
                act.activation(junk3, col(e.C, t * D, D), ACT.Square, accum_out=col(nf2, t)).then_inc(sf, 1)

            def step(s, first=False, last=False):
                for j in range(J):
                    t = J * s + j
                    if j == 2:
                        act.wait_ge(c_in[1], 16 * s + 16)
                        relu(1, 512)
                    if j == 6:
                        act.wait_ge(c_in[0], 16 * s + 32)
                        relu(0, 128 if last else 512)
                    cat_out(t + 1, (j + 1) % J)
                    att_norm(t, j)
                    if not (first and j == 0):
                        ft_square(t - 1)

            act.wait_ge(c_in[0], 16)
            relu(0, 512)
            cat_out(0, 0)
            step(0, first=True)
            with act.Fori(1, STEPS - 1) as s:
                step(s)
            step(STEPS - 1, last=True)
            att_norm(NT - 1, 0)
            ft_square(NT - 2)
            ft_square(NT - 1)

        @block.tensor
        def _(pe):
            def part_b(t, j):
                s = j % 2
                pe.wait_ge(att_rdy, t + 1)
                pe.wait_ge(eo, t)
                for c in range(4):
                    mm = pe.transpose(b_t[:, c * P:(c + 1) * P], att[:, s, c * P:(c + 1) * P], ident[:])
                mm.then_inc(t_done, 1)
                pe.wait_ge(eo, t + 1)
                pe.wait_ge(ft, t)
                for c in range(4):
                    mm = pe.matmul(b_r[:, 0:D], attT[:, c], wres[:, c], start=(c == 0), stop=(c == 3))
                mm.then_inc(res, 1)

            def part_a(t, j):
                b, n = j // 4, j % 4
                pe.wait_ge(ea, t)
                for c in range(NCH):
                    pe.transpose(b_h[c // 4][:, c % 4 * P:(c % 4 + 1) * P], hb[b][:, c, n * P:(n + 1) * P], ident[:])
                for c in range(NCH):
                    mm = pe.matmul(b_s[c // 4][:, c % 4 * P:(c % 4 + 1) * P], hb[b][:, c, n * P:(n + 1) * P],
                                   wbd[:, c], start=True, stop=True)
                mm.then_inc(a_done, 1)

            def step(s):
                for j in range(J):
                    nj = (j + 1) % J
                    if nj % 4 == 0:
                        pe.wait_ge(h_rdy, 2 * s + (2 if nj else 3))
                    part_a(J * s + (j + 1), nj)
                    part_b(J * s + j, j)

            pe.wait_ge(w_rdy, NCH)
            pe.wait_ge(h_rdy, 1)
            part_a(0, 0)
            with pe.Fori(0, STEPS) as s:
                step(s)
            part_b(NT - 1, 0)



def phase_edges(nc, e):
    io, ar = e.io, e.arena
    ar.reset()
    dst_i = [ar.take(HALF) for _ in range(2)]
    src_i = [ar.take(HALF) for _ in range(2)]
    src_f = [ar.take(HALF) for _ in range(2)]
    src_off = [ar.take(HALF) for _ in range(2)]
    sh = [ar.take(HALF, 4) for _ in range(2)]
    a8 = [ar.take(P) for _ in range(2)]
    h1s = ar.take(4 * P)
    h2T = [ar.take(4 * P) for _ in range(2)]
    w1v = ar.take(4, P)
    w2bd = ar.take(P)
    w3z = ar.take(2, D)
    yb = e.B[:, 0:2 * HALF * D].rearrange("p (h t d) -> p h t d", h=2, t=HALF)
    xb = ar.take(2, 2, 512)
    eq = e.eq
    seq = ar.take(2, 2, 4, P)
    msg = ar.take(8, ROW)
    idx = ar.take(8)
    mx = ar.take(2, 2)
    tmp = ar.take(2)
    row1 = ar.take(P)
    p1, trash, pint = ar.take(1), ar.take(1), ar.take(1)
    idx_u = idx.bitcast(U32)
    ident = e.ident
    bank_h1, bank_h2 = e.banks[0], e.banks[1]
    bank_w = e.banks[2:4]
    bank_r = e.banks[4:6]
    bank_m = e.banks[6:8]
    RC = 256

    S = e.sem
    c_zero, c_ld, c_iota, c_rdy = S("edge_zero"), S("edge_w_ld"), S("edge_iota"), S("edge_const")
    ld_dst = [S(f"ld_dst{h}") for h in range(2)]
    ld_src = [S(f"ld_src{h}") for h in range(2)]
    ld_sh = [S(f"ld_sh{h}") for h in range(2)]
    ld_a8 = [S(f"ld_a8{h}") for h in range(2)]
    srcf_rdy, srcoff_rdy = S("src_f_ready"), S("src_off_ready")
    h1_done, h2_done, silu1, silu2 = S("h1_done"), S("h2_done"), S("silu1"), S("silu2")
    w_done, rb_done, eq_done = S("w_done"), S("rows_done"), S("eq_done")
    mx_done, id_tmp, idx_rdy = S("last_edge"), S("idx_tmp"), S("idx_ready")
    sd_dve, sd_act = S("scaled_dve"), S("scaled_act")
    prod, comb, evac, cnt, cnt_done = S("products"), S("combined"), S("msg_ready"), S("count_ready"), S("counted")
    y_in = [[S(f"y_in{h}_{k}") for k in range(HALF)] for h in range(2)]
    scat = [S(f"scattered{r}") for r in range(TABLES)]

    idx0, msg0 = S("idx_first"), S("msg_zeroed")
    FIRST = 2
    PROD_C, EQ_C, COMB_C, EVAC_C, CNT_C = 4, 2, 4, 2, 2

    def slot_landed(eng, g, j, tables):
        for r in tables:
            eng.wait_ge(scat[r], 16 * (g - 3 + FIRST if j else g))

    with nc.Block() as block:
        @block.sync
        def _(sp):
            sp.wait_ge(c_zero, 1)
            for q in range(4):
                for t in range(2):
                    r = 16 * q + 8 * t
                    sp.dma_start(w1v[r:r + 8, q, 64 * t:64 * t + 64], io["fc1"]).then_inc(c_ld, 16)
            for t in range(2):
                sp.dma_start(w2bd[64 * t:64 * t + 64, 64 * t:64 * t + 64], io["fc2"]).then_inc(c_ld, 16)
                sp.dma_start(w3z[64 * t:64 * t + 64, t], io["fc3"]).then_inc(c_ld, 16)

            def load(buf, name, half, sem):
                src = io[name][bass.ds(half, 1)]
                dims = " ".join("xyz"[:len(src.shape) - 2])
                sp.dma_start(buf, src.rearrange(f"a p {dims} -> (a p) {dims}")).then_inc(sem, 16)

            for h in range(2):
                load(dst_i[h].bitcast(I32), "dst", h, ld_dst[h])
                load(a8[h][0:64], "a8", h, ld_a8[h])
                load(src_i[h].bitcast(I32), "src", h, ld_src[h])
                load(sh[h], "sh", h, ld_sh[h])
            with sp.Fori(0, NI - 1) as i:
                for h in range(2):
                    for k in range(HALF):
                        sp.wait_ge(y_in[h][k], 16 * i + 16)
                    load(dst_i[h].bitcast(I32), "dst", 2 * i + (2 + h), ld_dst[h])
                    sp.wait_ge(h1_done, 2 * i + (1 + h))
                    load(a8[h][0:64], "a8", 2 * i + (2 + h), ld_a8[h])
                for h in range(2):
                    sp.wait_ge(srcf_rdy, 2 * i + (1 + h))
                    load(src_i[h].bitcast(I32), "src", 2 * i + (2 + h), ld_src[h])
                    sp.wait_ge(comb, 16 * i + (8 * (h + 1) + COMB_C))
                    load(sh[h], "sh", 2 * i + (2 + h), ld_sh[h])

        @block.gpsimd
        def _(pool):
            for buf in (w1v, w2bd, w3z):
                last = pool.memset(buf, 0.0)
            last.then_inc(c_zero, 1)
            pool.memset(msg, 0.0).then_inc(msg0, 1)
            pool.iota(row1.bitcast(I32), pattern=[[1, P]], base=1, channel_multiplier=0)
            pool.iota(pint.bitcast(I32), pattern=[[0, 1]], base=0, channel_multiplier=1).then_inc(c_iota, 1)

            def gather(h, k, i, g):
                if k == 0:
                    pool.wait_ge(ld_dst[h], 16 * i + 16)
                if g is not None:
                    pool.wait_ge(prod, g + (PROD_C - 3))
                    pool.nop(nofuse=True)
                pool.indirect_dma_start(yb[:, h, k], None, e.y_d, bass.IndirectOffsetOnAxis(
                    ap=dst_i[h].bitcast(U32)[:, k:k + 1], axis=0)).then_inc(y_in[h][k], 16)

            def scatter(g, j, k):
                slot = 2 * (j % 4) + k
                if k == 0:
                    pool.wait_ge(idx_rdy, g + 1)
                    pool.wait_ge(cnt_done, g + (1 + CNT_C))
                pool.wait_ge(evac, 2 * g + (k + 1 + EVAC_C))
                pool.wait_ge(scat[k], 16 * g + 16 * FIRST)
                pool.nop(nofuse=True)
                pool.indirect_dma_start(e.agg_d[k], bass.IndirectOffsetOnAxis(ap=idx_u[:, slot:slot + 1], axis=0),
                                        msg[:, slot], None, compute_op=ALU.add).then_inc(scat[k], 16)

            def step(i, last):
                for j in range(HALF):
                    for k in range(2):
                        kk = 2 * (j % 4) + k
                        if j < 4:
                            gather(1, kk, i, 8 * i + j)
                        elif not last:
                            gather(0, kk, i + 1, 8 * i + j)
                        scatter(8 * i + j, j, k)

            pool.wait_ge(idx0, 4)
            pool.wait_ge(msg0, 1)
            for n in range(FIRST):
                for r in range(TABLES):
                    pool.wait_ge(scat[r], 16 * n)
                    pool.indirect_dma_start(e.agg_d[r], bass.IndirectOffsetOnAxis(ap=idx_u[:, 6 + r:7 + r], axis=0),
                                            msg[:, 6 + r], None, compute_op=ALU.add).then_inc(scat[r], 16)
            for k in range(HALF):
                gather(0, k, 0, None)
            with pool.Fori(0, NI - 1) as i:
                step(i, False)
            step(NI - 1, True)
            for r in range(TABLES):
                pool.wait_ge(scat[r], 16 * (8 * NI + FIRST))

        @block.vector
        def _(dve):
            dve.wait_ge(c_iota, 1)
            dve.tensor_copy(e.row1, row1.bitcast(I32)).then_inc(c_rdy, 1)
            dve.tensor_scalar(p1, pint.bitcast(I32), 1.0, None, ALU.add).then_inc(c_rdy, 1)
            dve.tensor_scalar(trash, pint.bitcast(I32), float(TRASH), None, ALU.add).then_inc(c_rdy, 1)
            dve.memset(e.ones_b[:], 1.0).then_inc(c_rdy, 1)
            dve.wait_ge(c_rdy, 4)
            dve.sem_inc(prod, PROD_C)
            dve.sem_inc(eq_done, EQ_C)
            dve.sem_inc(comb, COMB_C)
            dve.sem_inc(evac, EVAC_C)
            dve.sem_inc(cnt_done, CNT_C)
            for s in range(4, 8):
                dve.tensor_copy(idx_u[:, s:s + 1], trash).then_inc(idx0, 1)

            def sources(h, i, H):
                dve.wait_ge(ld_src[h], 16 * i + 16)
                dve.tensor_copy(src_f[h], src_i[h].bitcast(I32)).then_inc(srcf_rdy, 1)
                dve.wait_ge(srcf_rdy, H + 1)
                dve.tensor_scalar(src_off[h], src_f[h], trash, None, ALU.subtract).then_inc(srcoff_rdy, 1)

            def products(g, h, j, i):
                s, q = j % 2, j % 4
                dve.wait_ge(w_done, g + 1)
                for k in range(2):
                    dve.wait_ge(y_in[h][2 * q + k], 16 * i + 16)
                dve.wait_ge(comb, 2 * g + (COMB_C - 2))
                w = bank_w[s][:, :].rearrange("p (t f u) -> p t f u", t=2, f=4)
                y = yb[:, h, 2 * q:2 * q + 2]
                x = xb[:, s].rearrange("p t (h s u) -> p t h s u", h=2, s=4)
                dve.tensor_tensor(x[:, :, :, 0], w[:, :, 0:2],
                                  y[:, :, 0:64].rearrange("p t (o u) -> p t o u", o=1).broadcast_to([P, 2, 2, 64]),
                                  ALU.mult)
                for k in range(2):
                    last = dve.tensor_tensor(
                        x[:, k, :, 1:4],
                        w[:, k, 2:4].rearrange("p (f o) u -> p f o u", o=1).broadcast_to([P, 2, 3, 64]),
                        y[:, k, 64:256].rearrange("p (o c u) -> p o c u", o=1, c=3).broadcast_to([P, 2, 3, 64]),
                        ALU.mult)
                last.then_inc(prod, 1)

            def equality(g, h, j, H):
                s, q = j % 2, j % 4
                dve.wait_ge(srcoff_rdy, H + 1)
                dve.wait_ge(rb_done, g + 1)
                dve.wait_ge(comb, 2 * g + (COMB_C - 2))
                for k in range(2):
                    t = 2 * q + k
                    last = dve.tensor_scalar(eq[:, s, k], bank_r[s][:, k * P:(k + 1) * P], src_f[h][:, t:t + 1], None,
                                             ALU.is_equal)
                last.then_inc(eq_done, 1)
                dve.wait_ge(eq_done, g + (1 + EQ_C))
                for k in range(2):
                    for c in range(2):
                        last = dve.tensor_scalar(seq[:, s, k, c], eq[:, s, k], sh[h][:, 2 * q + k, c:c + 1], None,
                                                 ALU.mult)
                last.then_inc(sd_dve, 1)
                for k in range(2):
                    last = dve.tensor_tensor_reduce(e.junk[:, k], eq[:, s, k], e.row1, 1.0, 0.0, ALU.mult, ALU.max,
                                                    mx[:, s, k:k + 1])
                last.then_inc(mx_done, 1)
                dve.wait_ge(mx_done, g + 1)
                dve.scalar_tensor_tensor(out=tmp, in0=mx[:, s], scalar=p1, in1=src_off[h][:, 2 * q:2 * q + 2],
                                         op0=ALU.is_equal, op1=ALU.mult).then_inc(id_tmp, 1)
                dve.wait_ge(id_tmp, g + 1)
                slot_landed(dve, g, j, range(TABLES))
                b = 2 * (j % 4)
                dve.tensor_scalar(idx_u[:, b:b + 2], tmp, trash, None, ALU.add).then_inc(idx_rdy, 1)

            def counts(g, j):
                s = j % 2
                dve.wait_ge(cnt, g + 1)
                slot_landed(dve, g, j, range(TABLES))
                b = 2 * (j % 4)
                dve.tensor_copy(msg[:, b:b + 2, 512], bank_r[s][:, RC:RC + 2]).then_inc(cnt_done, 1)

            def step(i, last):
                for j in range(HALF):
                    if j == 1:
                        sources(1, i, 2 * i + 1)
                    if j == 5 and not last:
                        sources(0, i + 1, 2 * i + 2)
                    if j < 7 or not last:
                        nj = (j + 1) % HALF
                        nh, ni = nj // 4, i if j < 7 else i + 1
                        dve.wait_ge(ld_sh[nh], 16 * ni + 16)
                        equality(8 * i + (j + 1), nh, nj, 2 * i + (j + 1) // 4)
                        products(8 * i + (j + 1), nh, nj, ni)
                    counts(8 * i + j, j)

            sources(0, 0, 0)
            dve.wait_ge(ld_sh[0], 16)
            equality(0, 0, 0, 0)
            products(0, 0, 0, 0)
            with dve.Fori(0, NI - 1) as i:
                step(i, False)
            step(NI - 1, True)

        @block.scalar
        def _(act):
            def first(H):
                act.wait_ge(h1_done, H + 1)
                act.wait_ge(h2_done, H)
                act.activation(h1s, bank_h1[:, :], ACT.Silu, scale=float(8 ** -0.5)).then_inc(silu1, 1)

            def second(h, H, free):
                act.wait_ge(h2_done, H + 1)
                act.wait_ge(w_done, free)
                act.activation(h2T[h], bank_h2[:, :], ACT.Silu, scale=0.125).then_inc(silu2, 1)

            def scaled(g, h, j):
                s, q = j % 2, j % 4
                act.wait_ge(eq_done, g + (1 + EQ_C))
                act.wait_ge(comb, 2 * g + (COMB_C - 2))
                for k in range(2):
                    for c in range(2, 4):
                        last = act.activation(seq[:, s, k, c], eq[:, s, k], ACT.Copy,
                                              scale=sh[h][:, 2 * q + k, c:c + 1])
                last.then_inc(sd_act, 1)

            def evacuate(g, j):
                for k in range(2):
                    act.wait_ge(comb, 2 * g + (k + 1 + COMB_C))
                    slot_landed(act, g, j, [k])
                    act.activation(msg[:, 2 * (j % 4) + k, 0:512], bank_m[k][:, :], ACT.Copy).then_inc(evac, 1)

            def step(i, last):
                for j in range(HALF):
                    if j == 1:
                        first(2 * i + 1)
                    if j == 2:
                        second(1, 2 * i + 1, 8 * i)
                    if j == 5 and not last:
                        first(2 * i + 2)
                    if j == 6 and not last:
                        second(0, 2 * i + 2, 8 * i + 4)
                    if j < 7 or not last:
                        nj = (j + 1) % HALF
                        scaled(8 * i + (j + 1), nj // 4, nj)
                    evacuate(8 * i + j, j)

            act.wait_ge(c_rdy, 4)
            first(0)
            act.wait_ge(h2_done, 1)
            act.activation(h2T[0], bank_h2[:, :], ACT.Silu, scale=0.125).then_inc(silu2, 1)
            act.wait_ge(ld_sh[0], 16)
            scaled(0, 0, 0)
            with act.Fori(0, NI - 1) as i:
                step(i, False)
            step(NI - 1, True)

        @block.tensor
        def _(pe):
            def mlp1(h, i, H):
                pe.wait_ge(ld_a8[h], 16 * i + 16)
                pe.wait_ge(silu1, H)
                for q in range(4):
                    mm = pe.matmul(bank_h1[:, q * P:(q + 1) * P], w1v[0:64, q], a8[h][0:64], start=True, stop=True)
                mm.then_inc(h1_done, 1)

            def mlp2(H):
                pe.wait_ge(silu1, H + 1)
                pe.wait_ge(silu2, H)
                pe.matmul(bank_h2[:, :], w2bd, h1s, start=True, stop=True).then_inc(h2_done, 1)

            def stage(g, h, j, H):
                s, q = j % 2, j % 4
                if q == 0:
                    pe.wait_ge(silu2, H + 1)
                    pe.wait_ge(srcf_rdy, H + 1)
                pe.wait_ge(cnt_done, g + (CNT_C - 1))
                for k in range(2):
                    t = 2 * q + k
                    mm = pe.transpose(bank_r[s][:, k * P:(k + 1) * P], src_f[h][:, t:t + 1].broadcast_to([P, P]),
                                      ident[:])
                mm.then_inc(rb_done, 1)
                pe.wait_ge(prod, g + (PROD_C - 1))
                for k in range(2):
                    mm = pe.matmul(bank_w[s][:, k * D:(k + 1) * D], h2T[h][:, q * P:(q + 1) * P], w3z[:, k],
                                   start=True, stop=True)
                mm.then_inc(w_done, 1)

            def combine(g, j):
                s = j % 2
                pe.wait_ge(eq_done, g + (1 + EQ_C))
                for k in range(2):
                    mm = pe.matmul(bank_r[s][:, RC + k:RC + k + 1], eq[:, s, k], e.ones_b[:], start=True, stop=True)
                mm.then_inc(cnt, 1)
                pe.wait_ge(prod, g + (1 + PROD_C))
                pe.wait_ge(sd_dve, g + 1)
                pe.wait_ge(sd_act, g + 1)
                for k in range(2):
                    pe.wait_ge(evac, 2 * g + (k + EVAC_C - 1))
                    x = xb[:, s, k]
                    m = bank_m[k]
                    pe.matmul(m[:, 0:256], seq[:, s, k, 0], x[:, 0:256], start=True, stop=False,
                              skip_group_check=True)
                    z = x[:, 256:512].rearrange("p (s u) -> p s u", s=4)
                    o = m[:, 256:512].rearrange("p (s u) -> p s u", s=4)
                    for c in range(3):
                        mm = pe.matmul(o[:, c::3 - c], seq[:, s, k, c + 1], z[:, 0::c + 1][:, 0:2],
                                       start=False, stop=(c == 2), skip_group_check=True)
                    mm.then_inc(comb, 1)

            def step(i, last):
                for j in range(HALF):
                    if j == 1:
                        mlp1(1, i, 2 * i + 1)
                    if j == 2:
                        mlp2(2 * i + 1)
                    if j == 5 and not last:
                        mlp1(0, i + 1, 2 * i + 2)
                    if j == 6 and not last:
                        mlp2(2 * i + 2)
                    if j < 7 or not last:
                        nj = (j + 1) % HALF
                        stage(8 * i + (j + 1), nj // 4, nj, 2 * i + (j + 1) // 4)
                    combine(8 * i + j, j)

            pe.wait_ge(c_ld, 16 * 12)
            pe.wait_ge(c_rdy, 4)
            mlp1(0, 0, 0)
            mlp2(0)
            stage(0, 0, 0, 0)
            with pe.Fori(0, NI - 1) as i:
                step(i, False)
            step(NI - 1, True)



def phase_combine(nc, e):
    io, ar, S = e.io, e.arena, e.sem
    ar.reset()
    w2 = ar.take(4, P)
    agg = ar.take(G7, TABLES, ROW)
    sc = ar.take(G7, D)
    aggT = ar.take(2, 512)
    dg, rt, dn = ar.take(G7), ar.take(G7), ar.take(G7)
    junk = ar.take(D)
    ss, sv = e.stat[:, 4], e.stat[:, 5]
    ident = e.ident
    w_zero, w_ld, w_rdy = S("w2_zero"), S("w2_ld"), S("w2_ready")
    ld = [S(f"agg_in{k}") for k in range(G7)]
    summed, rooted, inv, t_done, aT, prod, g_rdy, sq = (S(n) for n in (
        "agg_sum", "deg_root", "deg_inverse", "agg_transposed", "aggT_ready", "w2_done", "g_ready", "g_squares"))
    b_t, b_r = e.banks[0:2], e.banks[2:4]

    with nc.Block() as block:
        @block.gpsimd
        def _(pool):
            pool.memset(w2, 0.0).then_inc(w_zero, 1)

        @block.sync
        def _(sp):
            sp.wait_ge(w_zero, 1)
            for c, r, k, name, top in ((0, 0, 0, "w2_s", 0), (0, 1, 1, "w2_v", 1), (1, 0, 0, "w2_v", 1),
                                       (1, 1, 1, "w2_v", 1), (2, 0, 0, "w2_v", 0), (2, 1, 1, "w2_v", 0),
                                       (3, 0, 1, "w2_v", 0), (3, 1, 0, "w2_s", 1)):
                sp.dma_start(w2[64 * r:64 * r + 64, c, 64 * k:64 * k + 64], io[name][64 * top:64 * top + 64, :]
                             ).then_inc(w_ld, 16)
            with sp.Fori(0, NT // G7) as it:
                for k in range(G7):
                    sp.wait_ge(sq, G7 * it)
                    for r in range(TABLES):
                        sp.dma_start(agg[:, k, r], e.agg_d[r][bass.ds(it * (G7 * P) + k * P, P), :]).then_inc(ld[k], 16)
                    sp.dma_start(sc[:, k], e.sc_d[bass.ds(it * (G7 * P) + k * P, P), :]).then_inc(ld[k], 16)

        @block.vector
        def _(dve):
            dve.wait_ge(w_ld, 16 * 8)
            scale = float(128 ** -0.5 / 8)
            dve.tensor_scalar(w2, w2, scale, None, ALU.mult).then_inc(w_rdy, 1)
            dve.wait_ge(w_rdy, 1)
            dve.tensor_scalar(w2[64:128, 3], w2[64:128, 3], INV_SQRT3, None, ALU.mult).then_inc(w_rdy, 1)

            def total(it, k):
                i = it * G7 + k
                dve.wait_ge(ld[k], 16 * (TABLES + 1) * (it + 1))
                dve.tensor_tensor(agg[:, k, 0, 0:513], agg[:, k, 0, 0:513], agg[:, k, 1, 0:513], ALU.add
                                  ).then_inc(summed, 1)
                dve.wait_ge(summed, 2 * i + 1)
                dve.tensor_scalar(dg[:, k:k + 1], agg[:, k, 0, 512:513], 1.0, None, ALU.max).then_inc(summed, 1)

            def node(it, k):
                i = it * G7 + k
                dve.wait_ge(rooted, i + 1)
                dve.reciprocal(dn[:, k:k + 1], rt[:, k:k + 1]).then_inc(inv, 1)
                dve.wait_ge(inv, i + 1)
                dve.wait_ge(prod, i + 1)
                dve.scalar_tensor_tensor(out=col(e.B, i * D, D), in0=b_r[k % 2][:, 0:D], scalar=dn[:, k:k + 1],
                                         in1=sc[:, k], op0=ALU.mult, op1=ALU.add).then_inc(g_rdy, 1)

            with dve.Fori(0, NT // G7) as it:
                for k in range(G7):
                    total(it, k)
                    if k:
                        node(it, k - 1)
                node(it, G7 - 1)

        @block.scalar
        def _(act):
            def squares(act, i):
                act.wait_ge(g_rdy, i + 1)
                act.wait_ge(sq, i)
                act.activation(junk[:, 0:64], col(e.B, i * D, 64), ACT.Square, accum_out=col(ss, i))
                act.activation(junk[:, 64:D], col(e.B, i * D + 64, 192), ACT.Square, accum_out=col(sv, i)
                               ).then_inc(sq, 1)

            with act.Fori(0, NT // G7) as it:
                for k in range(G7):
                    i = it * G7 + k
                    act.wait_ge(summed, 2 * i + 2)
                    act.activation(rt[:, k:k + 1], dg[:, k:k + 1], ACT.Sqrt).then_inc(rooted, 1)
                    act.wait_ge(t_done, i + 1)
                    act.wait_ge(prod, i - 1 if k else it * G7)
                    act.activation(aggT[:, k % 2], b_t[k % 2][:, :], ACT.Copy).then_inc(aT, 1)
                    if k:
                        squares(act, i - 1)
                squares(act, it * G7 + (G7 - 1))

        @block.tensor
        def _(pe):
            pe.wait_ge(w_rdy, 2)

            def project(it, k):
                i = it * G7 + k
                pe.wait_ge(aT, i + 1)
                pe.wait_ge(g_rdy, i - 1 if k else it * G7)
                b, a = b_r[k % 2], aggT[:, k % 2]
                o = b[:, 0:D]
                ends = b[:, 0:D].rearrange("p (s u) -> p s u", s=4)[:, 0::3]
                for c, out in enumerate((o[:, 0:128], o[:, 128:256], o[:, 64:192], ends)):
                    mm = pe.matmul(out, a[:, c * P:(c + 1) * P], w2[:, c], start=(c == 0), stop=(c == 3),
                                   skip_group_check=True)
                mm.then_inc(prod, 1)

            with pe.Fori(0, NT // G7) as it:
                for k in range(G7):
                    i = it * G7 + k
                    pe.wait_ge(summed, 2 * i + 1)
                    pe.wait_ge(aT, i - 1 if k else it * G7)
                    for c in range(4):
                        mm = pe.transpose(b_t[k % 2][:, c * P:(c + 1) * P], agg[:, k, 0, c * P:(c + 1) * P], ident[:])
                    mm.then_inc(t_done, 1)
                    if k:
                        project(it, k - 1)
                project(it, G7 - 1)


def phase_residual(nc, e):
    io, ar, S, st = e.io, e.arena, e.sem, e.stat
    ar.reset()
    gmul = ar.take(D)
    xs = ar.take(G7, D)
    bst, mean, var = ar.take(NT, 6), ar.take(NT), ar.take(NT)
    wr = ar.take(2, NE)
    br = ar.take(NE)
    row = ar.take(NE)
    eight = [ar.take(NE) for _ in range(6)]
    one = [ar.take(1) for _ in range(8)]
    pair = ar.take(2)
    sums = ar.take(2)
    ones = ar.take(P)
    nf2, ss, sv, rstd = st[:, 3], st[:, 4], st[:, 5], st[:, 0]
    dl, th, sv_r = st[:, 6], st[:, 7], st[:, 8]
    ident = e.ident
    w_ld, v, a = S("res_w_ld"), S("res_vec"), S("res_act")
    gn, x1, bs, x2, tt, cT = S("g_normed"), S("x1_ready"), S("x1_stats"), S("x2_ready"), S("x2_transposed"), S("x2T_ready")
    p, c_rdy, kept = S("route_pe"), S("route_const"), S("x2_kept")

    with nc.Block() as block:
        @block.sync
        def _(sp):
            sp.dma_start(gmul[:, 0:64], io["g_s"].broadcast_to([P, 64])).then_inc(w_ld, 16)
            for d in range(3):
                sp.dma_start(gmul[:, 64 * (d + 1):64 * (d + 2)], io["g_v"].broadcast_to([P, 64])).then_inc(w_ld, 16)
            sp.dma_start(wr, io["wr"].rearrange("(k p) n -> p k n", p=P)).then_inc(w_ld, 16)
            sp.dma_start(br[0:1], io["br"]).then_inc(w_ld, 16)

        @block.gpsimd
        def _(pool):
            pool.memset(ones, 1.0)
            pool.iota(row[0:1].bitcast(I32), pattern=[[1, NE]], base=0, channel_multiplier=0).then_inc(c_rdy, 1)
            with pool.Fori(0, NT) as i:
                pool.wait_ge(gn, 2 * i + 2)
                pool.tensor_tensor(col(e.A, i * D, D), col(e.A, i * D, D), col(e.B, i * D, D), ALU.add
                                   ).then_inc(x1, 1)
            with pool.Fori(0, NT // G7) as it:
                for k in range(G7):
                    i = it * G7 + k
                    pool.wait_ge(x2, i + 1)
                    pool.tensor_copy(col(e.B, i * D, D), xs[:, k]).then_inc(kept, 1)

        @block.vector
        def _(dve):
            link = linker(dve, v)
            link(dve.tensor_scalar(ss, ss, 1.0 / MUL, EPS, ALU.mult, ALU.add))
            link(dve.tensor_scalar(sv, sv, 1.0 / (3 * MUL), EPS, ALU.mult, ALU.add))
            dve.wait_ge(a, 3)
            link(dve.reciprocal(ss, ss))
            link(dve.reciprocal(sv_r, sv))
            link(dve.tensor_scalar(nf2, nf2, MIN_NORM, None, ALU.max))
            link(dve.reciprocal(dl, nf2))
            dve.wait_ge(a, 4)
            link(dve.tensor_scalar(th, th, MAXN, None, ALU.min))
            link(dve.tensor_tensor(dl, dl, th, ALU.mult))
            dve.wait_ge(w_ld, 16 * 6)
            with dve.Fori(0, NT) as i:
                dve.scalar_tensor_tensor(out=col(e.A, i * D, D), in0=col(e.C, i * D, D), scalar=col(dl, i),
                                         in1=col(e.A, i * D, D), op0=ALU.mult, op1=ALU.add).then_inc(gn, 1)
                dve.scalar_tensor_tensor(out=col(e.B, i * D, 64), in0=col(e.B, i * D, 64), scalar=col(ss, i),
                                         in1=gmul[:, 0:64], op0=ALU.mult, op1=ALU.mult)
                dve.scalar_tensor_tensor(out=col(e.B, i * D + 64, 192), in0=col(e.B, i * D + 64, 192),
                                         scalar=col(sv_r, i), in1=gmul[:, 64:D], op0=ALU.mult, op1=ALU.mult
                                         ).then_inc(gn, 1)
            bf = bst.rearrange("p a b -> p (a b)")
            with dve.Fori(0, NT) as i:
                dve.wait_ge(x1, i + 1)
                dve.bn_stats(col(bf, 6 * i, 6), col(e.A, i * D, D)).then_inc(bs, 1)
            dve.wait_ge(bs, NT)
            row_moments(link, dve, bst, mean, var, th)
            link(dve.tensor_scalar(rstd, var, EPS, None, ALU.add))
            dve.wait_ge(a, 5)
            link(dve.reciprocal(rstd, rstd))
            with dve.Fori(0, NT // G7) as it:
                for k in range(G7):
                    i = it * G7 + k
                    dve.wait_ge(tt, it * G7)
                    dve.wait_ge(kept, it * G7)
                    dve.tensor_scalar(xs[:, k], col(e.A, i * D, D), col(mean, i), col(rstd, i),
                                      ALU.subtract, ALU.mult).then_inc(x2, 1)
            dve.wait_ge(cT, NT)
            xc = e.C[:, :].rearrange("p (c n) -> p c n", c=2)
            link(dve.tensor_reduce(sums, xc[:, :, 0:N], AX.X, ALU.add))
            link(dve.tensor_scalar(sums, sums, 1.0 / N, None, ALU.mult))
            lg, ex, t1, t2, rw, ii = (z[0:1] for z in eight)
            mx, sm, i1, i2, v1, v2, e2, w1 = (z[0:1] for z in one)
            dve.wait_ge(c_rdy, 1)
            link(dve.tensor_copy(ii, row[0:1].bitcast(I32)))
            dve.wait_ge(p, 1)
            link(dve.tensor_tensor(lg, e.banks[4][0:1, 0:NE], br[0:1], ALU.add))
            link(dve.tensor_reduce(mx, lg, AX.X, ALU.max))
            link(dve.tensor_scalar(lg, lg, mx, None, ALU.subtract))
            dve.wait_ge(a, 6)
            link(dve.reciprocal(sm, sm))
            link(dve.tensor_scalar(rw, ex, sm, None, ALU.mult))
            link(dve.tensor_scalar(t1, rw, float(N), None, ALU.mult))
            link(dve.tensor_scalar(t2, t1, CAPACITY, None, ALU.is_gt))
            link(dve.tensor_scalar(t1, t1, CAPACITY, None, ALU.max))
            link(dve.reciprocal(t1, t1))
            link(dve.tensor_scalar(t1, t1, CAPACITY, -1.0, ALU.mult, ALU.add))
            link(dve.tensor_tensor(t1, t1, t2, ALU.mult))
            link(dve.tensor_scalar(t1, t1, 1.0, None, ALU.add))
            link(dve.tensor_tensor(rw, rw, t1, ALU.mult))
            link(dve.tensor_reduce(mx, rw, AX.X, ALU.max))
            link(dve.tensor_scalar(rw, rw, mx, None, ALU.subtract))
            dve.wait_ge(a, 7)
            link(dve.reciprocal(sm, sm))
            link(dve.tensor_scalar(rw, ex, sm, None, ALU.mult))
            for n, (val, at) in enumerate(((v1, i1), (v2, i2))):
                link(dve.tensor_reduce(val, rw, AX.X, ALU.max))
                link(dve.tensor_scalar(t1, rw, val, -1000.0, ALU.is_equal, ALU.mult))
                link(dve.tensor_tensor(t1, t1, ii, ALU.add))
                link(dve.tensor_reduce(at, t1, AX.X, ALU.min))
                link(dve.tensor_scalar(at, at, 1000.0, None, ALU.add))
                if n == 0:
                    link(dve.tensor_scalar(t1, ii, at, -4.0, ALU.is_equal, ALU.mult))
                    link(dve.tensor_tensor(rw, rw, t1, ALU.add))
            link(dve.tensor_copy(e.pick[0:1, 0:1], i1))
            link(dve.tensor_copy(e.pick[0:1, 1:2], i2))
            link(dve.tensor_tensor(e2, v2, v1, ALU.subtract))
            dve.wait_ge(a, 8)
            link(dve.tensor_scalar(w1, e2, 1.0, None, ALU.add))
            link(dve.reciprocal(pair[0:1, 0:1], w1))
            link(dve.tensor_tensor(pair[0:1, 1:2], e2, pair[0:1, 0:1], ALU.mult))
            dve.wait_ge(p, 2)
            link(dve.tensor_copy(e.weight[:], e.banks[5][:, 0:2]))

        @block.scalar
        def _(act):
            ex, sm, lg, rw, e2 = eight[1][0:1], one[1][0:1], eight[0][0:1], eight[4][0:1], one[6][0:1]
            act.wait_ge(v, 2)
            act.activation(ss, ss, ACT.Sqrt).then_inc(a, 1)
            act.activation(sv, sv, ACT.Sqrt).then_inc(a, 1)
            act.activation(nf2, nf2, ACT.Sqrt).then_inc(a, 1)
            act.wait_ge(v, 5)
            act.activation(th, nf2, ACT.Tanh).then_inc(a, 1)
            act.wait_ge(v, MOMENTS + 9)
            act.activation(rstd, rstd, ACT.Sqrt).then_inc(a, 1)
            act.wait_ge(gn, 2 * NT)
            xc = e.C[:, :].rearrange("p (c n) -> p c n", c=2)

            def out(i, s):
                act.wait_ge(tt, i + 1)
                act.activation(xc[:, :, bass.ds(i * P, P)],
                               e.banks[s][:, 0:D].rearrange("p (c n) -> p c n", c=2), ACT.Copy).then_inc(cT, 1)

            with act.Fori(0, NT // G7) as it:
                for k in range(G7):
                    out(it * G7 + k, k % 4)
            act.wait_ge(v, MOMENTS + 16)
            act.activation(ex, lg, ACT.Exp, accum_out=sm).then_inc(a, 1)
            act.wait_ge(v, MOMENTS + 28)
            act.activation(ex, rw, ACT.Exp, accum_out=sm).then_inc(a, 1)
            act.wait_ge(v, MOMENTS + 45)
            act.activation(e2, e2, ACT.Exp).then_inc(a, 1)

        @block.tensor
        def _(pe):
            def tile(i, k):
                pe.wait_ge(x2, i + 1)
                pe.wait_ge(cT, i - 3 if k > 3 else i - k)
                for c in range(2):
                    mm = pe.transpose(e.banks[k % 4][:, c * P:(c + 1) * P], xs[:, k, c * P:(c + 1) * P], ident[:])
                mm.then_inc(tt, 1)

            with pe.Fori(0, NT // G7) as it:
                for k in range(G7):
                    tile(it * G7 + k, k)
            pe.wait_ge(v, MOMENTS + 12)
            pe.wait_ge(w_ld, 16 * 6)
            for c in range(2):
                mm = pe.matmul(e.banks[4][0:1, 0:NE], sums[:, c:c + 1], wr[:, c], start=(c == 0), stop=(c == 1))
            mm.then_inc(p, 1)
            pe.wait_ge(v, MOMENTS + 48)
            pe.matmul(e.banks[5][:, 0:2], ones[0:1], pair[0:1], start=True, stop=True).then_inc(p, 1)


def phase_experts(nc, e):
    io, ar, S = e.io, e.arena, e.sem
    ar.reset()
    w1 = ar.take(2, 2, FF)
    w2 = ar.take(2, 4, D)
    hT = [ar.take(2, 4, 512) for _ in range(2)]
    b1 = ar.take(2, 4)
    b2 = ar.take(2, D)
    b2c = ar.take(D)
    lng, lnb = ar.take(D), ar.take(D)
    bst, mean, var = ar.take(NT, 6), ar.take(NT), ar.take(NT)
    rstd, nmr = e.stat[:, 0], e.stat[:, 1]
    z1 = w1.rearrange("p a b c -> p (a b c)")[:, 0:G7 * D].rearrange("p (k d) -> p k d", d=D)
    xc = e.C[:, :].rearrange("p (c n) -> p c n", c=2)
    bank_h, bank_o = e.banks[0:4], e.banks[4:8]
    STEPS, TAIL = NT // 8, 1
    w_ld, w_rdy, v, a = S("ffn_w_ld"), S("ffn_w_ready"), S("ffn_vec"), S("ffn_act")
    h_done, h_rdy, o_done, z_rdy, bs = S("ffn_h"), S("ffn_gelu"), S("ffn_out"), S("z_ready"), S("z_stats")
    xb, n_rdy, g_rdy, o_rdy = S("x1_beta"), S("z_normed"), S("z_gamma"), S("out_ready")
    st = [S(f"out_stored{k}") for k in range(G7)]

    with nc.Block() as block:
        @block.sync
        def _(sp):
            for n in range(2):
                ex = sp.value_load(e.pick[0:1, n:n + 1], min_val=0, max_val=NE - 1)
                sp.dma_start(w1[:, n], io["ffn1"][bass.ds(ex, 1)].rearrange("o (k p) f -> p (o k) f", p=P)
                             ).then_inc(w_ld, 16)
                sp.dma_start(w2[:, n], io["ffn2"][bass.ds(ex, 1)].rearrange("o (f p) d -> p (o f) d", p=P)
                             ).then_inc(w_ld, 16)
                sp.dma_start(b1[:, n], io["ffb1"][bass.ds(ex, 1)].rearrange("o p f -> p (o f)")).then_inc(w_ld, 16)
                sp.dma_start(b2[:, n], io["ffb2"][bass.ds(ex, 1), :].broadcast_to([P, D])).then_inc(w_ld, 16)
            sp.dma_start(lng, io["ln_g"].broadcast_to([P, D])).then_inc(w_ld, 16)
            sp.dma_start(lnb, io["ln_b"].broadcast_to([P, D])).then_inc(w_ld, 16)
            with sp.Fori(0, NT // G7) as it:
                for k in range(G7):
                    sp.wait_ge(o_rdy, G7 * it + (k + 1))
                    sp.dma_start(io["out"][bass.ds(it * (G7 * P) + k * P, P), :], z1[:, k]).then_inc(st[k], 16)
            for k in range(G7):
                sp.wait_ge(st[k], 16 * (NT // G7))

        @block.gpsimd
        def _(pool):
            pool.wait_ge(w_ld, 160)
            with pool.Fori(0, NT) as i:
                pool.tensor_tensor(col(e.A, i * D, D), col(e.A, i * D, D), lnb, ALU.add).then_inc(xb, 1)

        @block.vector
        def _(dve):
            dve.wait_ge(w_ld, 160)
            for n in range(2):
                dve.tensor_scalar(w2[:, n], w2[:, n], e.weight[:, n:n + 1], None, ALU.mult).then_inc(w_rdy, 1)
            dve.tensor_scalar(b2[:, 0], b2[:, 0], e.weight[:, 0:1], None, ALU.mult).then_inc(w_rdy, 1)
            dve.wait_ge(w_rdy, 3)
            dve.scalar_tensor_tensor(out=b2c, in0=b2[:, 1], scalar=e.weight[:, 1:2], in1=b2[:, 0], op0=ALU.mult,
                                     op1=ALU.add).then_inc(w_rdy, 1)
            dve.wait_ge(w_rdy, 4)
            bf = bst.rearrange("p a b -> p (a b)")

            def tile(i, k):
                z = col(e.B, i * D, D)
                dve.tensor_tensor(z, z, b2c, ALU.add).then_inc(z_rdy, 1)
                dve.wait_ge(o_done, i + 1)
                dve.wait_ge(z_rdy, 2 * i + 1)
                dve.tensor_tensor(z, bank_o[k % 4][:, 0:D], z, ALU.add).then_inc(z_rdy, 1)
                dve.wait_ge(z_rdy, 2 * i + 2)
                dve.bn_stats(col(bf, 6 * i, 6), z).then_inc(bs, 1)

            with dve.Fori(0, STEPS) as s:
                for j in range(8):
                    tile(8 * s + j, j)
            tile(NT - 1, 0)
            dve.wait_ge(bs, NT)
            link = linker(dve, v)
            row_moments(link, dve, bst, mean, var, nmr)
            link(dve.tensor_scalar(rstd, var, EPS, None, ALU.add))
            dve.wait_ge(a, 1)
            link(dve.reciprocal(rstd, rstd))
            link(dve.tensor_tensor(nmr, mean, rstd, ALU.mult))
            link(dve.tensor_scalar(nmr, nmr, -1.0, None, ALU.mult))
            with dve.Fori(0, NT // G7) as it:
                for k in range(G7):
                    i = it * G7 + k
                    dve.wait_ge(n_rdy, i + 1)
                    dve.tensor_tensor(z1[:, k], z1[:, k], lng, ALU.mult).then_inc(g_rdy, 1)
                    if k == 0:
                        dve.wait_ge(xb, NT)
                    dve.wait_ge(g_rdy, i + 1)
                    dve.tensor_tensor(z1[:, k], z1[:, k], col(e.A, i * D, D), ALU.add).then_inc(o_rdy, 1)

        @block.scalar
        def _(act):
            act.wait_ge(w_ld, 160)

            def gelu(n, s, w, free):
                act.wait_ge(o_done, free)
                for m in range(8):
                    x, f = m // 4, m % 4
                    act.wait_ge(h_done, 8 * n + (m + 1))
                    act.activation(hT[s][:, x, f, 0:w], bank_h[m % 4][:, 0:w], ACT.Gelu, bias=b1[:, x, f:f + 1]
                                   ).then_inc(h_rdy, 1)

            gelu(0, 0, 512, 0)
            with act.Fori(0, STEPS - 1) as s:
                for c in range(2):
                    gelu(2 * s + (c + 1), 1 - c, 512, 8 * s + 4 * c)
            gelu(2 * STEPS - 1, 1, 512, 8 * (STEPS - 1))
            gelu(2 * STEPS, 0, P, 8 * (STEPS - 1) + 4)
            act.wait_ge(v, MOMENTS + 1)
            act.activation(rstd, rstd, ACT.Sqrt).then_inc(a, 1)
            act.wait_ge(v, MOMENTS + 4)
            with act.Fori(0, NT // G7) as it:
                for k in range(G7):
                    i = it * G7 + k
                    act.wait_ge(st[k], 16 * it)
                    act.activation(z1[:, k], col(e.B, i * D, D), ACT.Identity, scale=col(rstd, i), bias=col(nmr, i)
                                   ).then_inc(n_rdy, 1)

        @block.tensor
        def _(pe):
            def up(n, w):
                for m in range(8):
                    x, f = m // 4, m % 4
                    pe.wait_ge(h_rdy, 8 * n + (m - 3) if m > 3 else 8 * n)
                    for k in range(2):
                        mm = pe.matmul(bank_h[m % 4][:, 0:w], w1[:, x, k, f * P:(f + 1) * P],
                                       xc[:, k, bass.ds(n * 512, w)], start=(k == 0), stop=(k == 1))
                    mm.then_inc(h_done, 1)

            def down(n, s, tiles):
                pe.wait_ge(h_rdy, 8 * n + 8)
                pe.wait_ge(z_rdy, 8 * n)
                for t in range(tiles):
                    for m in range(8):
                        mm = pe.matmul(bank_o[t][:, 0:D], hT[s][:, m // 4, m % 4, t * P:(t + 1) * P],
                                       w2[:, m // 4, m % 4], start=(m == 0), stop=(m == 7))
                    mm.then_inc(o_done, 1)

            pe.wait_ge(w_rdy, 4)
            up(0, 512)
            with pe.Fori(0, STEPS - 1) as s:
                for c in range(2):
                    up(2 * s + (c + 1), 512)
                    down(2 * s + c, c, 4)
            up(2 * STEPS - 1, 512)
            down(2 * STEPS - 2, 0, 4)
            up(2 * STEPS, P)
            down(2 * STEPS - 1, 1, 4)
            down(2 * STEPS, 0, 1)


def build(nc, io, upto=99):
    with ExitStack() as ctx:
        e = setup(nc, ctx, io)
        for n, phase in enumerate(PHASES):
            if n < upto:
                phase(nc, e)


PHASES = [phase_nodes, phase_convolve, phase_mix, phase_edges, phase_combine, phase_residual,
          phase_experts]


def _layout(inputs):
    import numpy as _np
    g = {k: _np.asarray(v) for k, v in inputs.items()}

    def feat(a, axis):
        a = _np.moveaxis(a, axis, -1)
        s, v = a[..., :MUL], a[..., MUL:]
        v = v.reshape(v.shape[:-1] + (MUL, 3)).swapaxes(-1, -2).reshape(v.shape)
        return _np.ascontiguousarray(_np.moveaxis(_np.concatenate([s, v], -1), -1, axis))

    def edges(a, pad):
        full = _np.full((NH * HALF * P,) + a.shape[1:], pad, a.dtype)
        full[:E] = a
        return _np.ascontiguousarray(full.reshape((NH, HALF, P) + a.shape[1:]).swapaxes(1, 2))

    x = _np.zeros((NP, D), g["x"].dtype)
    x[:N] = feat(g["x"], 1)
    a8 = edges(g["edge_attr_8"], 0)
    qkv = feat(g["L0_mix_w_qkv"], 1)
    row = lambda a: _np.ascontiguousarray(a.reshape(1, -1))
    out = {
        "x": x,
        "src": edges(g["src"], N),
        "dst": edges(g["dst"], 0),
        "sh": edges(g["edge_attr_4"], 0),
        "a8": _np.ascontiguousarray(a8.transpose(0, 2, 3, 1).reshape(NH, HALF * 8, P)),
        "w1_s": g["L0_gnn_w1_s"], "w1_v": g["L0_gnn_w1_v"], "wsc_s": g["L0_gnn_wsc_s"], "wsc_v": g["L0_gnn_wsc_v"],
        "w2_s": g["L0_gnn_w2_s"], "w2_v": g["L0_gnn_w2_v"],
        "fc1": g["L0_gnn_fc_w1"], "fc2": g["L0_gnn_fc_w2"], "fc3": g["L0_gnn_fc_w3"],
        "g_s": row(g["L0_gnn_g_s"]), "g_v": row(g["L0_gnn_g_v"]),
        "w_qkv": _np.ascontiguousarray(qkv.transpose(2, 1, 0)),
        "bn_g": _np.ascontiguousarray(g["L0_mix_bn_gamma"].reshape(NCH, P).T),
        "bn_b": _np.ascontiguousarray(g["L0_mix_bn_beta"].reshape(NCH, P).T),
        "w_dw": _np.ascontiguousarray(g["L0_mix_w_dw"].reshape(NCH, P, 5).transpose(2, 1, 0)),
        "w_pw": _np.ascontiguousarray(g["L0_mix_w_pw"].reshape(NCH, 4, DIM, DIM).transpose(1, 3, 0, 2)),
        "w_res": _np.ascontiguousarray(feat(g["L0_mix_w_res"], 0).reshape(D, GROUPS * DIM).T),
        "b_res": row(feat(g["L0_mix_b_res"], 0)),
        "wr": feat(g["L0_ffn_Wr"], 0), "br": row(g["L0_ffn_br"]),
        "ffn1": feat(g["L0_ffn_W1"], 1),
        "ffb1": _np.ascontiguousarray(g["L0_ffn_b1"].reshape(NE, 4, P).swapaxes(1, 2)),
        "ffn2": feat(g["L0_ffn_W2"], 2), "ffb2": feat(g["L0_ffn_b2"], 1),
        "ln_g": row(feat(g["L0_ffn_gamma"], 0)), "ln_b": row(feat(g["L0_ffn_beta"], 0)),
    }
    return out


def _result(out):
    import numpy as _np
    s, v = out[:N, :MUL], out[:N, MUL:]
    v = v.reshape(N, 3, MUL).swapaxes(1, 2).reshape(N, 3 * MUL)
    return _np.ascontiguousarray(_np.concatenate([s, v], 1))


def kernel(**inputs):
    import concourse.bacc as _bacc
    from concourse import mybir as _mybir
    from concourse.bass_utils import run_bass_kernel_spmd as _run

    nc = _bacc.Bacc("TRN2", target_bir_lowering=False, num_devices=1)
    arrays, io = {}, {}
    for name, a in _layout(inputs).items():
        arrays[f"in_{name}_dram"] = a
        io[name] = nc.dram_tensor(f"in_{name}_dram", a.shape, _mybir.dt.from_np(a.dtype), kind="ExternalInput").ap()
    io["out"] = nc.dram_tensor("out_0_dram", (NP, D), _mybir.dt.float32, kind="ExternalOutput").ap()
    build(nc, io)
    r = _run(nc, [arrays], core_ids=[0])
    return _result(r.results[0]["out_0_dram"])
```

```python
from contextlib import ExitStack

import numpy as np

import concourse.bass as bass
from concourse import mybir

F32 = mybir.dt.float32
BF16 = mybir.dt.bfloat16
I32 = mybir.dt.int32
U32 = mybir.dt.uint32
ALU = mybir.AluOpType
ACT = mybir.ActivationFunctionType
AX = mybir.AxisListType

P = 128
N = 6250
D = 256
MUL = 64
E = 206250
NT = -(-N // P)
NP = NT * P
LAST = N - (NT - 1) * P
G7 = 7
HALF = 8
STEP = 2 * HALF
NH = 2 * (-(-E // (STEP * P)))
NI = NH // 2
TABLES = 3
TABLE = [0, 1, 2] * 4 + [0, 1, 0, 2]
ROW = 516
TRASH = NP
TROWS = NP + P
CH = 768
NCH = CH // P
GROUPS = 16
DIM = 32
FF = 512
NE = 8
EPS = 1e-5
MIN_NORM = 1e-15
MAXN = float(np.float32(1.0 - 1e-5))
ATANH_MAXN = float(np.arctanh(np.float64(np.float32(1.0 - 1e-5))))
INV_SQRT3 = 0.5773502691896258
CAPACITY = float(-(-int(N * 1.25) // NE)) if (N * 1.25) == int(N * 1.25) else float(int(N * 1.25 / NE) + 1)


class Arena:

    def __init__(self, tensor, size):
        self.tensor, self.size, self.at = tensor, size, 0

    def reset(self):
        self.at = 0

    def take(self, *shape):
        n = int(np.prod(shape))
        ap = self.tensor[:, self.at:self.at + n]
        self.at += n
        assert self.at <= self.size, (self.at, self.size)
        if len(shape) == 1:
            return ap
        names = "abcd"[:len(shape)]
        spec = f"p ({' '.join(names)}) -> p {' '.join(names)}"
        return ap.rearrange(spec, **{names[i]: shape[i] for i in range(1, len(shape))})


class Env:
    pass


def free(eng, sem, value):
    if not isinstance(value, int) or value > 0:
        eng.wait_ge(sem, value)


def scatters(i, t):
    return TABLE.count(TABLE[t]) * i + TABLE[:t].count(TABLE[t])


def steps(eng, n, step):
    step(0)
    with eng.Fori(1, n) as i:
        step(i)


def col(ap, i, n=1):
    return ap[:, bass.ds(i, n)]


def setup(nc, ctx, io):
    e = Env()
    e.io = io
    e.sb = lambda n, s, d=F32: ctx.enter_context(nc.sbuf_tensor(n, s, d))
    e.ps = lambda n, s, d=F32: ctx.enter_context(nc.psum_tensor(n, s, d))
    e.sem = lambda n: ctx.enter_context(nc.semaphore(n))
    e.dram = lambda n, s: nc.dram_tensor(n, s, F32).ap()
    e.A = e.sb("region_a", [P, NT * D])
    e.B = e.sb("region_b", [P, 2 * NP])
    e.C = e.sb("region_c", [P, 2 * NP])
    e.arena = Arena(e.sb("scratch", [P, 14100]), 14100)
    e.ident = e.sb("ident", [P, P])
    e.pick = e.sb("picked_experts", [1, 2], I32)
    e.weight = e.sb("expert_weights", [P, 2])
    e.bn = e.sb("bn_scale_shift", [P, 2, NCH])
    e.eq = e.sb("equal_src", [P, 2, 2, P], BF16)
    e.row1 = e.sb("row_index", [P, P], BF16)[:, :]
    e.ident_b = e.sb("ident_bf16", [P, P], BF16)
    e.src_hl = e.sb("src_high_low", [P, 2, 2, HALF], BF16)
    e.junk = e.sb("junk", [P, 2, P], BF16)
    e.stat = e.sb("stat", [P, 12, NT])
    e.banks = [e.ps(f"bank{i}", [P, 512]) for i in range(8)]
    e.y_d = e.dram("y_d", [NP, D])
    e.sc_d = e.dram("sc_d", [NP, D])
    e.conv_d = e.dram("conv_d", [NCH, P, NP])
    e.agg_d = [e.dram(f"agg{r}_d", [TROWS, ROW]) for r in range(TABLES)]
    return e


def linker(eng, sem):
    n = [0]

    def link(ins):
        n[0] += 1
        ins.then_inc(sem, 1)
        eng.wait_ge(sem, n[0])
    return link


def row_moments(link, dve, bst, mean, var, tmp):
    link(dve.tensor_tensor(mean, bst[:, :, 1], bst[:, :, 4], ALU.add))
    link(dve.tensor_scalar(mean, mean, 0.5, None, ALU.mult))
    link(dve.tensor_tensor(tmp, mean, bst[:, :, 1], ALU.subtract))
    link(dve.tensor_tensor(tmp, tmp, tmp, ALU.mult))
    link(dve.tensor_tensor(var, bst[:, :, 2], bst[:, :, 5], ALU.add))
    link(dve.tensor_scalar(var, var, 1.0 / D, None, ALU.mult))
    link(dve.tensor_tensor(var, var, tmp, ALU.add))


MOMENTS = 7


def phase_nodes(nc, e):
    io, ar, st = e.io, e.arena, e.stat
    ar.reset()
    wy = ar.take(2, D)
    xn = ar.take(G7, D)
    hin = ar.take(G7, D)
    xnT = ar.take(2, 2, P)
    ysc = ar.take(G7, 2, D)
    bst = ar.take(NT, 6)
    mean, var = ar.take(NT), ar.take(NT)
    s1, s2, q, l1, l2, sq, ser, msk, e2 = (ar.take(NT) for _ in range(9))
    zero = e.C[:, 0:5 * ROW]
    rstd, ascale, norm = st[:, 0], st[:, 1], st[:, 2]
    ident = e.ident
    x_v = io["x"].rearrange("(t p) d -> p t d", p=P)
    x_ld, w_ld, z_ld = e.sem("x_ld"), e.sem("wy_ld"), e.sem("table_zeroed")
    w_zero, z_zero, id0, id1 = e.sem("wy_zero"), e.sem("zero_tile"), e.sem("ident0"), e.sem("ident_ready")
    bs_done, v, a = e.sem("bn_done"), e.sem("nodes_vec"), e.sem("nodes_act")
    xn_rdy, hin_rdy, t_done, xnT_rdy, hT_rdy = (e.sem(n) for n in (
        "xn_ready", "hin_ready", "node_transposed", "xnT_ready", "hinT_ready"))
    y_done, ysc_rdy = e.sem("y_done"), e.sem("ysc_ready")
    st_y = [e.sem(f"ysc_stored{k}") for k in range(G7)]
    e.v_total = 0

    with nc.Block() as block:
        @block.sync
        def _(sp):
            for g in range(NT // G7):
                sp.dma_start(e.A[:, g * G7 * D:(g + 1) * G7 * D].rearrange("p (t d) -> p t d", d=D),
                             x_v[:, g * G7:(g + 1) * G7, :]).then_inc(x_ld, 16)
            sp.wait_ge(w_zero, 1)
            for c, top in ((0, "s"), (1, "v")):
                for h, name in ((0, "w1"), (1, "wsc")):
                    sp.dma_start(wy[0:64, c, h * P:h * P + 64], io[f"{name}_{top}"]).then_inc(w_ld, 16)
                    sp.dma_start(wy[64:128, c, h * P + 64:h * P + 128], io[f"{name}_v"]).then_inc(w_ld, 16)
            sp.wait_ge(z_zero, 1)
            for r in range(TABLES):
                sp.dma_start(e.agg_d[r].rearrange("(p a b) c -> p a (b c)", p=P, b=5),
                             zero.rearrange("p (a n) -> p a n", a=1).broadcast_to([P, TROWS // P // 5, 5 * ROW])
                             ).then_inc(z_ld, 16)

            def each(it):
                for k in range(G7):
                    sp.wait_ge(ysc_rdy, G7 * it + (k + 1))
                    sp.dma_start(e.y_d[bass.ds(it * (G7 * P) + k * P, P), :], ysc[:, k, 0]).then_inc(st_y[k], 16)
                    sp.dma_start(e.sc_d[bass.ds(it * (G7 * P) + k * P, P), :], ysc[:, k, 1]).then_inc(st_y[k], 16)
            steps(sp, NT // G7, each)
            for k in range(G7):
                sp.wait_ge(st_y[k], 32 * (NT // G7))
            sp.wait_ge(z_ld, 16 * TABLES)

        @block.gpsimd
        def _(pool):
            pool.memset(ident[:], 0.0).then_inc(id0, 1)
            pool.memset(wy, 0.0).then_inc(w_zero, 1)
            pool.memset(zero, 0.0).then_inc(z_zero, 1)
            pool.wait_ge(id0, 1)
            pool.affine_select(out=ident[:], in_=ident[:], compare_op=ALU.not_equal, fill=1.0, base=0,
                               pattern=[[-1, P]], channel_multiplier=1).then_inc(id1, 1)

        def evac(dve, it, k):
            i = it * G7 + k
            dve.wait_ge(t_done, i + 1)
            free(dve, y_done, i - 1 if k else it * G7)
            dve.tensor_copy(xnT[:, k % 2], e.banks[k % 2][:, 0:D].rearrange("p (c n) -> p c n", c=2)).then_inc(xnT_rdy, 1)

        @block.vector
        def _(dve):
            link = linker(dve, v)
            dve.wait_ge(x_ld, 16 * (NT // G7))
            with dve.Fori(0, NT) as i:
                dve.bn_stats(col(bst.rearrange("p a b -> p (a b)"), 6 * i, 6),
                             col(e.A, i * D, D)).then_inc(bs_done, 1)
            dve.wait_ge(bs_done, NT)
            row_moments(link, dve, bst, mean, var, q)
            link(dve.tensor_scalar(s1, var, EPS, None, ALU.add))
            dve.wait_ge(a, 2)
            link(dve.reciprocal(rstd, s1))
            link(dve.tensor_tensor(norm, s2, rstd, ALU.mult))
            link(dve.tensor_scalar(norm, norm, MIN_NORM, None, ALU.max))
            link(dve.tensor_scalar(q, norm, MAXN, None, ALU.min))
            dve.wait_ge(a, 4)
            link(dve.tensor_tensor(l1, l1, l2, ALU.subtract))
            link(dve.tensor_scalar(l1, l1, 0.5, None, ALU.mult))
            link(dve.tensor_tensor(sq, q, q, ALU.mult))
            link(dve.tensor_scalar(ser, sq, 0.2, 1.0 / 3.0, ALU.mult, ALU.add))
            link(dve.tensor_tensor(ser, ser, sq, ALU.mult))
            link(dve.tensor_scalar(ser, ser, 1.0, None, ALU.add))
            link(dve.tensor_tensor(ser, ser, q, ALU.mult))
            link(dve.tensor_scalar(msk, q, 0.03, None, ALU.is_lt))
            link(dve.tensor_tensor(ser, ser, l1, ALU.subtract))
            link(dve.tensor_tensor(ser, ser, msk, ALU.mult))
            link(dve.tensor_tensor(l1, l1, ser, ALU.add))
            link(dve.reciprocal(e2, norm))
            link(dve.tensor_tensor(ascale, l1, e2, ALU.mult))

            def each(it):
                for k in range(G7):
                    i = it * G7 + k
                    free(dve, t_done, it * G7)
                    free(dve, hin_rdy, it * G7)
                    dve.tensor_scalar(xn[:, k], col(e.A, i * D, D), col(mean, i), col(rstd, i),
                                      ALU.subtract, ALU.mult).then_inc(xn_rdy, 1)
                    if k:
                        evac(dve, it, k - 1)
                evac(dve, it, G7 - 1)
            steps(dve, NT // G7, each)

        @block.scalar
        def _(act):
            act.wait_ge(v, MOMENTS + 1)
            act.activation(s1, s1, ACT.Sqrt).then_inc(a, 1)
            act.activation(s2, var, ACT.Sqrt, scale=float(D)).then_inc(a, 1)
            act.wait_ge(v, MOMENTS + 5)
            act.activation(l1, q, ACT.Ln, bias=1.0).then_inc(a, 1)
            act.activation(l2, q, ACT.Ln, bias=1.0, scale=-1.0).then_inc(a, 1)
            act.wait_ge(v, MOMENTS + 18)
            hT = e.B[:, :].rearrange("p (c n) -> p c n", c=2)

            def out(it, k):
                i = it * G7 + k
                act.wait_ge(t_done, i + 1)
                act.activation(hT[:, :, bass.ds(i * P, P)],
                               e.banks[4 + k % 2][:, 0:D].rearrange("p (c n) -> p c n", c=2),
                               ACT.Copy).then_inc(hT_rdy, 1)
                act.wait_ge(y_done, i + 1)
                free(act, st_y[k], 32 * it)
                act.activation(ysc[:, k].rearrange("p h (c n) -> p c h n", c=2),
                               e.banks[2 + k % 2][:, :].rearrange("p (c h n) -> p c h n", c=2, h=2),
                               ACT.Copy, scale=0.125).then_inc(ysc_rdy, 1)

            def each(it):
                for k in range(G7):
                    i = it * G7 + k
                    act.wait_ge(xn_rdy, i + 1)
                    act.activation(hin[:, k], xn[:, k], ACT.Copy, scale=col(ascale, i)).then_inc(hin_rdy, 1)
                    if k:
                        out(it, k - 1)
                out(it, G7 - 1)
            steps(act, NT // G7, each)

        @block.tensor
        def _(pe):
            pe.wait_ge(id1, 1)
            pe.wait_ge(w_ld, 16 * 8)

            def project(it, k):
                i = it * G7 + k
                pe.wait_ge(xnT_rdy, i + 1)
                free(pe, ysc_rdy, i - 1 if k else it * G7)
                for c in range(2):
                    mm = pe.matmul(e.banks[2 + k % 2][:, c * D:(c + 1) * D], xnT[:, k % 2, c], wy[:, c],
                                   start=True, stop=True)
                mm.then_inc(y_done, 1)

            def each(it):
                for k in range(G7):
                    i = it * G7 + k
                    pe.wait_ge(xn_rdy, i + 1)
                    pe.wait_ge(hin_rdy, i + 1)
                    free(pe, xnT_rdy, i - 1 if k else it * G7)
                    free(pe, hT_rdy, i - 1 if k else it * G7)
                    for c in range(4):
                        src = (xn if c < 2 else hin)[:, k, (c % 2) * P:(c % 2 + 1) * P]
                        mm = pe.transpose(e.banks[c // 2 * 4 + k % 2][:, c % 2 * P:(c % 2 + 1) * P], src, ident[:])
                    mm.then_inc(t_done, 1)
                    if k:
                        project(it, k - 1)
                project(it, G7 - 1)
            steps(pe, NT // G7, each)


def phase_convolve(nc, e):
    io, ar, S = e.io, e.arena, e.sem
    ar.reset()
    wq = ar.take(2, CH)
    stage = ar.take(NCH, 512)
    full = N // 512
    tail, tail_w = N - full * 512, NP - full * 512
    bst = ar.take(NCH, full + 1, 6)
    bstf = bst.rearrange("p a b c -> p (a b c)")
    mv = ar.take(NCH, 2)
    gb = ar.take(2, NCH)
    t1 = ar.take(NCH)
    hT = e.B[:, :].rearrange("p (c n) -> p c n", c=2)
    w_ld, conv, out, bs, v, a = S("wq_ld"), S("conv_done"), S("conv_out"), S("conv_stats"), S("bn_vec"), S("bn_act")
    stored = [S(f"conv_stored{c}") for c in range(NCH)]

    with nc.Block() as block:
        @block.sync
        def _(sp):
            sp.dma_start(wq, io["w_qkv"][2].rearrange("(k p) c -> p k c", p=P)).then_inc(w_ld, 16)
            sp.dma_start(gb[:, 0], io["bn_g"]).then_inc(w_ld, 16)
            sp.dma_start(gb[:, 1], io["bn_b"]).then_inc(w_ld, 16)

            def store(n, w):
                for c in range(NCH):
                    sp.wait_ge(out, NCH * n + (c + 1))
                    sp.dma_start(e.conv_d[c][:, bass.ds(n * 512, w)], stage[:, c, 0:w]).then_inc(stored[c], 16)

            def each(n):
                store(n, 512)
            steps(sp, full, each)
            store(full, tail_w)
            for c in range(NCH):
                sp.wait_ge(stored[c], 16 * (full + 1))

        @block.tensor
        def _(pe):
            pe.wait_ge(w_ld, 48)

            def chunk(n, w):
                for c in range(NCH):
                    free(pe, out, NCH * n)
                    for k in range(2):
                        mm = pe.matmul(e.banks[c][:, 0:w], wq[:, k, c * P:(c + 1) * P],
                                       hT[:, k, bass.ds(n * 512, w)], start=(k == 0), stop=(k == 1))
                    mm.then_inc(conv, 1)

            def each(n):
                chunk(n, 512)
            steps(pe, full, each)
            chunk(full, tail_w)

        @block.scalar
        def _(act):
            def chunk(n, w):
                for c in range(NCH):
                    act.wait_ge(conv, NCH * n + (c + 1))
                    free(act, stored[c], 16 * n)
                    free(act, bs, NCH * n)
                    act.activation(stage[:, c, 0:w], e.banks[c][:, 0:w], ACT.Copy).then_inc(out, 1)

            def each(n):
                chunk(n, 512)
            steps(act, full, each)
            chunk(full, tail_w)
            act.wait_ge(v, 1)
            act.activation(t1, t1, ACT.Sqrt).then_inc(a, 1)

        @block.vector
        def _(dve):
            def chunk(n, w):
                for c in range(NCH):
                    dve.wait_ge(out, NCH * n + (c + 1))
                    dve.bn_stats(col(bstf, (n + c * (full + 1)) * 6, 6), stage[:, c, 0:w]).then_inc(bs, 1)

            def each(n):
                chunk(n, 512)
            steps(dve, full, each)
            chunk(full, tail)
            dve.wait_ge(bs, NCH * (full + 1))
            for c in range(NCH):
                dve.bn_aggr(mv[:, c], bst[:, c].rearrange("p a b -> p (a b)")).then_inc(bs, 1)
            dve.wait_ge(bs, NCH * (full + 2))
            n = [0]

            def link(ins):
                n[0] += 1
                ins.then_inc(v, 1)
                dve.wait_ge(v, n[0])

            link(dve.tensor_scalar(t1, mv[:, :, 1], EPS, None, ALU.add))
            dve.wait_ge(a, 1)
            dve.wait_ge(w_ld, 48)
            link(dve.reciprocal(t1, t1))
            link(dve.tensor_tensor(e.bn[:, 0], t1, gb[:, 0], ALU.mult))
            link(dve.tensor_tensor(t1, mv[:, :, 0], e.bn[:, 0], ALU.mult))
            link(dve.tensor_tensor(e.bn[:, 1], gb[:, 1], t1, ALU.subtract))


def phase_mix(nc, e):
    io, ar, S = e.io, e.arena, e.sem
    ar.reset()
    hb = [e.B[:, c * 3072:(c + 1) * 3072].rearrange("p (c n) -> p c n", c=NCH) for c in range(2)]
    wbd = ar.take(NCH, P)
    wres = ar.take(4, D)
    bres = ar.take(D)
    dw = ar.take(NCH)
    cat = ar.take(2, 2 * CH)
    kr = ar.take(GROUPS, DIM)
    qv = ar.take(GROUPS, DIM)
    den = ar.take(GROUPS, DIM)
    rat = ar.take(GROUPS, DIM)
    att = ar.take(2, GROUPS * DIM)
    attT = ar.take(4, P)
    junk = ar.take(2, CH)
    junk3 = ar.take(D)
    n2, r2, kap = ar.take(2, 2), ar.take(2, 2), ar.take(2, 1)
    ks = ar.take(GROUPS)
    o2, gam, o2a = ar.take(2, 1), ar.take(2, 1), ar.take(2, 1)
    junk2 = ar.take(512)
    nf2 = e.stat[:, 3]
    ident = e.ident
    b_h, b_s, b_t, b_r = e.banks[0:2], e.banks[2:4], e.banks[4], e.banks[5]
    STEPS, J = 6, 8
    w_zero, w_ld, w_rdy = S("mix_zero"), S("mix_w_ld"), S("mix_w_ready")
    c_in = [S(f"conv_in{c}") for c in range(2)]
    h_rdy, a_done, ea, nrm = S("h_ready"), S("mix_a_done"), S("cat_ready"), S("norm_ready")
    v, att_rdy, so, t_done, eo, res, ft, sf = (S(n) for n in (
        "mix_vec", "att_ready", "att_norm", "att_transposed", "attT_ready", "res_done", "ft_ready", "ft_square"))
    sq, sq2, v2 = S("mix_squares"), S("att_square"), S("mix_scale")

    with nc.Block() as block:
        @block.gpsimd
        def _(pool):
            pool.memset(wbd, 0.0).then_inc(w_zero, 1)

        @block.sync
        def _(sp):
            def load(n, w, b):
                sp.dma_start(hb[b][:, :, 0:w], e.conv_d[:, :, bass.ds(n * 512, w)].rearrange("c p n -> p c n")
                             ).then_inc(c_in[b], 16)

            load(0, 512, 0)
            load(1, 512, 1)
            sp.wait_ge(w_zero, 1)
            for b in range(4):
                sp.dma_start(wbd[32 * b:32 * b + 32, :, 32 * b:32 * b + 32], io["w_pw"][b]).then_inc(w_ld, 16)
            sp.dma_start(dw, io["w_dw"][2]).then_inc(w_ld, 16)
            sp.dma_start(wres, io["w_res"].rearrange("(k p) c -> p k c", p=P)).then_inc(w_ld, 16)
            sp.dma_start(bres, io["b_res"].broadcast_to([P, D])).then_inc(w_ld, 16)
            def each(s):
                for b in range(2):
                    sp.wait_ge(a_done, 8 * s + 4 * (b + 1))
                    load(2 * s + (2 + b), 512, b)
            steps(sp, STEPS - 1, each)
            sp.wait_ge(a_done, 8 * (STEPS - 1) + 4)
            load(2 * STEPS, NP - 1024 * STEPS, 0)

        @block.vector
        def _(dve):
            n = [0]
            dve.wait_ge(w_ld, 16 * 7)
            for c in range(NCH):
                dve.tensor_scalar(wbd[:, c], wbd[:, c], dw[:, c:c + 1], None, ALU.mult).then_inc(w_rdy, 1)

            LINKS = 8

            def attention(t, j):
                s = j % 2
                m = [0]

                def link(ins):
                    m[0] += 1
                    ins.then_inc(v, 1)
                    dve.wait_ge(v, LINKS * t + m[0])

                x = cat[:, s].rearrange("p (g c d) -> p g c d", g=GROUPS, c=3)
                dve.wait_ge(nrm, t + 1)
                link(dve.tensor_scalar(r2[:, s], r2[:, s], MIN_NORM, None, ALU.max))
                link(dve.reciprocal(r2[:, s], r2[:, s]))
                link(dve.tensor_scalar(r2[:, s], r2[:, s], ATANH_MAXN, 1.0, ALU.mult, ALU.min))
                link(dve.tensor_tensor(kap[:, s], r2[:, s, 0:1], r2[:, s, 1:2], ALU.min))
                dve.tensor_scalar(kr, x[:, :, 1], 0.0, None, ALU.max)
                link(dve.tensor_scalar(den, x[:, :, 2], kap[:, s], MIN_NORM, ALU.mult, ALU.add))
                dve.scalar_tensor_tensor(out=qv, in0=x[:, :, 0], scalar=0.0, in1=x[:, :, 2], op0=ALU.max, op1=ALU.mult)
                link(dve.reciprocal(den, den))
                dve.tensor_reduce(ks, kr, AX.X, ALU.add)
                link(dve.scalar_tensor_tensor(out=rat, in0=qv, scalar=kap[:, s], in1=den,
                                              op0=ALU.mult, op1=ALU.mult))
                link(dve.tensor_scalar(ks, ks, kap[:, s], kap[:, s], ALU.mult, ALU.mult))
                free(dve, t_done, t - 1)
                dve.tensor_tensor(att[:, s].rearrange("p (g d) -> p g d", g=GROUPS), rat,
                                  ks.rearrange("p (g o) -> p g o", o=1).broadcast_to([P, GROUPS, DIM]),
                                  ALU.mult).then_inc(att_rdy, 1)

            def finish(t, j):
                s = j % 2
                dve.wait_ge(so, t + 1)
                dve.tensor_scalar(o2[:, s], o2[:, s], MIN_NORM, None, ALU.max).then_inc(v2, 1)
                dve.wait_ge(v2, 3 * t + 1)
                dve.reciprocal(gam[:, s], o2[:, s]).then_inc(v2, 1)
                dve.wait_ge(v2, 3 * t + 2)
                dve.tensor_scalar(gam[:, s], gam[:, s], ATANH_MAXN, 1.0, ALU.mult, ALU.min).then_inc(v2, 1)
                dve.wait_ge(v2, 3 * t + 3)
                dve.wait_ge(res, t + 1)
                dve.scalar_tensor_tensor(out=col(e.C, t * D, D), in0=b_r[:, 0:D], scalar=gam[:, s], in1=bres,
                                         op0=ALU.mult, op1=ALU.add).then_inc(ft, 1)

            def step(s, first=False):
                for j in range(J):
                    attention(J * s + j, j)
                    if not (first and j == 0):
                        finish(J * s + (j - 1), (j - 1) % J)

            step(0, True)
            with dve.Fori(1, STEPS) as s:
                step(s)
            attention(NT - 1, 0)
            finish(NT - 2, 7)
            finish(NT - 1, 0)

        @block.scalar
        def _(act):
            def relu(b, w):
                for c in range(NCH):
                    last = act.activation(hb[b][:, c, 0:w], hb[b][:, c, 0:w], ACT.Relu, scale=e.bn[:, 0, c:c + 1],
                                          bias=e.bn[:, 1, c:c + 1])
                last.then_inc(h_rdy, 1)

            def cat_out(t, j):
                s = j % 2
                act.wait_ge(a_done, t + 1)
                free(act, att_rdy, t - 1)
                for b, (o, w) in zip((*b_h, *b_s), ((0, 512), (512, 256), (768, 512), (1280, 256))):
                    last = act.activation(cat[:, s, o:o + w], b[:, 0:w], ACT.Copy)
                last.then_inc(ea, 1)
                act.wait_ge(ea, t + 1)
                for h in range(2):
                    last = act.activation(junk[:, h], cat[:, s, h * CH:(h + 1) * CH], ACT.Square,
                                          accum_out=n2[:, s, h:h + 1])
                last.then_inc(sq, 1)
                act.wait_ge(sq, t + 1)
                act.activation(r2[:, s, 1:2], n2[:, s, 0:1], ACT.Sqrt, bias=n2[:, s, 1:2])
                act.activation(r2[:, s, 0:1], n2[:, s, 0:1], ACT.Sqrt).then_inc(nrm, 1)

            def att_norm(t, j):
                s = j % 2
                act.wait_ge(att_rdy, t + 1)
                act.activation(junk2, att[:, s], ACT.Square, accum_out=o2a[:, s]).then_inc(sq2, 1)
                act.wait_ge(sq2, t + 1)
                act.activation(o2[:, s], o2a[:, s], ACT.Sqrt).then_inc(so, 1)
                act.wait_ge(t_done, t + 1)
                free(act, res, t)
                act.activation(attT.rearrange("p a b -> p (a b)"), b_t[:, :], ACT.Copy).then_inc(eo, 1)

            def ft_square(t):
                act.wait_ge(ft, t + 1)
                free(act, sf, t)
                act.activation(junk3, col(e.C, t * D, D), ACT.Square, accum_out=col(nf2, t)).then_inc(sf, 1)

            def step(s, first=False, last=False):
                for j in range(J):
                    t = J * s + j
                    if j == 2:
                        act.wait_ge(c_in[1], 16 * s + 16)
                        relu(1, 512)
                    if j == 6:
                        act.wait_ge(c_in[0], 16 * s + 32)
                        relu(0, 128 if last else 512)
                    cat_out(t + 1, (j + 1) % J)
                    att_norm(t, j)
                    if not (first and j == 0):
                        ft_square(t - 1)

            act.wait_ge(c_in[0], 16)
            relu(0, 512)
            cat_out(0, 0)
            step(0, first=True)
            with act.Fori(1, STEPS - 1) as s:
                step(s)
            step(STEPS - 1, last=True)
            att_norm(NT - 1, 0)
            ft_square(NT - 2)
            ft_square(NT - 1)

        @block.tensor
        def _(pe):
            def part_b(t, j):
                s = j % 2
                pe.wait_ge(att_rdy, t + 1)
                free(pe, eo, t)
                for c in range(4):
                    mm = pe.transpose(b_t[:, c * P:(c + 1) * P], att[:, s, c * P:(c + 1) * P], ident[:])
                mm.then_inc(t_done, 1)
                pe.wait_ge(eo, t + 1)
                free(pe, ft, t)
                for c in range(4):
                    mm = pe.matmul(b_r[:, 0:D], attT[:, c], wres[:, c], start=(c == 0), stop=(c == 3))
                mm.then_inc(res, 1)

            def part_a(t, j):
                b, n = j // 4, j % 4
                free(pe, ea, t)
                for c in range(NCH):
                    pe.transpose(b_h[c // 4][:, c % 4 * P:(c % 4 + 1) * P], hb[b][:, c, n * P:(n + 1) * P], ident[:])
                for c in range(NCH):
                    mm = pe.matmul(b_s[c // 4][:, c % 4 * P:(c % 4 + 1) * P], hb[b][:, c, n * P:(n + 1) * P],
                                   wbd[:, c], start=True, stop=True)
                mm.then_inc(a_done, 1)

            def step(s):
                for j in range(J):
                    nj = (j + 1) % J
                    if nj % 4 == 0:
                        pe.wait_ge(h_rdy, 2 * s + (2 if nj else 3))
                    part_a(J * s + (j + 1), nj)
                    part_b(J * s + j, j)

            pe.wait_ge(w_rdy, NCH)
            pe.wait_ge(h_rdy, 1)
            part_a(0, 0)
            def each(s):
                step(s)
            steps(pe, STEPS, each)
            part_b(NT - 1, 0)



def phase_edges(nc, e):
    io, ar = e.io, e.arena
    ar.reset()
    dst_i = [ar.take(HALF) for _ in range(2)]
    src_i = [ar.take(HALF) for _ in range(2)]
    src_f = [ar.take(HALF) for _ in range(2)]
    src_off = [ar.take(HALF) for _ in range(2)]
    sh = [ar.take(HALF, 4) for _ in range(2)]
    a8 = ar.take(P)
    h1s = ar.take(4 * P)
    h2T = [ar.take(4 * P) for _ in range(2)]
    w1v = ar.take(HALF, P)
    w2bd = ar.take(P)
    w3z = ar.take(2, D)
    yb = e.B[:, 0:2 * HALF * D].rearrange("p (h t d) -> p h t d", h=2, t=HALF)
    xb = ar.take(2, 2, 512)
    eq = e.eq
    seq = ar.take(2, 2, 4, P)
    msg = ar.take(8, ROW)
    idx = ar.take(8)
    mx = ar.take(2, 2)
    tmp = ar.take(2)
    row1 = ar.take(P)
    p1, trash, pint = ar.take(1), ar.take(1), ar.take(1)
    idx_u = idx.bitcast(U32)
    ident = e.ident
    bank_h1, bank_h2 = e.banks[0], e.banks[1]
    bank_w = e.banks[2:4]
    bank_r = e.banks[4:6]
    bank_m = e.banks[6:8]

    S = e.sem
    c_zero, c_ld, c_iota, c_rdy = S("edge_zero"), S("edge_w_ld"), S("edge_iota"), S("edge_const")
    ld_dst = [S(f"ld_dst{h}") for h in range(2)]
    ld_src = [S(f"ld_src{h}") for h in range(2)]
    ld_sh = [S(f"ld_sh{h}") for h in range(2)]
    ld_a8 = S("ld_a8")
    srcf_rdy, srchi_rdy, srcoff_rdy = S("src_f_ready"), S("src_high_ready"), S("src_off_ready")
    h1_done, h2_done, silu1, silu2 = S("h1_done"), S("h2_done"), S("silu1"), S("silu2")
    w_done, rb_done, eq_done = S("w_done"), S("rows_done"), S("eq_done")
    mx_done, id_tmp, idx_rdy = S("last_edge"), S("idx_tmp"), S("idx_ready")
    sd_dve, sd_act = S("scaled_dve"), S("scaled_act")
    prod, comb, evac = S("products"), S("combined"), S("msg_ready")
    y_in = [[S(f"y_in{h}_{k}") for k in range(HALF)] for h in range(2)]
    scat = [S(f"scattered{r}") for r in range(TABLES)]

    msg0 = S("msg_zeroed")

    def slot_landed(eng, i, t):
        before, u = (i, t - 8) if t >= 8 else (i - 1, t + 8)
        free(eng, scat[TABLE[u]], 16 * scatters(before, u) + 16)

    with nc.Block() as block:
        @block.sync
        def _(sp):
            sp.wait_ge(c_zero, 1)
            for q in range(HALF):
                for t in range(2):
                    r = 16 * q + 8 * t
                    sp.dma_start(w1v[r:r + 8, q, 64 * t:64 * t + 64], io["fc1"]).then_inc(c_ld, 16)
            for t in range(2):
                sp.dma_start(w2bd[64 * t:64 * t + 64, 64 * t:64 * t + 64], io["fc2"]).then_inc(c_ld, 16)
                sp.dma_start(w3z[64 * t:64 * t + 64, t], io["fc3"]).then_inc(c_ld, 16)

            def load(buf, name, half, sem):
                src = io[name][bass.ds(half, 1)]
                dims = " ".join("xyz"[:len(src.shape) - 2])
                sp.dma_start(buf, src.rearrange(f"a p {dims} -> (a p) {dims}")).then_inc(sem, 16)

            sp.dma_start(a8, io["a8"][0]).then_inc(ld_a8, 16)
            for h in range(2):
                load(dst_i[h].bitcast(I32), "dst", h, ld_dst[h])
                load(src_i[h].bitcast(I32), "src", h, ld_src[h])
                load(sh[h], "sh", h, ld_sh[h])

            def each(i):
                for h in range(2):
                    for k in range(HALF):
                        sp.wait_ge(y_in[h][k], 16 * i + 16)
                    load(dst_i[h].bitcast(I32), "dst", 2 * i + (2 + h), ld_dst[h])
                    sp.wait_ge(srcf_rdy, 2 * i + (1 + h))
                    load(src_i[h].bitcast(I32), "src", 2 * i + (2 + h), ld_src[h])
                    if h == 0:
                        sp.wait_ge(h1_done, 2 * i + 2)
                        sp.dma_start(a8, io["a8"][bass.ds(i + 1, 1)].rearrange("a r e -> (a r) e")).then_inc(ld_a8, 16)
                    sp.wait_ge(comb, 16 * i + 8 * (h + 1))
                    load(sh[h], "sh", 2 * i + (2 + h), ld_sh[h])

            steps(sp, NI - 1, each)

        @block.gpsimd
        def _(pool):
            for buf in (w1v, w2bd, w3z):
                last = pool.memset(buf, 0.0)
            last.then_inc(c_zero, 1)
            pool.memset(msg, 0.0).then_inc(msg0, 1)
            pool.iota(row1.bitcast(I32), pattern=[[1, P]], base=1, channel_multiplier=0)
            pool.iota(pint.bitcast(I32), pattern=[[0, 1]], base=0, channel_multiplier=1).then_inc(c_iota, 1)

            def gather(h, k, i, g):
                if k == 0:
                    pool.wait_ge(ld_dst[h], 16 * i + 16)
                if g is not None:
                    free(pool, prod, g - 3)
                    pool.nop(nofuse=True)
                pool.indirect_dma_start(yb[:, h, k], None, e.y_d, bass.IndirectOffsetOnAxis(
                    ap=dst_i[h].bitcast(U32)[:, k:k + 1], axis=0)).then_inc(y_in[h][k], 16)

            def scatter(i, j, k):
                t, slot = 2 * j + k, 2 * (j % 4) + k
                r = TABLE[t]
                if k == 0:
                    pool.wait_ge(idx_rdy, 8 * i + (j + 1))
                pool.wait_ge(evac, 16 * i + (t + 1))
                free(pool, scat[r], 16 * scatters(i, t))
                pool.nop(nofuse=True)
                pool.indirect_dma_start(e.agg_d[r], bass.IndirectOffsetOnAxis(ap=idx_u[:, slot:slot + 1], axis=0),
                                        msg[:, slot], None, compute_op=ALU.add).then_inc(scat[r], 16)

            def step(i, last):
                for j in range(HALF):
                    for k in range(2):
                        kk = 2 * (j % 4) + k
                        if j < 4:
                            gather(1, kk, i, 8 * i + j)
                        elif not last:
                            gather(0, kk, i + 1, 8 * i + j)
                        scatter(i, j, k)

            for k in range(HALF):
                gather(0, k, 0, None)
            def each(i):
                step(i, False)
            steps(pool, NI - 1, each)
            step(NI - 1, True)
            for r in range(TABLES):
                pool.wait_ge(scat[r], 16 * TABLE.count(r) * NI)

        @block.vector
        def _(dve):
            dve.wait_ge(c_iota, 1)
            dve.tensor_copy(e.row1, row1.bitcast(I32)).then_inc(c_rdy, 1)
            dve.tensor_scalar(p1, pint.bitcast(I32), 1.0, None, ALU.add).then_inc(c_rdy, 1)
            dve.tensor_scalar(trash, pint.bitcast(I32), float(TRASH), None, ALU.add).then_inc(c_rdy, 1)
            dve.tensor_copy(e.ident_b[:], ident[:]).then_inc(c_rdy, 1)
            dve.wait_ge(c_rdy, 4)
            dve.wait_ge(msg0, 1)

            def sources(h, i, H):
                dve.wait_ge(ld_src[h], 16 * i + 16)
                dve.tensor_copy(src_f[h], src_i[h].bitcast(I32)).then_inc(srcf_rdy, 1)
                dve.wait_ge(srcf_rdy, H + 1)
                dve.tensor_copy(e.src_hl[:, h, 0], src_f[h]).then_inc(srchi_rdy, 1)
                dve.wait_ge(srchi_rdy, H + 1)
                dve.tensor_tensor(e.src_hl[:, h, 1], src_f[h], e.src_hl[:, h, 0], ALU.subtract)
                dve.tensor_scalar(src_off[h], src_f[h], trash, None, ALU.subtract).then_inc(srcoff_rdy, 1)

            def products(g, h, j, i):
                s, q = j % 2, j % 4
                dve.wait_ge(w_done, g + 1)
                for k in range(2):
                    dve.wait_ge(y_in[h][2 * q + k], 16 * i + 16)
                free(dve, comb, 2 * g - 2)
                w = bank_w[s][:, :].rearrange("p (t f u) -> p t f u", t=2, f=4)
                y = yb[:, h, 2 * q:2 * q + 2]
                x = xb[:, s].rearrange("p t (h s u) -> p t h s u", h=2, s=4)
                dve.tensor_tensor(x[:, :, :, 0], w[:, :, 0:2],
                                  y[:, :, 0:64].rearrange("p t (o u) -> p t o u", o=1).broadcast_to([P, 2, 2, 64]),
                                  ALU.mult)
                for k in range(2):
                    last = dve.tensor_tensor(
                        x[:, k, :, 1:4],
                        w[:, k, 2:4].rearrange("p (f o) u -> p f o u", o=1).broadcast_to([P, 2, 3, 64]),
                        y[:, k, 64:256].rearrange("p (o c u) -> p o c u", o=1, c=3).broadcast_to([P, 2, 3, 64]),
                        ALU.mult)
                last.then_inc(prod, 1)

            def equality(i, h, j, H):
                s, q, g = j % 2, j % 4, 8 * i + j
                dve.wait_ge(srcoff_rdy, H + 1)
                dve.wait_ge(rb_done, g + 1)
                free(dve, comb, 2 * g - 2)
                for k in range(2):
                    t = 2 * q + k
                    slot_landed(dve, i, 2 * j + k)
                    last = dve.tensor_scalar(eq[:, s, k], bank_r[s][:, k * P:(k + 1) * P], src_f[h][:, t:t + 1], None,
                                             ALU.is_equal, ALU.add, accum_out=msg[:, t, 512:513])
                last.then_inc(eq_done, 1)
                dve.wait_ge(eq_done, g + 1)
                for k in range(2):
                    for c in range(2):
                        last = dve.tensor_scalar(seq[:, s, k, c], eq[:, s, k], sh[h][:, 2 * q + k, c:c + 1], None,
                                                 ALU.mult)
                last.then_inc(sd_dve, 1)
                for k in range(2):
                    last = dve.tensor_tensor_reduce(e.junk[:, k], eq[:, s, k], e.row1, 1.0, 0.0, ALU.mult, ALU.max,
                                                    mx[:, s, k:k + 1])
                last.then_inc(mx_done, 1)
                dve.wait_ge(mx_done, g + 1)
                dve.scalar_tensor_tensor(out=tmp, in0=mx[:, s], scalar=p1, in1=src_off[h][:, 2 * q:2 * q + 2],
                                         op0=ALU.is_equal, op1=ALU.mult).then_inc(id_tmp, 1)
                dve.wait_ge(id_tmp, g + 1)
                dve.tensor_scalar(idx_u[:, 2 * q:2 * q + 2], tmp, trash, None, ALU.add).then_inc(idx_rdy, 1)

            def step(i, last):
                for j in range(HALF):
                    if j == 1:
                        sources(1, i, 2 * i + 1)
                    if j == 5 and not last:
                        sources(0, i + 1, 2 * i + 2)
                    if j < 7 or not last:
                        nj = (j + 1) % HALF
                        nh, ni = nj // 4, i if j < 7 else i + 1
                        dve.wait_ge(ld_sh[nh], 16 * ni + 16)
                        equality(ni, nh, nj, 2 * i + (j + 1) // 4)
                        products(8 * i + (j + 1), nh, nj, ni)

            sources(0, 0, 0)
            dve.wait_ge(ld_sh[0], 16)
            equality(0, 0, 0, 0)
            products(0, 0, 0, 0)
            def each(i):
                step(i, False)
            steps(dve, NI - 1, each)
            step(NI - 1, True)

        @block.scalar
        def _(act):
            def first(H):
                act.wait_ge(h1_done, H + 1)
                free(act, h2_done, H)
                act.activation(h1s, bank_h1[:, :], ACT.Silu, scale=float(8 ** -0.5)).then_inc(silu1, 1)

            def second(h, H, used):
                act.wait_ge(h2_done, H + 1)
                free(act, w_done, used)
                act.activation(h2T[h], bank_h2[:, :], ACT.Silu, scale=0.125).then_inc(silu2, 1)

            def scaled(g, h, j):
                s, q = j % 2, j % 4
                act.wait_ge(eq_done, g + 1)
                free(act, comb, 2 * g - 2)
                for k in range(2):
                    for c in range(2, 4):
                        last = act.activation(seq[:, s, k, c], eq[:, s, k], ACT.Copy,
                                              scale=sh[h][:, 2 * q + k, c:c + 1])
                last.then_inc(sd_act, 1)

            def evacuate(i, j):
                for k in range(2):
                    act.wait_ge(comb, 16 * i + (2 * j + k + 1))
                    slot_landed(act, i, 2 * j + k)
                    act.activation(msg[:, 2 * (j % 4) + k, 0:512], bank_m[k][:, :], ACT.Copy).then_inc(evac, 1)

            def step(i, last):
                for j in range(HALF):
                    if j == 1:
                        first(2 * i + 1)
                    if j == 2:
                        second(1, 2 * i + 1, 8 * i)
                    if j == 5 and not last:
                        first(2 * i + 2)
                    if j == 6 and not last:
                        second(0, 2 * i + 2, 8 * i + 4)
                    if j < 7 or not last:
                        nj = (j + 1) % HALF
                        scaled(8 * i + (j + 1), nj // 4, nj)
                    evacuate(i, j)

            act.wait_ge(c_rdy, 4)
            act.wait_ge(msg0, 1)
            first(0)
            act.wait_ge(h2_done, 1)
            act.activation(h2T[0], bank_h2[:, :], ACT.Silu, scale=0.125).then_inc(silu2, 1)
            act.wait_ge(ld_sh[0], 16)
            scaled(0, 0, 0)
            def each(i):
                step(i, False)
            steps(act, NI - 1, each)
            step(NI - 1, True)

        @block.tensor
        def _(pe):
            def mlp1(h, i, H):
                pe.wait_ge(ld_a8, 16 * i + 16)
                free(pe, silu1, H)
                for q in range(4):
                    mm = pe.matmul(bank_h1[:, q * P:(q + 1) * P], w1v[:, 4 * h + q], a8, start=True, stop=True)
                mm.then_inc(h1_done, 1)

            def mlp2(H):
                pe.wait_ge(silu1, H + 1)
                free(pe, silu2, H)
                pe.matmul(bank_h2[:, :], w2bd, h1s, start=True, stop=True).then_inc(h2_done, 1)

            def stage(g, h, j, H):
                s, q = j % 2, j % 4
                if q == 0:
                    pe.wait_ge(silu2, H + 1)
                    pe.wait_ge(srcoff_rdy, H + 1)
                free(pe, eq_done, g - 1)
                for k in range(2):
                    t = 2 * q + k
                    for part in range(2):
                        mm = pe.matmul(bank_r[s][:, k * P:(k + 1) * P],
                                       e.src_hl[:, h, part, t:t + 1].broadcast_to([P, P]), e.ident_b[:],
                                       start=(part == 0), stop=(part == 1))
                mm.then_inc(rb_done, 1)
                free(pe, prod, g - 1)
                for k in range(2):
                    mm = pe.matmul(bank_w[s][:, k * D:(k + 1) * D], h2T[h][:, q * P:(q + 1) * P], w3z[:, k],
                                   start=True, stop=True)
                mm.then_inc(w_done, 1)

            def combine(g, j):
                s = j % 2
                pe.wait_ge(eq_done, g + 1)
                pe.wait_ge(prod, g + 1)
                pe.wait_ge(sd_dve, g + 1)
                pe.wait_ge(sd_act, g + 1)
                for k in range(2):
                    free(pe, evac, 2 * g + (k - 1))
                    x = xb[:, s, k]
                    m = bank_m[k]
                    pe.matmul(m[:, 0:256], seq[:, s, k, 0], x[:, 0:256], start=True, stop=False,
                              skip_group_check=True)
                    z = x[:, 256:512].rearrange("p (s u) -> p s u", s=4)
                    o = m[:, 256:512].rearrange("p (s u) -> p s u", s=4)
                    for c in range(3):
                        mm = pe.matmul(o[:, c::3 - c], seq[:, s, k, c + 1], z[:, 0::c + 1][:, 0:2],
                                       start=False, stop=(c == 2), skip_group_check=True)
                    mm.then_inc(comb, 1)

            def step(i, last):
                for j in range(HALF):
                    if j == 1:
                        mlp1(1, i, 2 * i + 1)
                    if j == 2:
                        mlp2(2 * i + 1)
                    if j == 5 and not last:
                        mlp1(0, i + 1, 2 * i + 2)
                    if j == 6 and not last:
                        mlp2(2 * i + 2)
                    if j < 7 or not last:
                        nj = (j + 1) % HALF
                        stage(8 * i + (j + 1), nj // 4, nj, 2 * i + (j + 1) // 4)
                    combine(8 * i + j, j)

            pe.wait_ge(c_ld, 16 * 20)
            pe.wait_ge(c_rdy, 4)
            mlp1(0, 0, 0)
            mlp2(0)
            stage(0, 0, 0, 0)
            def each(i):
                step(i, False)
            steps(pe, NI - 1, each)
            step(NI - 1, True)



def phase_combine(nc, e):
    io, ar, S = e.io, e.arena, e.sem
    ar.reset()
    w2 = ar.take(4, P)
    agg = ar.take(G7, TABLES, ROW)
    aggT = ar.take(2, 512)
    dg, rt, dn = ar.take(G7), ar.take(G7), ar.take(G7)
    junk = ar.take(D)
    ss, sv = e.stat[:, 4], e.stat[:, 5]
    ident = e.ident
    w_zero, w_ld, w_rdy, sc_ld, part = S("w2_zero"), S("w2_ld"), S("w2_ready"), S("sc_ld"), S("agg_part")
    ld = [S(f"agg_in{k}") for k in range(G7)]
    summed, rooted, inv, t_done, aT, prod, g_rdy, sq = (S(n) for n in (
        "agg_sum", "deg_root", "deg_inverse", "agg_transposed", "aggT_ready", "w2_done", "g_ready", "g_squares"))
    b_t, b_r = e.banks[0:2], e.banks[2:4]

    with nc.Block() as block:
        @block.gpsimd
        def _(pool):
            pool.memset(w2, 0.0).then_inc(w_zero, 1)

            def each(it):
                for k in range(G7):
                    pool.wait_ge(ld[k], 16 * TABLES * (it + 1))
                    pool.tensor_tensor(agg[:, k, 0, 0:513], agg[:, k, 0, 0:513], agg[:, k, 1, 0:513], ALU.add
                                       ).then_inc(part, 1)
            steps(pool, NT // G7, each)

        @block.sync
        def _(sp):
            sp.wait_ge(w_zero, 1)
            for c, r, k, name, top in ((0, 0, 0, "w2_s", 0), (0, 1, 1, "w2_v", 1), (1, 0, 0, "w2_v", 1),
                                       (1, 1, 1, "w2_v", 1), (2, 0, 0, "w2_v", 0), (2, 1, 1, "w2_v", 0),
                                       (3, 0, 1, "w2_v", 0), (3, 1, 0, "w2_s", 1)):
                sp.dma_start(w2[64 * r:64 * r + 64, c, 64 * k:64 * k + 64], io[name][64 * top:64 * top + 64, :]
                             ).then_inc(w_ld, 16)
            sp.dma_start(e.B[:, :].rearrange("p (t d) -> p t d", d=D), e.sc_d.rearrange("(t p) d -> p t d", p=P)
                         ).then_inc(sc_ld, 16)

            def each(it):
                for k in range(G7):
                    free(sp, t_done, G7 * it + (k + 1 - G7))
                    free(sp, rooted, G7 * it + (k + 1 - G7))
                    for r in range(TABLES):
                        sp.dma_start(agg[:, k, r], e.agg_d[r][bass.ds(it * (G7 * P) + k * P, P), :]).then_inc(ld[k], 16)
            steps(sp, NT // G7, each)

        @block.vector
        def _(dve):
            dve.wait_ge(w_ld, 16 * 8)
            dve.wait_ge(sc_ld, 16)
            scale = float(128 ** -0.5 / 8)
            dve.tensor_scalar(w2, w2, scale, None, ALU.mult).then_inc(w_rdy, 1)
            dve.wait_ge(w_rdy, 1)
            dve.tensor_scalar(w2[64:128, 3], w2[64:128, 3], INV_SQRT3, None, ALU.mult).then_inc(w_rdy, 1)

            def total(it, k):
                i = it * G7 + k
                dve.wait_ge(part, i + 1)
                dve.tensor_tensor(agg[:, k, 0, 0:513], agg[:, k, 0, 0:513], agg[:, k, 2, 0:513], ALU.add
                                  ).then_inc(summed, 1)
                dve.wait_ge(summed, 2 * i + 1)
                dve.tensor_scalar(dg[:, k:k + 1], agg[:, k, 0, 512:513], 1.0, None, ALU.max).then_inc(summed, 1)

            def node(it, k):
                i = it * G7 + k
                dve.wait_ge(rooted, i + 1)
                dve.reciprocal(dn[:, k:k + 1], rt[:, k:k + 1]).then_inc(inv, 1)
                dve.wait_ge(inv, i + 1)
                dve.wait_ge(prod, i + 1)
                dve.scalar_tensor_tensor(out=col(e.B, i * D, D), in0=b_r[k % 2][:, 0:D], scalar=dn[:, k:k + 1],
                                         in1=col(e.B, i * D, D), op0=ALU.mult, op1=ALU.add).then_inc(g_rdy, 1)

            def each(it):
                for k in range(G7):
                    total(it, k)
                    if k:
                        node(it, k - 1)
                node(it, G7 - 1)
            steps(dve, NT // G7, each)

        @block.scalar
        def _(act):
            def squares(act, i):
                act.wait_ge(g_rdy, i + 1)
                free(act, sq, i)
                act.activation(junk[:, 0:64], col(e.B, i * D, 64), ACT.Square, accum_out=col(ss, i))
                act.activation(junk[:, 64:D], col(e.B, i * D + 64, 192), ACT.Square, accum_out=col(sv, i)
                               ).then_inc(sq, 1)

            def each(it):
                for k in range(G7):
                    i = it * G7 + k
                    act.wait_ge(summed, 2 * i + 2)
                    act.activation(rt[:, k:k + 1], dg[:, k:k + 1], ACT.Sqrt).then_inc(rooted, 1)
                    act.wait_ge(t_done, i + 1)
                    free(act, prod, i - 1 if k else it * G7)
                    act.activation(aggT[:, k % 2], b_t[k % 2][:, :], ACT.Copy).then_inc(aT, 1)
                    if k:
                        squares(act, i - 1)
                squares(act, it * G7 + (G7 - 1))
            steps(act, NT // G7, each)

        @block.tensor
        def _(pe):
            pe.wait_ge(w_rdy, 2)

            def project(it, k):
                i = it * G7 + k
                pe.wait_ge(aT, i + 1)
                free(pe, g_rdy, i - 1 if k else it * G7)
                b, a = b_r[k % 2], aggT[:, k % 2]
                o = b[:, 0:D]
                ends = b[:, 0:D].rearrange("p (s u) -> p s u", s=4)[:, 0::3]
                for c, out in enumerate((o[:, 0:128], o[:, 128:256], o[:, 64:192], ends)):
                    mm = pe.matmul(out, a[:, c * P:(c + 1) * P], w2[:, c], start=(c == 0), stop=(c == 3),
                                   skip_group_check=True)
                mm.then_inc(prod, 1)

            def each(it):
                for k in range(G7):
                    i = it * G7 + k
                    pe.wait_ge(summed, 2 * i + 1)
                    free(pe, aT, i - 1 if k else it * G7)
                    for c in range(4):
                        mm = pe.transpose(b_t[k % 2][:, c * P:(c + 1) * P], agg[:, k, 0, c * P:(c + 1) * P], ident[:])
                    mm.then_inc(t_done, 1)
                    if k:
                        project(it, k - 1)
                project(it, G7 - 1)
            steps(pe, NT // G7, each)


def phase_residual(nc, e):
    io, ar, S, st = e.io, e.arena, e.sem, e.stat
    ar.reset()
    gmul = ar.take(D)
    xs = ar.take(G7, D)
    bst, mean, var = ar.take(NT, 6), ar.take(NT), ar.take(NT)
    wr = ar.take(2, NE)
    br = ar.take(NE)
    row = ar.take(NE)
    eight = [ar.take(NE) for _ in range(6)]
    one = [ar.take(1) for _ in range(8)]
    pair = ar.take(2)
    sums = ar.take(2)
    ones = ar.take(P)
    nf2, ss, sv, rstd = st[:, 3], st[:, 4], st[:, 5], st[:, 0]
    dl, th, sv_r = st[:, 6], st[:, 7], st[:, 8]
    ident = e.ident
    w_ld, v, a = S("res_w_ld"), S("res_vec"), S("res_act")
    gn, x1, bs, x2, tt, cT = S("g_normed"), S("x1_ready"), S("x1_stats"), S("x2_ready"), S("x2_transposed"), S("x2T_ready")
    p, c_rdy, kept = S("route_pe"), S("route_const"), S("x2_kept")

    with nc.Block() as block:
        @block.sync
        def _(sp):
            sp.dma_start(gmul[:, 0:64], io["g_s"].broadcast_to([P, 64])).then_inc(w_ld, 16)
            for d in range(3):
                sp.dma_start(gmul[:, 64 * (d + 1):64 * (d + 2)], io["g_v"].broadcast_to([P, 64])).then_inc(w_ld, 16)
            sp.dma_start(wr, io["wr"].rearrange("(k p) n -> p k n", p=P)).then_inc(w_ld, 16)
            sp.dma_start(br[0:1], io["br"]).then_inc(w_ld, 16)

        @block.gpsimd
        def _(pool):
            pool.memset(ones, 1.0)
            pool.iota(row[0:1].bitcast(I32), pattern=[[1, NE]], base=0, channel_multiplier=0).then_inc(c_rdy, 1)
            with pool.Fori(0, NT) as i:
                pool.wait_ge(gn, 2 * i + 2)
                pool.tensor_tensor(col(e.A, i * D, D), col(e.A, i * D, D), col(e.B, i * D, D), ALU.add
                                   ).then_inc(x1, 1)
            def each(it):
                for k in range(G7):
                    i = it * G7 + k
                    pool.wait_ge(x2, i + 1)
                    pool.tensor_copy(col(e.B, i * D, D), xs[:, k]).then_inc(kept, 1)
            steps(pool, NT // G7, each)

        @block.vector
        def _(dve):
            link = linker(dve, v)
            link(dve.tensor_scalar(ss, ss, 1.0 / MUL, EPS, ALU.mult, ALU.add))
            link(dve.tensor_scalar(sv, sv, 1.0 / (3 * MUL), EPS, ALU.mult, ALU.add))
            dve.wait_ge(a, 3)
            link(dve.reciprocal(ss, ss))
            link(dve.reciprocal(sv_r, sv))
            link(dve.tensor_scalar(nf2, nf2, MIN_NORM, None, ALU.max))
            link(dve.reciprocal(dl, nf2))
            dve.wait_ge(a, 4)
            link(dve.tensor_scalar(th, th, MAXN, None, ALU.min))
            link(dve.tensor_tensor(dl, dl, th, ALU.mult))
            dve.wait_ge(w_ld, 16 * 6)
            with dve.Fori(0, NT) as i:
                dve.scalar_tensor_tensor(out=col(e.A, i * D, D), in0=col(e.C, i * D, D), scalar=col(dl, i),
                                         in1=col(e.A, i * D, D), op0=ALU.mult, op1=ALU.add).then_inc(gn, 1)
                dve.scalar_tensor_tensor(out=col(e.B, i * D, 64), in0=col(e.B, i * D, 64), scalar=col(ss, i),
                                         in1=gmul[:, 0:64], op0=ALU.mult, op1=ALU.mult)
                dve.scalar_tensor_tensor(out=col(e.B, i * D + 64, 192), in0=col(e.B, i * D + 64, 192),
                                         scalar=col(sv_r, i), in1=gmul[:, 64:D], op0=ALU.mult, op1=ALU.mult
                                         ).then_inc(gn, 1)
            bf = bst.rearrange("p a b -> p (a b)")
            with dve.Fori(0, NT) as i:
                dve.wait_ge(x1, i + 1)
                dve.bn_stats(col(bf, 6 * i, 6), col(e.A, i * D, D)).then_inc(bs, 1)
            dve.wait_ge(bs, NT)
            row_moments(link, dve, bst, mean, var, th)
            link(dve.tensor_scalar(rstd, var, EPS, None, ALU.add))
            dve.wait_ge(a, 5)
            link(dve.reciprocal(rstd, rstd))
            def each(it):
                for k in range(G7):
                    i = it * G7 + k
                    free(dve, tt, it * G7)
                    free(dve, kept, it * G7)
                    dve.tensor_scalar(xs[:, k], col(e.A, i * D, D), col(mean, i), col(rstd, i),
                                      ALU.subtract, ALU.mult).then_inc(x2, 1)
            steps(dve, NT // G7, each)
            dve.wait_ge(cT, NT)
            xc = e.C[:, :].rearrange("p (c n) -> p c n", c=2)
            link(dve.tensor_reduce(sums, xc[:, :, 0:N], AX.X, ALU.add))
            link(dve.tensor_scalar(sums, sums, 1.0 / N, None, ALU.mult))
            lg, ex, t1, t2, rw, ii = (z[0:1] for z in eight)
            mx, sm, i1, i2, v1, v2, e2, w1 = (z[0:1] for z in one)
            dve.wait_ge(c_rdy, 1)
            link(dve.tensor_copy(ii, row[0:1].bitcast(I32)))
            dve.wait_ge(p, 1)
            link(dve.tensor_tensor(lg, e.banks[4][0:1, 0:NE], br[0:1], ALU.add))
            link(dve.tensor_reduce(mx, lg, AX.X, ALU.max))
            link(dve.tensor_scalar(lg, lg, mx, None, ALU.subtract))
            dve.wait_ge(a, 6)
            link(dve.reciprocal(sm, sm))
            link(dve.tensor_scalar(rw, ex, sm, None, ALU.mult))
            link(dve.tensor_scalar(t1, rw, float(N), None, ALU.mult))
            link(dve.tensor_scalar(t2, t1, CAPACITY, None, ALU.is_gt))
            link(dve.tensor_scalar(t1, t1, CAPACITY, None, ALU.max))
            link(dve.reciprocal(t1, t1))
            link(dve.tensor_scalar(t1, t1, CAPACITY, -1.0, ALU.mult, ALU.add))
            link(dve.tensor_tensor(t1, t1, t2, ALU.mult))
            link(dve.tensor_scalar(t1, t1, 1.0, None, ALU.add))
            link(dve.tensor_tensor(rw, rw, t1, ALU.mult))
            link(dve.tensor_reduce(mx, rw, AX.X, ALU.max))
            link(dve.tensor_scalar(rw, rw, mx, None, ALU.subtract))
            dve.wait_ge(a, 7)
            link(dve.reciprocal(sm, sm))
            link(dve.tensor_scalar(rw, ex, sm, None, ALU.mult))
            for n, (val, at) in enumerate(((v1, i1), (v2, i2))):
                link(dve.tensor_reduce(val, rw, AX.X, ALU.max))
                link(dve.tensor_scalar(t1, rw, val, -1000.0, ALU.is_equal, ALU.mult))
                link(dve.tensor_tensor(t1, t1, ii, ALU.add))
                link(dve.tensor_reduce(at, t1, AX.X, ALU.min))
                link(dve.tensor_scalar(at, at, 1000.0, None, ALU.add))
                if n == 0:
                    link(dve.tensor_scalar(t1, ii, at, -4.0, ALU.is_equal, ALU.mult))
                    link(dve.tensor_tensor(rw, rw, t1, ALU.add))
            link(dve.tensor_copy(e.pick[0:1, 0:1], i1))
            link(dve.tensor_copy(e.pick[0:1, 1:2], i2))
            link(dve.tensor_tensor(e2, v2, v1, ALU.subtract))
            dve.wait_ge(a, 8)
            link(dve.tensor_scalar(w1, e2, 1.0, None, ALU.add))
            link(dve.reciprocal(pair[0:1, 0:1], w1))
            link(dve.tensor_tensor(pair[0:1, 1:2], e2, pair[0:1, 0:1], ALU.mult))
            dve.wait_ge(p, 2)
            link(dve.tensor_copy(e.weight[:], e.banks[5][:, 0:2]))

        @block.scalar
        def _(act):
            ex, sm, lg, rw, e2 = eight[1][0:1], one[1][0:1], eight[0][0:1], eight[4][0:1], one[6][0:1]
            act.wait_ge(v, 2)
            act.activation(ss, ss, ACT.Sqrt).then_inc(a, 1)
            act.activation(sv, sv, ACT.Sqrt).then_inc(a, 1)
            act.activation(nf2, nf2, ACT.Sqrt).then_inc(a, 1)
            act.wait_ge(v, 5)
            act.activation(th, nf2, ACT.Tanh).then_inc(a, 1)
            act.wait_ge(v, MOMENTS + 9)
            act.activation(rstd, rstd, ACT.Sqrt).then_inc(a, 1)
            act.wait_ge(gn, 2 * NT)
            xc = e.C[:, :].rearrange("p (c n) -> p c n", c=2)

            def out(i, s):
                act.wait_ge(tt, i + 1)
                act.activation(xc[:, :, bass.ds(i * P, P)],
                               e.banks[s][:, 0:D].rearrange("p (c n) -> p c n", c=2), ACT.Copy).then_inc(cT, 1)

            def each(it):
                for k in range(G7):
                    out(it * G7 + k, k % 4)
            steps(act, NT // G7, each)
            act.wait_ge(v, MOMENTS + 16)
            act.activation(ex, lg, ACT.Exp, accum_out=sm).then_inc(a, 1)
            act.wait_ge(v, MOMENTS + 28)
            act.activation(ex, rw, ACT.Exp, accum_out=sm).then_inc(a, 1)
            act.wait_ge(v, MOMENTS + 45)
            act.activation(e2, e2, ACT.Exp).then_inc(a, 1)

        @block.tensor
        def _(pe):
            def tile(i, k):
                pe.wait_ge(x2, i + 1)
                free(pe, cT, i - 3 if k > 3 else i - k)
                for c in range(2):
                    mm = pe.transpose(e.banks[k % 4][:, c * P:(c + 1) * P], xs[:, k, c * P:(c + 1) * P], ident[:])
                mm.then_inc(tt, 1)

            def each(it):
                for k in range(G7):
                    tile(it * G7 + k, k)
            steps(pe, NT // G7, each)
            pe.wait_ge(v, MOMENTS + 12)
            pe.wait_ge(w_ld, 16 * 6)
            for c in range(2):
                mm = pe.matmul(e.banks[4][0:1, 0:NE], sums[:, c:c + 1], wr[:, c], start=(c == 0), stop=(c == 1))
            mm.then_inc(p, 1)
            pe.wait_ge(v, MOMENTS + 48)
            pe.matmul(e.banks[5][:, 0:2], ones[0:1], pair[0:1], start=True, stop=True).then_inc(p, 1)


def phase_experts(nc, e):
    io, ar, S = e.io, e.arena, e.sem
    ar.reset()
    w1 = ar.take(2, 2, FF)
    w2 = ar.take(2, 4, D)
    hT = [ar.take(2, 4, 512) for _ in range(2)]
    b1 = ar.take(2, 4)
    b2 = ar.take(2, D)
    b2c = ar.take(D)
    lng, lnb = ar.take(D), ar.take(D)
    bst, mean, var = ar.take(NT, 6), ar.take(NT), ar.take(NT)
    rstd, nmr = e.stat[:, 0], e.stat[:, 1]
    z1 = w1.rearrange("p a b c -> p (a b c)")[:, 0:G7 * D].rearrange("p (k d) -> p k d", d=D)
    xc = e.C[:, :].rearrange("p (c n) -> p c n", c=2)
    bank_h, bank_o = e.banks[0:4], e.banks[4:8]
    STEPS, TAIL = NT // 8, 1
    w_ld, w_rdy, v, a = S("ffn_w_ld"), S("ffn_w_ready"), S("ffn_vec"), S("ffn_act")
    h_done, h_rdy, o_done, z_rdy, bs = S("ffn_h"), S("ffn_gelu"), S("ffn_out"), S("z_ready"), S("z_stats")
    xb, n_rdy, g_rdy, o_rdy = S("x1_beta"), S("z_normed"), S("z_gamma"), S("out_ready")
    st = [S(f"out_stored{k}") for k in range(G7)]

    with nc.Block() as block:
        @block.sync
        def _(sp):
            for n in range(2):
                ex = sp.value_load(e.pick[0:1, n:n + 1], min_val=0, max_val=NE - 1)
                sp.dma_start(w1[:, n], io["ffn1"][bass.ds(ex, 1)].rearrange("o (k p) f -> p (o k) f", p=P)
                             ).then_inc(w_ld, 16)
                sp.dma_start(w2[:, n], io["ffn2"][bass.ds(ex, 1)].rearrange("o (f p) d -> p (o f) d", p=P)
                             ).then_inc(w_ld, 16)
                sp.dma_start(b1[:, n], io["ffb1"][bass.ds(ex, 1)].rearrange("o p f -> p (o f)")).then_inc(w_ld, 16)
                sp.dma_start(b2[:, n], io["ffb2"][bass.ds(ex, 1), :].broadcast_to([P, D])).then_inc(w_ld, 16)
            sp.dma_start(lng, io["ln_g"].broadcast_to([P, D])).then_inc(w_ld, 16)
            sp.dma_start(lnb, io["ln_b"].broadcast_to([P, D])).then_inc(w_ld, 16)
            def each(it):
                for k in range(G7):
                    sp.wait_ge(o_rdy, G7 * it + (k + 1))
                    sp.dma_start(io["out"][bass.ds(it * (G7 * P) + k * P, P), :], z1[:, k]).then_inc(st[k], 16)
            steps(sp, NT // G7, each)
            for k in range(G7):
                sp.wait_ge(st[k], 16 * (NT // G7))

        @block.gpsimd
        def _(pool):
            pool.wait_ge(w_ld, 160)
            with pool.Fori(0, NT) as i:
                pool.tensor_tensor(col(e.A, i * D, D), col(e.A, i * D, D), lnb, ALU.add).then_inc(xb, 1)

        @block.vector
        def _(dve):
            dve.wait_ge(w_ld, 160)
            for n in range(2):
                dve.tensor_scalar(w2[:, n], w2[:, n], e.weight[:, n:n + 1], None, ALU.mult).then_inc(w_rdy, 1)
            dve.tensor_scalar(b2[:, 0], b2[:, 0], e.weight[:, 0:1], None, ALU.mult).then_inc(w_rdy, 1)
            dve.wait_ge(w_rdy, 3)
            dve.scalar_tensor_tensor(out=b2c, in0=b2[:, 1], scalar=e.weight[:, 1:2], in1=b2[:, 0], op0=ALU.mult,
                                     op1=ALU.add).then_inc(w_rdy, 1)
            dve.wait_ge(w_rdy, 4)
            bf = bst.rearrange("p a b -> p (a b)")

            def tile(i, k):
                z = col(e.B, i * D, D)
                dve.tensor_tensor(z, z, b2c, ALU.add).then_inc(z_rdy, 1)
                dve.wait_ge(o_done, i + 1)
                dve.wait_ge(z_rdy, 2 * i + 1)
                dve.tensor_tensor(z, bank_o[k % 4][:, 0:D], z, ALU.add).then_inc(z_rdy, 1)
                dve.wait_ge(z_rdy, 2 * i + 2)
                dve.bn_stats(col(bf, 6 * i, 6), z).then_inc(bs, 1)

            def each(s):
                for j in range(8):
                    tile(8 * s + j, j)
            steps(dve, STEPS, each)
            tile(NT - 1, 0)
            dve.wait_ge(bs, NT)
            link = linker(dve, v)
            row_moments(link, dve, bst, mean, var, nmr)
            link(dve.tensor_scalar(rstd, var, EPS, None, ALU.add))
            dve.wait_ge(a, 1)
            link(dve.reciprocal(rstd, rstd))
            link(dve.tensor_tensor(nmr, mean, rstd, ALU.mult))
            link(dve.tensor_scalar(nmr, nmr, -1.0, None, ALU.mult))
            def each(it):
                for k in range(G7):
                    i = it * G7 + k
                    dve.wait_ge(n_rdy, i + 1)
                    dve.tensor_tensor(z1[:, k], z1[:, k], lng, ALU.mult).then_inc(g_rdy, 1)
                    if k == 0:
                        dve.wait_ge(xb, NT)
                    dve.wait_ge(g_rdy, i + 1)
                    dve.tensor_tensor(z1[:, k], z1[:, k], col(e.A, i * D, D), ALU.add).then_inc(o_rdy, 1)
            steps(dve, NT // G7, each)

        @block.scalar
        def _(act):
            act.wait_ge(w_ld, 160)

            def gelu(n, s, w, used):
                free(act, o_done, used)
                for m in range(8):
                    x, f = m // 4, m % 4
                    act.wait_ge(h_done, 8 * n + (m + 1))
                    act.activation(hT[s][:, x, f, 0:w], bank_h[m % 4][:, 0:w], ACT.Gelu, bias=b1[:, x, f:f + 1]
                                   ).then_inc(h_rdy, 1)

            gelu(0, 0, 512, 0)
            def each(s):
                for c in range(2):
                    gelu(2 * s + (c + 1), 1 - c, 512, 8 * s + 4 * c)
            steps(act, STEPS - 1, each)
            gelu(2 * STEPS - 1, 1, 512, 8 * (STEPS - 1))
            gelu(2 * STEPS, 0, P, 8 * (STEPS - 1) + 4)
            act.wait_ge(v, MOMENTS + 1)
            act.activation(rstd, rstd, ACT.Sqrt).then_inc(a, 1)
            act.wait_ge(v, MOMENTS + 4)
            def each(it):
                for k in range(G7):
                    i = it * G7 + k
                    free(act, st[k], 16 * it)
                    act.activation(z1[:, k], col(e.B, i * D, D), ACT.Identity, scale=col(rstd, i), bias=col(nmr, i)
                                   ).then_inc(n_rdy, 1)
            steps(act, NT // G7, each)

        @block.tensor
        def _(pe):
            def up(n, w):
                for m in range(8):
                    x, f = m // 4, m % 4
                    free(pe, h_rdy, 8 * n + (m - 3) if m > 3 else 8 * n)
                    for k in range(2):
                        mm = pe.matmul(bank_h[m % 4][:, 0:w], w1[:, x, k, f * P:(f + 1) * P],
                                       xc[:, k, bass.ds(n * 512, w)], start=(k == 0), stop=(k == 1))
                    mm.then_inc(h_done, 1)

            def down(n, s, tiles):
                pe.wait_ge(h_rdy, 8 * n + 8)
                free(pe, z_rdy, 8 * n)
                for t in range(tiles):
                    for m in range(8):
                        mm = pe.matmul(bank_o[t][:, 0:D], hT[s][:, m // 4, m % 4, t * P:(t + 1) * P],
                                       w2[:, m // 4, m % 4], start=(m == 0), stop=(m == 7))
                    mm.then_inc(o_done, 1)

            pe.wait_ge(w_rdy, 4)
            up(0, 512)
            def each(s):
                for c in range(2):
                    up(2 * s + (c + 1), 512)
                    down(2 * s + c, c, 4)
            steps(pe, STEPS - 1, each)
            up(2 * STEPS - 1, 512)
            down(2 * STEPS - 2, 0, 4)
            up(2 * STEPS, P)
            down(2 * STEPS - 1, 1, 4)
            down(2 * STEPS, 0, 1)


def build(nc, io, upto=99):
    with ExitStack() as ctx:
        e = setup(nc, ctx, io)
        for n, phase in enumerate(PHASES):
            if n < upto:
                phase(nc, e)


PHASES = [phase_nodes, phase_convolve, phase_mix, phase_edges, phase_combine, phase_residual,
          phase_experts]


def _layout(inputs):
    import numpy as _np
    g = {k: _np.asarray(v) for k, v in inputs.items()}

    def feat(a, axis):
        a = _np.moveaxis(a, axis, -1)
        s, v = a[..., :MUL], a[..., MUL:]
        v = v.reshape(v.shape[:-1] + (MUL, 3)).swapaxes(-1, -2).reshape(v.shape)
        return _np.ascontiguousarray(_np.moveaxis(_np.concatenate([s, v], -1), -1, axis))

    def edges(a, pad):
        full = _np.full((NH * HALF * P,) + a.shape[1:], pad, a.dtype)
        full[:E] = a
        return _np.ascontiguousarray(full.reshape((NH, HALF, P) + a.shape[1:]).swapaxes(1, 2))

    x = _np.zeros((NP, D), g["x"].dtype)
    x[:N] = feat(g["x"], 1)
    a8 = edges(g["edge_attr_8"], 0)
    qkv = feat(g["L0_mix_w_qkv"], 1)
    row = lambda a: _np.ascontiguousarray(a.reshape(1, -1))
    out = {
        "x": x,
        "src": edges(g["src"], N),
        "dst": edges(g["dst"], 0),
        "sh": edges(g["edge_attr_4"], 0),
        "a8": _np.ascontiguousarray(a8.transpose(0, 2, 3, 1).reshape(NI, P, P)),
        "w1_s": g["L0_gnn_w1_s"], "w1_v": g["L0_gnn_w1_v"], "wsc_s": g["L0_gnn_wsc_s"], "wsc_v": g["L0_gnn_wsc_v"],
        "w2_s": g["L0_gnn_w2_s"], "w2_v": g["L0_gnn_w2_v"],
        "fc1": g["L0_gnn_fc_w1"], "fc2": g["L0_gnn_fc_w2"], "fc3": g["L0_gnn_fc_w3"],
        "g_s": row(g["L0_gnn_g_s"]), "g_v": row(g["L0_gnn_g_v"]),
        "w_qkv": _np.ascontiguousarray(qkv.transpose(2, 1, 0)),
        "bn_g": _np.ascontiguousarray(g["L0_mix_bn_gamma"].reshape(NCH, P).T),
        "bn_b": _np.ascontiguousarray(g["L0_mix_bn_beta"].reshape(NCH, P).T),
        "w_dw": _np.ascontiguousarray(g["L0_mix_w_dw"].reshape(NCH, P, 5).transpose(2, 1, 0)),
        "w_pw": _np.ascontiguousarray(g["L0_mix_w_pw"].reshape(NCH, 4, DIM, DIM).transpose(1, 3, 0, 2)),
        "w_res": _np.ascontiguousarray(feat(g["L0_mix_w_res"], 0).reshape(D, GROUPS * DIM).T),
        "b_res": row(feat(g["L0_mix_b_res"], 0)),
        "wr": feat(g["L0_ffn_Wr"], 0), "br": row(g["L0_ffn_br"]),
        "ffn1": feat(g["L0_ffn_W1"], 1),
        "ffb1": _np.ascontiguousarray(g["L0_ffn_b1"].reshape(NE, 4, P).swapaxes(1, 2)),
        "ffn2": feat(g["L0_ffn_W2"], 2), "ffb2": feat(g["L0_ffn_b2"], 1),
        "ln_g": row(feat(g["L0_ffn_gamma"], 0)), "ln_b": row(feat(g["L0_ffn_beta"], 0)),
    }
    return out


def _result(out):
    import numpy as _np
    s, v = out[:N, :MUL], out[:N, MUL:]
    v = v.reshape(N, 3, MUL).swapaxes(1, 2).reshape(N, 3 * MUL)
    return _np.ascontiguousarray(_np.concatenate([s, v], 1))


def kernel(**inputs):
    import concourse.bacc as _bacc
    from concourse import mybir as _mybir
    from concourse.bass_utils import run_bass_kernel_spmd as _run

    nc = _bacc.Bacc("TRN2", target_bir_lowering=False, num_devices=1)
    arrays, io = {}, {}
    for name, a in _layout(inputs).items():
        arrays[f"in_{name}_dram"] = a
        io[name] = nc.dram_tensor(f"in_{name}_dram", a.shape, _mybir.dt.from_np(a.dtype), kind="ExternalInput").ap()
    io["out"] = nc.dram_tensor("out_0_dram", (NP, D), _mybir.dt.float32, kind="ExternalOutput").ap()
    build(nc, io)
    r = _run(nc, [arrays], core_ids=[0])
    return _result(r.results[0]["out_0_dram"])
```

```python
import math
from contextlib import ExitStack

import numpy as np

import concourse.bass as bass
from concourse import mybir

F32 = mybir.dt.float32
BF16 = mybir.dt.bfloat16
I32 = mybir.dt.int32
U32 = mybir.dt.uint32
ALU = mybir.AluOpType
ACT = mybir.ActivationFunctionType
AX = mybir.AxisListType

P = 128
N = 6250
D = 256
MUL = 64
E = 206250
NT = -(-N // P)
NP = NT * P
LAST = N - (NT - 1) * P
G7 = 7
HALF = 8
STEP = 2 * HALF
NH = 2 * (-(-E // (STEP * P)))
NI = NH // 2
TABLES = 3
TABLE = [0, 1, 2] * 4 + [0, 1, 0, 2]
ROW = 516
TRASH = NP
TROWS = NP + P
ZERO_ROWS = 5
ZERO_PARTS = TROWS // (P * ZERO_ROWS)
CH = 768
NCH = CH // P
GROUPS = 16
DIM = 32
FF = 512
NE = 8
EPS = 1e-5
MIN_NORM = 1e-15
MAXN = float(np.float32(1.0 - 1e-5))
ATANH_MAXN = float(np.arctanh(np.float64(np.float32(1.0 - 1e-5))))
INV_SQRT3 = 0.5773502691896258
CAPACITY = float(math.ceil(N * 1.25 / NE))


class Arena:

    def __init__(self, tensor, size):
        self.tensor, self.size, self.at = tensor, size, 0

    def reset(self):
        self.at = 0

    def take(self, *shape):
        n = int(np.prod(shape))
        ap = self.tensor[:, self.at:self.at + n]
        self.at += n
        assert self.at <= self.size, (self.at, self.size)
        if len(shape) == 1:
            return ap
        names = "abcd"[:len(shape)]
        spec = f"p ({' '.join(names)}) -> p {' '.join(names)}"
        return ap.rearrange(spec, **{names[i]: shape[i] for i in range(1, len(shape))})


class Env:
    pass


def free(eng, sem, value):
    if not isinstance(value, int) or value > 0:
        eng.wait_ge(sem, value)


def scatters(i, t):
    return TABLE.count(TABLE[t]) * i + TABLE[:t].count(TABLE[t])


ROT, AGO = (0, 1, 2, 0, 1, 2, 1), (4, 2, 4, 3, 3, 3, 2)


def tile_steps(eng, *stages):
    def step(it):
        for k in range(G7):
            for f, lag in stages:
                if k >= lag:
                    f(it, k - lag)
                elif not isinstance(it, int) or it:
                    f(it - 1, k - lag + G7)

    step(0)
    step(1)
    with eng.Fori(2, NT // G7) as it:
        step(it)
    for k in range(max(lag for _, lag in stages)):
        for f, lag in stages:
            if k < lag:
                f(NT // G7 - 1, k - lag + G7)


def steps(eng, n, step):
    step(0)
    with eng.Fori(1, n) as i:
        step(i)


def col(ap, i, n=1):
    return ap[:, bass.ds(i, n)]


def setup(nc, ctx, io):
    e = Env()
    e.io = io
    e.sb = lambda n, s, d=F32: ctx.enter_context(nc.sbuf_tensor(n, s, d))
    e.ps = lambda n, s, d=F32: ctx.enter_context(nc.psum_tensor(n, s, d))
    e.sem = lambda n: ctx.enter_context(nc.semaphore(n))
    e.dram = lambda n, s: nc.dram_tensor(n, s, F32).ap()
    e.A = e.sb("region_a", [P, NT * D])
    e.B = e.sb("region_b", [P, 2 * NP])
    e.C = e.sb("region_c", [P, 2 * NP])
    e.zero = e.C[:, 0:ZERO_ROWS * ROW]
    e.arena = Arena(e.sb("scratch", [P, 14100]), 14100)
    e.ident = e.sb("ident", [P, P])
    e.pick = e.sb("picked_experts", [1, 2], I32)
    e.weight = e.sb("expert_weights", [P, 2])
    e.bn = e.sb("bn_scale_shift", [P, 2, NCH])
    e.eq = e.sb("equal_src", [P, 2, 2, P], BF16)
    e.row1 = e.sb("row_index", [P, P], BF16)[:, :]
    e.ident_b = e.sb("ident_bf16", [P, P], BF16)
    e.src_hl = e.sb("src_high_low", [P, 2, 2, HALF], BF16)
    e.junk = e.sb("junk", [P, 2, P], BF16)
    e.stat = e.sb("stat", [P, 12, NT])
    e.banks = [e.ps(f"bank{i}", [P, 512]) for i in range(8)]
    e.table_zeroed = e.sem("table_zeroed")
    e.stored = [e.sem(f"tile_stored{k}") for k in range(G7)]
    e.y_d = e.dram("y_d", [NP, D])
    e.sc_d = e.dram("sc_d", [NP, D])
    e.conv_d = e.dram("conv_d", [NCH, P, NP])
    e.agg_d = [e.dram(f"agg{r}_d", [TROWS, ROW]) for r in range(TABLES)]
    return e


def zero_table(sp, e, r, part):
    rows = e.agg_d[r][bass.ds(part * (P * ZERO_ROWS), P * ZERO_ROWS), :]
    sp.dma_start(rows.rearrange("(p b) c -> p (b c)", b=ZERO_ROWS), e.zero).then_inc(e.table_zeroed, 16)


def linker(eng, sem):
    n = [0]

    def link(ins):
        n[0] += 1
        ins.then_inc(sem, 1)
        eng.wait_ge(sem, n[0])
    return link


def row_moments(link, dve, bst, mean, var, tmp):
    link(dve.tensor_tensor(mean, bst[:, :, 1], bst[:, :, 4], ALU.add))
    link(dve.tensor_scalar(mean, mean, 0.5, None, ALU.mult))
    link(dve.tensor_tensor(tmp, mean, bst[:, :, 1], ALU.subtract))
    link(dve.tensor_tensor(tmp, tmp, tmp, ALU.mult))
    link(dve.tensor_tensor(var, bst[:, :, 2], bst[:, :, 5], ALU.add))
    link(dve.tensor_scalar(var, var, 1.0 / D, None, ALU.mult))
    link(dve.tensor_tensor(var, var, tmp, ALU.add))


MOMENTS = 7


def phase_nodes(nc, e):
    io, ar, st = e.io, e.arena, e.stat
    ar.reset()
    e.wq, e.bn_gb, e.wq_ld = ar.take(2, CH), ar.take(2, NCH), e.sem("wq_ld")
    wy = ar.take(2, D)
    xn = ar.take(G7, D)
    hin = ar.take(G7, D)
    xnT = ar.take(G7, 2, P)
    ysc = ar.take(G7, 2, D)
    bst = ar.take(NT, 6)
    mean, var = ar.take(NT), ar.take(NT)
    s1, s2, q, l1, l2, sq, ser, msk, e2 = (ar.take(NT) for _ in range(9))
    rstd, ascale, norm = st[:, 0], st[:, 1], st[:, 2]
    ident = e.ident
    PARTS = ((0, 16), (16, 32), (32, 44), (44, NT))
    x_v = io["x"].rearrange("(t p) d -> p t d", p=P)
    x_ld, w_ld = [e.sem(f"x_ld{g}") for g in range(len(PARTS))], e.sem("wy_ld")
    z_zero, id0, id1 = e.sem("zero_tile"), e.sem("ident0"), e.sem("ident_ready")
    bs_done, v, a = e.sem("bn_done"), e.sem("nodes_vec"), e.sem("nodes_act")
    xn_rdy, hin_rdy, t_done, xnT_rdy, hT_rdy = (e.sem(n) for n in (
        "xn_ready", "hin_ready", "node_transposed", "xnT_ready", "hinT_ready"))
    y_done, ysc_rdy = e.sem("y_done"), e.sem("ysc_ready")
    st_y = e.stored
    bank_x = [(e.banks[0], e.banks[1], e.banks[6])[r] for r in ROT]
    bank_h = [(e.banks[4], e.banks[5], e.banks[7])[r] for r in ROT]
    bank_y = [e.banks[2 + k % 2] for k in range(G7)]
    Y_AGO = (1, 2, 2, 2, 2, 2, 2)

    with nc.Block() as block:
        @block.sync
        def _(sp):
            sp.dma_start(wy, io["w_nodes"]).then_inc(w_ld, 16)
            for g, (first, end) in enumerate(PARTS):
                sp.dma_start(e.A[:, first * D:end * D].rearrange("p (t d) -> p t d", d=D), x_v[:, first:end, :]
                             ).then_inc(x_ld[g], 16)
            sp.dma_start(e.wq, io["w_qkv"][2].rearrange("(k p) c -> p k c", p=P)).then_inc(e.wq_ld, 16)
            for n, name in enumerate(("bn_g", "bn_b")):
                sp.dma_start(e.bn_gb[:, n], io[name]).then_inc(e.wq_ld, 16)
            sp.wait_ge(z_zero, 1)

            def each(it):
                for k in range(G7):
                    sp.wait_ge(ysc_rdy, G7 * it + (k + 1))
                    sp.dma_start(e.y_d[bass.ds(it * (G7 * P) + k * P, P), :], ysc[:, k, 0]).then_inc(st_y[k], 16)
                    sp.dma_start(e.sc_d[bass.ds(it * (G7 * P) + k * P, P), :], ysc[:, k, 1]).then_inc(st_y[k], 16)
                zero_table(sp, e, 0, it)

            steps(sp, NT // G7, each)
            for k in range(G7):
                sp.wait_ge(st_y[k], 32 * (NT // G7))
            for part in range(NT // G7, ZERO_PARTS):
                zero_table(sp, e, 0, part)

        @block.gpsimd
        def _(pool):
            pool.memset(ident[:], 0.0).then_inc(id0, 1)
            pool.memset(e.zero, 0.0).then_inc(z_zero, 1)
            pool.wait_ge(id0, 1)
            pool.affine_select(out=ident[:], in_=ident[:], compare_op=ALU.not_equal, fill=1.0, base=0,
                               pattern=[[-1, P]], channel_multiplier=1).then_inc(id1, 1)

        @block.vector
        def _(dve):
            link = linker(dve, v)
            bstf = bst.rearrange("p a b -> p (a b)")
            for g, (first, end) in enumerate(PARTS):
                dve.wait_ge(x_ld[g], 16)
                with dve.Fori(first, end) as i:
                    dve.bn_stats(col(bstf, 6 * i, 6), col(e.A, i * D, D)).then_inc(bs_done, 1)
            dve.wait_ge(bs_done, NT)
            row_moments(link, dve, bst, mean, var, q)
            link(dve.tensor_scalar(s1, var, EPS, None, ALU.add))
            dve.wait_ge(a, 2)
            link(dve.reciprocal(rstd, s1))
            link(dve.tensor_tensor(norm, s2, rstd, ALU.mult))
            link(dve.tensor_scalar(norm, norm, MIN_NORM, None, ALU.max))
            link(dve.tensor_scalar(q, norm, MAXN, None, ALU.min))
            dve.wait_ge(a, 4)
            link(dve.tensor_tensor(l1, l1, l2, ALU.subtract))
            link(dve.tensor_scalar(l1, l1, 0.5, None, ALU.mult))
            link(dve.tensor_tensor(sq, q, q, ALU.mult))
            link(dve.tensor_scalar(ser, sq, 0.2, 1.0 / 3.0, ALU.mult, ALU.add))
            link(dve.tensor_tensor(ser, ser, sq, ALU.mult))
            link(dve.tensor_scalar(ser, ser, 1.0, None, ALU.add))
            link(dve.tensor_tensor(ser, ser, q, ALU.mult))
            link(dve.tensor_scalar(msk, q, 0.03, None, ALU.is_lt))
            link(dve.tensor_tensor(ser, ser, l1, ALU.subtract))
            link(dve.tensor_tensor(ser, ser, msk, ALU.mult))
            link(dve.tensor_tensor(l1, l1, ser, ALU.add))
            link(dve.reciprocal(e2, norm))
            link(dve.tensor_tensor(ascale, l1, e2, ALU.mult))

            def evac(it, k):
                i = it * G7 + k
                dve.wait_ge(t_done, i + 1)
                free(dve, y_done, i + 1 - G7)
                dve.tensor_copy(xnT[:, k], bank_x[k][:, 0:D].rearrange("p (c n) -> p c n", c=2)
                                ).then_inc(xnT_rdy, 1)

            def normed(it, k):
                i = it * G7 + k
                free(dve, t_done, i + 1 - G7)
                free(dve, hin_rdy, i + 1 - G7)
                dve.tensor_scalar(xn[:, k], col(e.A, i * D, D), col(mean, i), col(rstd, i),
                                  ALU.subtract, ALU.mult).then_inc(xn_rdy, 1)

            tile_steps(dve, (normed, 0), (evac, 2))

        @block.scalar
        def _(act):
            act.wait_ge(v, MOMENTS + 1)
            act.activation(s1, s1, ACT.Sqrt).then_inc(a, 1)
            act.activation(s2, var, ACT.Sqrt, scale=float(D)).then_inc(a, 1)
            act.wait_ge(v, MOMENTS + 5)
            act.activation(l1, q, ACT.Ln, bias=1.0).then_inc(a, 1)
            act.activation(l2, q, ACT.Ln, bias=1.0, scale=-1.0).then_inc(a, 1)
            act.wait_ge(v, MOMENTS + 18)
            hT = e.B[:, :].rearrange("p (c n) -> p c n", c=2)

            def scale(it, k):
                i = it * G7 + k
                act.wait_ge(xn_rdy, i + 1)
                free(act, t_done, i + 1 - G7)
                act.activation(hin[:, k], xn[:, k], ACT.Copy, scale=col(ascale, i)).then_inc(hin_rdy, 1)

            def keep(it, k):
                i = it * G7 + k
                act.wait_ge(t_done, i + 1)
                act.activation(hT[:, :, bass.ds(i * P, P)], bank_h[k][:, 0:D].rearrange("p (c n) -> p c n", c=2),
                               ACT.Copy).then_inc(hT_rdy, 1)

            def out(it, k):
                act.wait_ge(y_done, it * G7 + (k + 1))
                free(act, st_y[k], 32 * it)
                act.activation(ysc[:, k].rearrange("p h (c n) -> p c h n", c=2),
                               bank_y[k][:, :].rearrange("p (c h n) -> p c h n", c=2, h=2),
                               ACT.Copy, scale=0.125).then_inc(ysc_rdy, 1)

            tile_steps(act, (scale, 0), (keep, 2), (out, 3))

        @block.tensor
        def _(pe):
            pe.wait_ge(id1, 1)
            pe.wait_ge(w_ld, 16)

            def transposed(it, k):
                i = it * G7 + k
                pe.wait_ge(xn_rdy, i + 1)
                pe.wait_ge(hin_rdy, i + 1)
                free(pe, xnT_rdy, i + 1 - AGO[k])
                free(pe, hT_rdy, i + 1 - AGO[k])
                for bank, src in ((bank_x[k], xn[:, k]), (bank_h[k], hin[:, k])):
                    for c in range(2):
                        mm = pe.transpose(bank[:, c * P:(c + 1) * P], src[:, c * P:(c + 1) * P], ident[:])
                mm.then_inc(t_done, 1)

            def project(it, k):
                i = it * G7 + k
                pe.wait_ge(xnT_rdy, i + 1)
                free(pe, ysc_rdy, i + 1 - Y_AGO[k])
                for c in range(2):
                    mm = pe.matmul(bank_y[k][:, c * D:(c + 1) * D], xnT[:, k, c], wy[:, c], start=True, stop=True)
                mm.then_inc(y_done, 1)

            tile_steps(pe, (transposed, 0), (project, 2))


def phase_convolve(nc, e):
    ar, S = e.arena, e.sem
    ar.reset()
    wq, gb = ar.take(2, CH), ar.take(2, NCH)
    stage = ar.take(NCH, 512)
    full = N // 512
    tail, tail_w = N - full * 512, NP - full * 512
    bst = ar.take(NCH, full + 1, 6)
    bstf = bst.rearrange("p a b c -> p (a b c)")
    mv = ar.take(NCH, 2)
    t1 = ar.take(NCH)
    hT = e.B[:, :].rearrange("p (c n) -> p c n", c=2)
    conv, out, bs, v, a = S("conv_done"), S("conv_out"), S("conv_stats"), S("bn_vec"), S("bn_act")
    stored = [S(f"conv_stored{c}") for c in range(NCH)]

    with nc.Block() as block:
        @block.sync
        def _(sp):
            def store(n, w):
                for c in range(NCH):
                    sp.wait_ge(out, NCH * n + (c + 1))
                    sp.dma_start(e.conv_d[c][:, bass.ds(n * 512, w)], stage[:, c, 0:w]).then_inc(stored[c], 16)

            def with_zeros(n):
                store(n, 512)
                for r in range(1, TABLES):
                    zero_table(sp, e, r, n)

            steps(sp, ZERO_PARTS, with_zeros)
            for n in range(ZERO_PARTS, full):
                store(n, 512)
            store(full, tail_w)
            for c in range(NCH):
                sp.wait_ge(stored[c], 16 * (full + 1))

        @block.tensor
        def _(pe):
            pe.wait_ge(e.wq_ld, 48)

            def chunk(n, w):
                for c in range(NCH):
                    free(pe, out, NCH * n)
                    for k in range(2):
                        mm = pe.matmul(e.banks[c][:, 0:w], wq[:, k, c * P:(c + 1) * P],
                                       hT[:, k, bass.ds(n * 512, w)], start=(k == 0), stop=(k == 1))
                    mm.then_inc(conv, 1)

            def each(n):
                chunk(n, 512)

            steps(pe, full, each)
            chunk(full, tail_w)

        @block.scalar
        def _(act):
            def chunk(n, w):
                for c in range(NCH):
                    act.wait_ge(conv, NCH * n + (c + 1))
                    free(act, stored[c], 16 * n)
                    free(act, bs, NCH * n)
                    act.activation(stage[:, c, 0:w], e.banks[c][:, 0:w], ACT.Copy).then_inc(out, 1)

            def each(n):
                chunk(n, 512)

            steps(act, full, each)
            chunk(full, tail_w)
            act.wait_ge(v, 1)
            act.activation(t1, t1, ACT.Sqrt).then_inc(a, 1)

        @block.vector
        def _(dve):
            def chunk(n, w):
                for c in range(NCH):
                    dve.wait_ge(out, NCH * n + (c + 1))
                    dve.bn_stats(col(bstf, (n + c * (full + 1)) * 6, 6), stage[:, c, 0:w]).then_inc(bs, 1)

            def each(n):
                chunk(n, 512)

            steps(dve, full, each)
            chunk(full, tail)
            dve.wait_ge(bs, NCH * (full + 1))
            for c in range(NCH):
                dve.bn_aggr(mv[:, c], bst[:, c].rearrange("p a b -> p (a b)")).then_inc(bs, 1)
            dve.wait_ge(bs, NCH * (full + 2))
            link = linker(dve, v)
            link(dve.tensor_scalar(t1, mv[:, :, 1], EPS, None, ALU.add))
            dve.wait_ge(a, 1)
            dve.wait_ge(e.wq_ld, 48)
            link(dve.reciprocal(t1, t1))
            link(dve.tensor_tensor(e.bn[:, 0], t1, gb[:, 0], ALU.mult))
            link(dve.tensor_tensor(t1, mv[:, :, 0], e.bn[:, 0], ALU.mult))
            link(dve.tensor_tensor(e.bn[:, 1], gb[:, 1], t1, ALU.subtract))


def phase_edges(nc, e):
    io, ar = e.io, e.arena
    ar.reset()
    dst_i = [ar.take(HALF) for _ in range(2)]
    src_i = [ar.take(HALF) for _ in range(2)]
    src_f = [ar.take(HALF) for _ in range(2)]
    src_off = [ar.take(HALF) for _ in range(2)]
    sh = [ar.take(HALF, 4) for _ in range(2)]
    a8 = ar.take(P)
    h1s = ar.take(4 * P)
    h2T = [ar.take(4 * P) for _ in range(2)]
    w1v = ar.take(HALF, P)
    w2bd = ar.take(P)
    w3z = ar.take(2, D)
    yb = e.B[:, 0:2 * HALF * D].rearrange("p (h t d) -> p h t d", h=2, t=HALF)
    xb = ar.take(2, 2, 512)
    eq = e.eq
    seq = ar.take(2, 2, 4, P)
    msg = ar.take(8, ROW)
    idx = ar.take(STEP)
    count = ar.take(8)
    mx = ar.take(2, 2)
    tmp = ar.take(2)
    row1 = ar.take(P)
    p1, trash, pint = ar.take(1), ar.take(1), ar.take(1)
    idx_u = idx.bitcast(U32)
    ident = e.ident
    bank_h = e.banks[0]
    bank_r = e.banks[1]
    bank_w = e.banks[2:4]
    bank_m = e.banks[4:6]

    wide, narrow = e.banks[6], e.banks[7]
    mix = Arena(e.B, 2 * NP)
    mix.take(2 * HALF * D)
    hb = mix.take(NCH, P)
    wbd = mix.take(NCH, P)
    wres = mix.take(4, D)
    cat = mix.take(2 * CH)
    qkv = cat.rearrange("p (g c d) -> p g c d", g=GROUPS, c=3)
    kr = mix.take(GROUPS, DIM)
    qv = mix.take(GROUPS, DIM)
    den = mix.take(GROUPS, DIM)
    att = mix.take(GROUPS * DIM)
    attT = mix.take(4, P)
    dw = mix.take(NCH)
    n2, r2, kap, ks = mix.take(2), mix.take(2), mix.take(1), mix.take(GROUPS)
    squares = mix.take(CH).bitcast(BF16)
    squares_o = mix.take(GROUPS * DIM // 2).bitcast(BF16)
    o2 = e.stat[:, 9]

    S = e.sem
    c_ld, c_iota, c_rdy = S("edge_w_ld"), S("edge_iota"), S("edge_const")
    ld_dst = [S(f"ld_dst{h}") for h in range(2)]
    ld_src = [S(f"ld_src{h}") for h in range(2)]
    ld_sh = [S(f"ld_sh{h}") for h in range(2)]
    ld_a8 = S("ld_a8")
    srcf_rdy, srchi_rdy, srcoff_rdy = S("src_f_ready"), S("src_high_ready"), S("src_off_ready")
    h1_done, h2_done, silu1, silu2 = S("h1_done"), S("h2_done"), S("silu1"), S("silu2")
    w_done, rb_done, eq_done = S("w_done"), S("rows_done"), S("eq_done")
    mx_done, id_tmp, idx_rdy = S("last_edge"), S("idx_tmp"), S("idx_ready")
    sd_dve, sd_act = S("scaled_dve"), S("scaled_act")
    prod, comb, evac = S("products"), S("combined"), S("msg_ready")
    y_in = [[S(f"y_in{h}_{k}") for k in range(HALF)] for h in range(2)]
    scat = [S(f"scattered{r}") for r in range(TABLES)]

    msg0 = S("msg_zeroed")
    mw_ld, mw_rdy = S("mix_w_ld"), S("mix_w_ready")
    h_in, h_rdy, m_done, m_out, nrm = (S(n) for n in ("mix_in", "h_ready", "mix_product", "mix_copied", "mix_norm"))
    m_sq, mv, cat_used, att_rdy, t_done, o2_rdy, aT, res, r_out = (S(n) for n in (
        "mix_squares", "mix_vec", "cat_used", "att_ready", "att_transposed", "att_square", "attT_ready", "res_done",
        "res_copied"))
    BY_DVE = (range(2), range(1))
    LINKS = 13

    def slot_landed(eng, i, t):
        before, u = (i, t - 8) if t >= 8 else (i - 1, t + 8)
        free(eng, scat[TABLE[u]], 16 * scatters(before, u) + 16)

    def edge_steps(eng, step):
        def both(t, ahead):
            step(2 * t, 0, t, ahead)
            step(2 * t + 1, 1, t, ahead)

        both(0, True)
        with eng.Fori(1, NT - 1) as t:
            both(t, True)
        both(NT - 1, False)
        for i in range(2 * NT, NI):
            step(i)

    with nc.Block() as block:
        @block.sync
        def _(sp):
            def load_mix(t):
                sp.dma_start(hb, e.conv_d[:, :, bass.ds(t * P, P)].rearrange("c p n -> p c n")).then_inc(h_in, 16)

            def load(buf, name, half, sem):
                src = io[name][bass.ds(half, 1)]
                dims = " ".join("xyz"[:len(src.shape) - 2])
                sp.dma_start(buf, src.rearrange(f"a p {dims} -> (a p) {dims}")).then_inc(sem, 16)

            load(dst_i[0].bitcast(I32), "dst", 0, ld_dst[0])
            load(src_i[0].bitcast(I32), "src", 0, ld_src[0])
            sp.dma_start(a8, io["a8"][0]).then_inc(ld_a8, 16)
            for buf, name in ((w1v, "w_fc1"), (w2bd, "w_fc2"), (w3z, "w_fc3")):
                sp.dma_start(buf, io[name]).then_inc(c_ld, 16)
            load(sh[0], "sh", 0, ld_sh[0])
            load(dst_i[1].bitcast(I32), "dst", 1, ld_dst[1])
            load(src_i[1].bitcast(I32), "src", 1, ld_src[1])
            load(sh[1], "sh", 1, ld_sh[1])
            load_mix(0)
            sp.dma_start(wbd, io["w_point"]).then_inc(mw_ld, 16)
            sp.dma_start(dw, io["w_dw"][2]).then_inc(mw_ld, 16)
            sp.dma_start(wres, io["w_res"].rearrange("(k p) c -> p k c", p=P)).then_inc(mw_ld, 16)

            def step(i, half=0, t=None, ahead=False):
                if isinstance(i, int) and i == NI - 1:
                    return
                for h in range(2):
                    for k in range(HALF):
                        sp.wait_ge(y_in[h][k], 16 * i + 16)
                    load(dst_i[h].bitcast(I32), "dst", 2 * i + (2 + h), ld_dst[h])
                    sp.wait_ge(srcf_rdy, 2 * i + (1 + h))
                    load(src_i[h].bitcast(I32), "src", 2 * i + (2 + h), ld_src[h])
                    if h == 0:
                        sp.wait_ge(h1_done, 2 * i + 2)
                        sp.dma_start(a8, io["a8"][bass.ds(i + 1, 1)].rearrange("a r e -> (a r) e")).then_inc(ld_a8, 16)
                    sp.wait_ge(comb, 16 * i + 8 * (h + 1))
                    load(sh[h], "sh", 2 * i + (2 + h), ld_sh[h])
                    if h == 0 and half == 0 and ahead:
                        sp.wait_ge(m_done, 4 * t + 4)
                        load_mix(t + 1)

            edge_steps(sp, step)

        @block.gpsimd
        def _(pool):
            pool.iota(row1.bitcast(I32), pattern=[[1, P]], base=1, channel_multiplier=0)
            pool.iota(pint.bitcast(I32), pattern=[[0, 1]], base=0, channel_multiplier=1).then_inc(c_iota, 1)

            def gather(h, k, i, g):
                if k == 0:
                    pool.wait_ge(ld_dst[h], 16 * i + 16)
                if g is not None:
                    free(pool, prod, g - 3)
                    pool.nop(nofuse=True)
                pool.indirect_dma_start(yb[:, h, k], None, e.y_d, bass.IndirectOffsetOnAxis(
                    ap=dst_i[h].bitcast(U32)[:, k:k + 1], axis=0)).then_inc(y_in[h][k], 16)

            def scatter(i, j, k):
                t, slot = 2 * j + k, 2 * (j % 4) + k
                r = TABLE[t]
                if k == 0:
                    pool.wait_ge(idx_rdy, 8 * i + (j + 1))
                pool.wait_ge(evac, 16 * i + (t + 1))
                free(pool, scat[r], 16 * scatters(i, t))
                pool.nop(nofuse=True)
                pool.indirect_dma_start(e.agg_d[r], bass.IndirectOffsetOnAxis(ap=idx_u[:, t:t + 1], axis=0),
                                        msg[:, slot], None, compute_op=ALU.add).then_inc(scat[r], 16)

            def step(i, half=0, t=None, ahead=False):
                last = isinstance(i, int) and i == NI - 1
                for j in range(HALF):
                    for k in range(2):
                        kk = 2 * (j % 4) + k
                        if j < 4:
                            gather(1, kk, i, 8 * i + j)
                        elif not last:
                            gather(0, kk, i + 1, 8 * i + j)
                        scatter(i, j, k)

            for k in range(HALF):
                gather(0, k, 0, None)
            pool.memset(msg[:, :, 512:ROW], 0.0).then_inc(msg0, 1)
            pool.wait_ge(e.table_zeroed, 16 * TABLES * ZERO_PARTS)
            edge_steps(pool, step)
            for r in range(TABLES):
                pool.wait_ge(scat[r], 16 * TABLE.count(r) * NI)

        @block.vector
        def _(dve):
            dve.wait_ge(c_iota, 1)
            dve.tensor_copy(e.row1, row1.bitcast(I32)).then_inc(c_rdy, 1)
            dve.tensor_scalar(p1, pint.bitcast(I32), 1.0, None, ALU.add).then_inc(c_rdy, 1)
            dve.tensor_scalar(trash, pint.bitcast(I32), float(TRASH), None, ALU.add).then_inc(c_rdy, 1)
            dve.tensor_copy(e.ident_b[:], ident[:]).then_inc(c_rdy, 1)
            dve.wait_ge(c_rdy, 4)

            def sources(h, i, H):
                dve.wait_ge(ld_src[h], 16 * i + 16)
                dve.tensor_copy(src_f[h], src_i[h].bitcast(I32)).then_inc(srcf_rdy, 1)
                dve.wait_ge(srcf_rdy, H + 1)
                dve.tensor_copy(e.src_hl[:, h, 0], src_f[h]).then_inc(srchi_rdy, 1)
                dve.wait_ge(srchi_rdy, H + 1)
                dve.tensor_tensor(e.src_hl[:, h, 1], src_f[h], e.src_hl[:, h, 0], ALU.subtract)
                dve.tensor_scalar(src_off[h], src_f[h], trash, None, ALU.subtract).then_inc(srcoff_rdy, 1)

            def pair(i, h, j, H):
                s, q, g = j % 2, j % 4, 8 * i + j
                w = bank_w[s][:, :].rearrange("p (t f u) -> p t f u", t=2, f=4)
                y = yb[:, h, 2 * q:2 * q + 2]
                x = xb[:, s].rearrange("p t (h s u) -> p t h s u", h=2, s=4)

                def vectors(k):
                    return dve.tensor_tensor(
                        x[:, k, :, 1:4],
                        w[:, k, 2:4].rearrange("p (f o) u -> p f o u", o=1).broadcast_to([P, 2, 3, 64]),
                        y[:, k, 64:256].rearrange("p (o c u) -> p o c u", o=1, c=3).broadcast_to([P, 2, 3, 64]),
                        ALU.mult)

                dve.wait_ge(srcoff_rdy, H + 1)
                dve.wait_ge(rb_done, g + 1)
                free(dve, comb, 2 * g - 2)
                free(dve, evac, 2 * g - 6)
                for k in range(2):
                    t = 2 * q + k
                    last = dve.tensor_scalar(eq[:, s, k], bank_r[:, k * P:(k + 1) * P], src_f[h][:, t:t + 1], None,
                                             ALU.is_equal, ALU.add, accum_out=count[:, t:t + 1])
                last.then_inc(eq_done, 1)
                dve.wait_ge(w_done, g + 1)
                for k in range(2):
                    dve.wait_ge(y_in[h][2 * q + k], 16 * i + 16)
                dve.tensor_tensor(x[:, :, :, 0], w[:, :, 0:2],
                                  y[:, :, 0:64].rearrange("p t (o u) -> p t o u", o=1).broadcast_to([P, 2, 2, 64]),
                                  ALU.mult)
                dve.wait_ge(eq_done, g + 1)
                for k in range(2):
                    for c in BY_DVE[k]:
                        last = dve.tensor_scalar(seq[:, s, k, c], eq[:, s, k], sh[h][:, 2 * q + k, c:c + 1], None,
                                                 ALU.mult)
                last.then_inc(sd_dve, 1)
                for k in range(2):
                    last = dve.tensor_tensor_reduce(e.junk[:, k], eq[:, s, k], e.row1, 1.0, 0.0, ALU.mult, ALU.max,
                                                    mx[:, s, k:k + 1])
                last.then_inc(mx_done, 1)
                vectors(0)
                dve.wait_ge(mx_done, g + 1)
                dve.scalar_tensor_tensor(out=tmp, in0=mx[:, s], scalar=p1, in1=src_off[h][:, 2 * q:2 * q + 2],
                                         op0=ALU.is_equal, op1=ALU.mult).then_inc(id_tmp, 1)
                vectors(1).then_inc(prod, 1)
                dve.wait_ge(id_tmp, g + 1)
                for t in range(2 * j, 2 * j + 2):
                    free(dve, scat[TABLE[t]], 16 * scatters(i - 1, t) + 16)
                dve.tensor_scalar(idx_u[:, 2 * j:2 * j + 2], tmp, trash, None, ALU.add).then_inc(idx_rdy, 1)

            def mark(ins):
                ins.then_inc(mv, 1)

            def keys_values(t):
                dve.wait_ge(m_out, 4 * t + 4)
                free(dve, att_rdy, t)
                mark(dve.tensor_scalar(kr, qkv[:, :, 1], 0.0, None, ALU.max))
                mark(dve.scalar_tensor_tensor(out=qv, in0=qkv[:, :, 0], scalar=0.0, in1=qkv[:, :, 2], op0=ALU.max,
                                              op1=ALU.mult))

            def factor(t):
                dve.wait_ge(nrm, t + 1)
                mark(dve.tensor_scalar(r2, r2, MIN_NORM, None, ALU.max))
                dve.wait_ge(mv, LINKS * t + 4)
                mark(dve.reciprocal(r2, r2))
                dve.wait_ge(mv, LINKS * t + 5)
                mark(dve.tensor_scalar(r2, r2, ATANH_MAXN, 1.0, ALU.mult, ALU.min))
                dve.wait_ge(mv, LINKS * t + 6)
                mark(dve.tensor_tensor(kap, r2[:, 0:1], r2[:, 1:2], ALU.min))
                dve.wait_ge(mv, LINKS * t + 7)
                mark(dve.tensor_scalar(den, qkv[:, :, 2], kap, MIN_NORM, ALU.mult, ALU.add))
                dve.wait_ge(mv, LINKS * t + 8)
                dve.sem_inc(cat_used, 1)

            def attention(t):
                dve.wait_ge(mv, LINKS * t + 11)
                mark(dve.scalar_tensor_tensor(out=qv, in0=qv, scalar=kap, in1=den, op0=ALU.mult, op1=ALU.mult))
                mark(dve.tensor_scalar(ks, ks, kap, kap, ALU.mult, ALU.mult))
                dve.wait_ge(mv, LINKS * t + 13)
                free(dve, t_done, t)
                free(dve, o2_rdy, t)
                dve.tensor_tensor(att.rearrange("p (g d) -> p g d", g=GROUPS), qv,
                                  ks.rearrange("p (g o) -> p g o", o=1).broadcast_to([P, GROUPS, DIM]),
                                  ALU.mult).then_inc(att_rdy, 1)

            def mixer(t, place):
                if place == 0 and isinstance(t, int) and t == 0:
                    dve.wait_ge(mw_ld, 16 * 3)
                    for c in range(NCH):
                        dve.tensor_scalar(wbd[:, c], wbd[:, c], dw[:, c:c + 1], None, ALU.mult).then_inc(mw_rdy, 1)
                if place == 5:
                    keys_values(t)
                if place == 6:
                    dve.wait_ge(mv, LINKS * t + 1)
                    mark(dve.tensor_reduce(ks, kr, AX.X, ALU.add))
                if place == 7:
                    factor(t)
                if place in (8, 9, 10):
                    part = den[:, (0, 6, 11)[place - 8]:(6, 11, GROUPS)[place - 8]]
                    mark(dve.reciprocal(part, part))
                if place == 11:
                    attention(t)

            def step(i, half=0, t=None, ahead=False):
                last = isinstance(i, int) and i == NI - 1
                for j in range(HALF):
                    if j == 1:
                        sources(1, i, 2 * i + 1)
                    if j == 5 and not last:
                        sources(0, i + 1, 2 * i + 2)
                    if j < 7 or not last:
                        nj = (j + 1) % HALF
                        nh, ni = nj // 4, i if j < 7 else i + 1
                        dve.wait_ge(ld_sh[nh], 16 * ni + 16)
                        pair(ni, nh, nj, 2 * i + (j + 1) // 4)
                    if t is not None:
                        mixer(t, HALF * half + j)

            sources(0, 0, 0)
            dve.wait_ge(ld_sh[0], 16)
            pair(0, 0, 0, 0)
            edge_steps(dve, step)

        @block.scalar
        def _(act):
            def first(H):
                act.wait_ge(h1_done, H + 1)
                free(act, h2_done, H)
                act.activation(h1s, bank_h[:, :], ACT.Silu, scale=float(8 ** -0.5)).then_inc(silu1, 1)

            def second(h, H, used):
                act.wait_ge(h2_done, H + 1)
                free(act, w_done, used)
                act.activation(h2T[h], bank_h[:, :], ACT.Silu, scale=0.125).then_inc(silu2, 1)

            def scaled(g, h, j):
                s, q = j % 2, j % 4
                act.wait_ge(eq_done, g + 1)
                free(act, comb, 2 * g - 2)
                for k in range(2):
                    for c in range(len(BY_DVE[k]), 4):
                        last = act.activation(seq[:, s, k, c], eq[:, s, k], ACT.Copy,
                                              scale=sh[h][:, 2 * q + k, c:c + 1])
                last.then_inc(sd_act, 1)

            def evacuate(i, j):
                for k in range(2):
                    act.wait_ge(comb, 16 * i + (2 * j + k + 1))
                    slot_landed(act, i, 2 * j + k)
                    slot = 2 * (j % 4) + k
                    act.activation(msg[:, slot, 0:512], bank_m[k][:, :], ACT.Copy)
                    act.activation(msg[:, slot, 512:513], count[:, slot:slot + 1], ACT.Copy).then_inc(evac, 1)

            def relu(t, part):
                act.wait_ge(h_in, 16 * t + 16)
                for c in range(3 * part, 3 * part + 3):
                    last = act.activation(hb[:, c], hb[:, c], ACT.Relu, scale=e.bn[:, 0, c:c + 1],
                                          bias=e.bn[:, 1, c:c + 1])
                last.then_inc(h_rdy, 1)

            def square(part):
                return act.activation(squares[:, part * CH:(part + 1) * CH], cat[:, part * CH:(part + 1) * CH],
                                      ACT.Square, accum_out=n2[:, part:part + 1])

            def mixer(t, place, ahead):
                if 1 <= place <= 4:
                    bank, at, w = ((wide, 0, 512), (narrow, 512, 256), (wide, 768, 512), (narrow, 1280, 256))[place - 1]
                    act.wait_ge(m_done, 4 * t + place)
                    if place == 1:
                        free(act, cat_used, t)
                    act.activation(cat[:, at:at + w], bank[:, 0:w], ACT.Copy).then_inc(m_out, 1)
                if place == 3:
                    act.wait_ge(m_out, 4 * t + 2)
                    square(0)
                if place == 5:
                    act.wait_ge(m_out, 4 * t + 4)
                    square(1).then_inc(m_sq, 1)
                if place == 6:
                    act.wait_ge(m_sq, t + 1)
                    act.activation(r2[:, 1:2], n2[:, 0:1], ACT.Sqrt, bias=n2[:, 1:2])
                    act.activation(r2[:, 0:1], n2[:, 0:1], ACT.Sqrt).then_inc(nrm, 1)
                if place in (8, 9) and ahead:
                    relu(t + 1, place - 8)
                if place == 13:
                    act.wait_ge(t_done, t + 1)
                    act.activation(attT.rearrange("p a b -> p (a b)"), wide[:, :], ACT.Copy).then_inc(aT, 1)
                if place == 14:
                    act.wait_ge(att_rdy, t + 1)
                    act.activation(squares_o, att, ACT.Square, accum_out=col(o2, t)).then_inc(o2_rdy, 1)
                if place == 15:
                    act.wait_ge(res, t + 1)
                    act.activation(col(e.C, t * D, D), narrow[:, 0:D], ACT.Copy).then_inc(r_out, 1)

            def step(i, half=0, t=None, ahead=False):
                last = isinstance(i, int) and i == NI - 1
                for j in range(HALF):
                    if j == 1:
                        first(2 * i + 1)
                    if j == 2:
                        second(1, 2 * i + 1, 8 * i)
                    if j == 5 and not last:
                        first(2 * i + 2)
                    if j == 6 and not last:
                        second(0, 2 * i + 2, 8 * i + 4)
                    if j < 7 or not last:
                        nj = (j + 1) % HALF
                        scaled(8 * i + (j + 1), nj // 4, nj)
                    evacuate(i, j)
                    if t is not None:
                        mixer(t, HALF * half + j, ahead)

            act.wait_ge(c_rdy, 4)
            act.wait_ge(msg0, 1)
            first(0)
            act.wait_ge(h2_done, 1)
            act.activation(h2T[0], bank_h[:, :], ACT.Silu, scale=0.125).then_inc(silu2, 1)
            act.wait_ge(ld_sh[0], 16)
            scaled(0, 0, 0)
            relu(0, 0)
            relu(0, 1)
            edge_steps(act, step)

        @block.tensor
        def _(pe):
            def mlp1(h, i, H):
                pe.wait_ge(ld_a8, 16 * i + 16)
                free(pe, silu2, H)
                for q in range(4):
                    mm = pe.matmul(bank_h[:, q * P:(q + 1) * P], w1v[:, 4 * h + q], a8, start=True, stop=True)
                mm.then_inc(h1_done, 1)

            def mlp2(H):
                pe.wait_ge(silu1, H + 1)
                pe.matmul(bank_h[:, :], w2bd, h1s, start=True, stop=True).then_inc(h2_done, 1)

            def stage(g, h, j, H):
                s, q = j % 2, j % 4
                if q == 0:
                    pe.wait_ge(silu2, H + 1)
                    pe.wait_ge(srcoff_rdy, H + 1)
                free(pe, eq_done, g)
                for k in range(2):
                    t = 2 * q + k
                    for part in range(2):
                        mm = pe.matmul(bank_r[:, k * P:(k + 1) * P],
                                       e.src_hl[:, h, part, t:t + 1].broadcast_to([P, P]), e.ident_b[:],
                                       start=(part == 0), stop=(part == 1))
                mm.then_inc(rb_done, 1)
                free(pe, prod, g - 1)
                for k in range(2):
                    mm = pe.matmul(bank_w[s][:, k * D:(k + 1) * D], h2T[h][:, q * P:(q + 1) * P], w3z[:, k],
                                   start=True, stop=True)
                mm.then_inc(w_done, 1)

            def combine(g, j):
                s = j % 2
                pe.wait_ge(eq_done, g + 1)
                pe.wait_ge(prod, g + 1)
                pe.wait_ge(sd_dve, g + 1)
                pe.wait_ge(sd_act, g + 1)
                for k in range(2):
                    free(pe, evac, 2 * g + (k - 1))
                    x = xb[:, s, k]
                    m = bank_m[k]
                    pe.matmul(m[:, 0:256], seq[:, s, k, 0], x[:, 0:256], start=True, stop=False,
                              skip_group_check=True)
                    z = x[:, 256:512].rearrange("p (s u) -> p s u", s=4)
                    o = m[:, 256:512].rearrange("p (s u) -> p s u", s=4)
                    for c in range(3):
                        mm = pe.matmul(o[:, c::3 - c], seq[:, s, k, c + 1], z[:, 0::c + 1][:, 0:2],
                                       start=False, stop=(c == 2), skip_group_check=True)
                    mm.then_inc(comb, 1)

            def mixer(t, place):
                if place in (0, 1):
                    bank, chunks = ((wide, range(4)), (narrow, range(4, NCH)))[place]
                    if place == 0:
                        pe.wait_ge(h_rdy, 2 * t + 2)
                        free(pe, aT, t)
                    else:
                        free(pe, r_out, t)
                    for c in chunks:
                        mm = pe.transpose(bank[:, c % 4 * P:(c % 4 + 1) * P], hb[:, c], ident[:])
                    mm.then_inc(m_done, 1)
                if place in (2, 3):
                    bank, chunks = ((wide, range(4)), (narrow, range(4, NCH)))[place - 2]
                    if isinstance(t, int) and t == 0:
                        pe.wait_ge(mw_rdy, NCH)
                    pe.wait_ge(m_out, 4 * t + (place - 1))
                    for c in chunks:
                        mm = pe.matmul(bank[:, c % 4 * P:(c % 4 + 1) * P], hb[:, c], wbd[:, c], start=True, stop=True)
                    mm.then_inc(m_done, 1)
                if place == 12:
                    pe.wait_ge(att_rdy, t + 1)
                    pe.wait_ge(m_out, 4 * t + 3)
                    for c in range(4):
                        mm = pe.transpose(wide[:, c * P:(c + 1) * P], att[:, c * P:(c + 1) * P], ident[:])
                    mm.then_inc(t_done, 1)
                if place == 14:
                    pe.wait_ge(aT, t + 1)
                    pe.wait_ge(m_out, 4 * t + 4)
                    for c in range(4):
                        mm = pe.matmul(narrow[:, 0:D], attT[:, c], wres[:, c], start=(c == 0), stop=(c == 3))
                    mm.then_inc(res, 1)

            def step(i, half=0, t=None, ahead=False):
                last = isinstance(i, int) and i == NI - 1
                for j in range(HALF):
                    if j == 1:
                        mlp1(1, i, 2 * i + 1)
                    if j == 2:
                        mlp2(2 * i + 1)
                    if j == 5 and not last:
                        mlp1(0, i + 1, 2 * i + 2)
                    if j == 6 and not last:
                        mlp2(2 * i + 2)
                    if j < 7 or not last:
                        nj = (j + 1) % HALF
                        stage(8 * i + (j + 1), nj // 4, nj, 2 * i + (j + 1) // 4)
                    combine(8 * i + j, j)
                    if t is not None:
                        mixer(t, HALF * half + j)

            pe.wait_ge(c_ld, 16 * 3)
            pe.wait_ge(c_rdy, 4)
            mlp1(0, 0, 0)
            mlp2(0)
            stage(0, 0, 0, 0)
            edge_steps(pe, step)



def phase_combine(nc, e):
    io, ar, S = e.io, e.arena, e.sem
    ar.reset()
    w2 = ar.take(4, P)
    agg = ar.take(G7, TABLES, ROW)
    aggT = ar.take(3, 512)
    dg, rt, dn = ar.take(G7), ar.take(G7), ar.take(G7)
    junk = ar.take(2 * D).bitcast(BF16).rearrange("p (k h d) -> p k h d", k=2, h=2)
    bres = ar.take(D)
    ss, sv, nf2, o2, gam = (e.stat[:, k] for k in (4, 5, 3, 9, 10))
    ident = e.ident
    w_ld, w_rdy, bres_ld, part = S("w2_ld"), S("w2_ready"), S("b_res_ld"), S("agg_part")
    o2_root, v, ft = S("att_root"), S("scale_vec"), S("ft_ready")
    ld = [S(f"agg_in{k}") for k in range(G7)]
    summed, rooted, inv, t_done, aT, prod, g_rdy, sq = (S(n) for n in (
        "agg_sum", "deg_root", "deg_inverse", "agg_transposed", "aggT_ready", "w2_done", "g_ready", "g_squares"))
    b_t, b_r = ([e.banks[first + r] for r in ROT] for first in (0, 3))

    with nc.Block() as block:
        @block.gpsimd
        def _(pool):
            def each(it):
                for k in range(G7):
                    pool.wait_ge(ld[k], 16 * (TABLES + 1) * (it + 1))
                    pool.tensor_tensor(agg[:, k, 0, 0:513], agg[:, k, 0, 0:513], agg[:, k, 1, 0:513], ALU.add
                                       ).then_inc(part, 1)

            steps(pool, NT // G7, each)

        @block.sync
        def _(sp):
            sp.dma_start(w2, io["w_node2"]).then_inc(w_ld, 16)
            sp.dma_start(bres, io["b_res"].broadcast_to([P, D])).then_inc(bres_ld, 16)

            def each(it):
                for k in range(G7):
                    free(sp, t_done, G7 * it + (k + 1 - G7))
                    free(sp, rooted, G7 * it + (k + 1 - G7))
                    for r in range(TABLES):
                        sp.dma_start(agg[:, k, r], e.agg_d[r][bass.ds(it * (G7 * P) + k * P, P), :]).then_inc(ld[k], 16)
                    sp.dma_start(col(e.B, it * (G7 * D) + k * D, D), e.sc_d[bass.ds(it * (G7 * P) + k * P, P), :]
                                 ).then_inc(ld[k], 16)

            steps(sp, NT // G7, each)

        @block.vector
        def _(dve):
            dve.wait_ge(w_ld, 16)
            dve.wait_ge(bres_ld, 16)
            link = linker(dve, v)
            dve.wait_ge(o2_root, 1)
            link(dve.tensor_scalar(o2, o2, MIN_NORM, None, ALU.max))
            link(dve.reciprocal(gam, o2))
            link(dve.tensor_scalar(gam, gam, ATANH_MAXN, 1.0, ALU.mult, ALU.min))
            scale = float(128 ** -0.5 / 8)
            dve.tensor_scalar(w2, w2, scale, None, ALU.mult).then_inc(w_rdy, 1)
            dve.wait_ge(w_rdy, 1)
            dve.tensor_scalar(w2[64:128, 3], w2[64:128, 3], INV_SQRT3, None, ALU.mult).then_inc(w_rdy, 1)

            def total(it, k):
                i = it * G7 + k
                dve.wait_ge(part, i + 1)
                dve.tensor_tensor(agg[:, k, 0, 0:513], agg[:, k, 0, 0:513], agg[:, k, 2, 0:513], ALU.add
                                  ).then_inc(summed, 1)
                dve.wait_ge(summed, 2 * i + 1)
                dve.tensor_scalar(dg[:, k:k + 1], agg[:, k, 0, 512:513], 1.0, None, ALU.max).then_inc(summed, 1)

            def node(it, k):
                i = it * G7 + k
                dve.wait_ge(rooted, i + 1)
                dve.reciprocal(dn[:, k:k + 1], rt[:, k:k + 1]).then_inc(inv, 1)
                dve.wait_ge(inv, i + 1)
                dve.wait_ge(prod, i + 1)
                dve.scalar_tensor_tensor(out=col(e.B, i * D, D), in0=b_r[k][:, 0:D], scalar=dn[:, k:k + 1],
                                         in1=col(e.B, i * D, D), op0=ALU.mult, op1=ALU.add).then_inc(g_rdy, 1)
                c = col(e.C, i * D, D)
                dve.scalar_tensor_tensor(out=c, in0=c, scalar=col(gam, i), in1=bres, op0=ALU.mult, op1=ALU.add
                                         ).then_inc(ft, 1)

            tile_steps(dve, (total, 0), (node, 3))

        @block.scalar
        def _(act):
            act.activation(o2, o2, ACT.Sqrt).then_inc(o2_root, 1)

            def squares(it, k):
                i = it * G7 + k
                act.wait_ge(g_rdy, i + 1)
                free(act, sq, i - 1 if k else i)
                act.activation(junk[:, k % 2, 0, 0:64], col(e.B, i * D, 64), ACT.Square, accum_out=col(ss, i))
                act.activation(junk[:, k % 2, 0, 64:D], col(e.B, i * D + 64, 192), ACT.Square, accum_out=col(sv, i))
                act.wait_ge(ft, i + 1)
                act.activation(junk[:, k % 2, 1], col(e.C, i * D, D), ACT.Square, accum_out=col(nf2, i)).then_inc(sq, 1)

            def root(it, k):
                act.wait_ge(summed, 2 * G7 * it + (2 * k + 2))
                act.activation(rt[:, k:k + 1], dg[:, k:k + 1], ACT.Sqrt).then_inc(rooted, 1)

            def transposed(it, k):
                i = it * G7 + k
                act.wait_ge(t_done, i + 1)
                free(act, prod, i + 1 - AGO[k])
                act.activation(aggT[:, ROT[k]], b_t[k][:, :], ACT.Copy).then_inc(aT, 1)

            tile_steps(act, (root, 0), (transposed, 1), (squares, 4))

        @block.tensor
        def _(pe):
            pe.wait_ge(w_rdy, 2)

            def project(it, k):
                i = it * G7 + k
                pe.wait_ge(aT, i + 1)
                free(pe, g_rdy, i + 1 - AGO[k])
                b, a = b_r[k], aggT[:, ROT[k]]
                o = b[:, 0:D]
                ends = b[:, 0:D].rearrange("p (s u) -> p s u", s=4)[:, 0::3]
                for c, out in enumerate((o[:, 0:128], o[:, 128:256], o[:, 64:192], ends)):
                    mm = pe.matmul(out, a[:, c * P:(c + 1) * P], w2[:, c], start=(c == 0), stop=(c == 3),
                                   skip_group_check=True)
                mm.then_inc(prod, 1)

            def transposed(it, k):
                i = it * G7 + k
                pe.wait_ge(summed, 2 * i + 1)
                free(pe, aT, i + 1 - AGO[k])
                for c in range(4):
                    mm = pe.transpose(b_t[k][:, c * P:(c + 1) * P], agg[:, k, 0, c * P:(c + 1) * P], ident[:])
                mm.then_inc(t_done, 1)

            tile_steps(pe, (transposed, 0), (project, 2))


def phase_residual(nc, e):
    io, ar, S, st = e.io, e.arena, e.sem, e.stat
    ar.reset()
    gmul = ar.take(D)
    xs = ar.take(G7, D)
    bst, mean, var = ar.take(NT, 6), ar.take(NT), ar.take(NT)
    wr = ar.take(2, NE)
    br = ar.take(NE)
    row = ar.take(NE)
    eight = [ar.take(NE) for _ in range(6)]
    one = [ar.take(1) for _ in range(8)]
    pair = ar.take(2)
    sums = ar.take(2)
    ones = ar.take(P)
    nf2, ss, sv, rstd = st[:, 3], st[:, 4], st[:, 5], st[:, 0]
    dl, th, sv_r, nmr = st[:, 6], st[:, 7], st[:, 8], st[:, 11]
    b_t, b_sum = [e.banks[r] for r in ROT], e.banks[6:8]
    BY_ACT = (1, 3, 5)
    ident = e.ident
    w_ld, v, a = S("res_w_ld"), S("res_vec"), S("res_act")
    gs, xm, summed = S("g_scaled"), S("x_and_mixer"), S("x2_summed")
    gn, x1, bs, x2, tt, cT = S("g_normed"), S("x1_ready"), S("x1_stats"), S("x2_ready"), S("x2_transposed"), S("x2T_ready")
    p, c_rdy = S("route_pe"), S("route_const")

    with nc.Block() as block:
        @block.sync
        def _(sp):
            sp.dma_start(gmul[:, 0:64], io["g_s"].broadcast_to([P, 64])).then_inc(w_ld, 16)
            for d in range(3):
                sp.dma_start(gmul[:, 64 * (d + 1):64 * (d + 2)], io["g_v"].broadcast_to([P, 64])).then_inc(w_ld, 16)
            sp.dma_start(wr, io["wr"].rearrange("(k p) n -> p k n", p=P)).then_inc(w_ld, 16)
            sp.dma_start(br[0:1], io["br"]).then_inc(w_ld, 16)

        @block.gpsimd
        def _(pool):
            pool.memset(ones, 1.0)
            pool.iota(row[0:1].bitcast(I32), pattern=[[1, NE]], base=0, channel_multiplier=0).then_inc(c_rdy, 1)
            pool.wait_ge(w_ld, 16 * 6)
            with pool.Fori(0, NT) as i:
                pool.wait_ge(gs, i + 1)
                pool.tensor_tensor(col(e.B, i * D, D), col(e.B, i * D, D), gmul, ALU.mult).then_inc(gn, 1)

        @block.vector
        def _(dve):
            link = linker(dve, v)
            link(dve.tensor_scalar(ss, ss, 1.0 / MUL, EPS, ALU.mult, ALU.add))
            link(dve.tensor_scalar(sv, sv, 1.0 / (3 * MUL), EPS, ALU.mult, ALU.add))
            dve.wait_ge(a, 3)
            link(dve.reciprocal(ss, ss))
            link(dve.reciprocal(sv_r, sv))
            link(dve.tensor_scalar(nf2, nf2, MIN_NORM, None, ALU.max))
            link(dve.reciprocal(dl, nf2))
            dve.wait_ge(a, 4)
            link(dve.tensor_scalar(th, th, MAXN, None, ALU.min))
            link(dve.tensor_tensor(dl, dl, th, ALU.mult))
            bf = bst.rearrange("p a b -> p (a b)")

            def mixed(it, k):
                i = it * G7 + k
                dve.scalar_tensor_tensor(out=col(e.A, i * D, D), in0=col(e.C, i * D, D), scalar=col(dl, i),
                                         in1=col(e.A, i * D, D), op0=ALU.mult, op1=ALU.add).then_inc(xm, 1)

            def added(it, k):
                i = it * G7 + k
                dve.wait_ge(xm, i + 1)
                dve.wait_ge(gn, i + 1)
                dve.tensor_tensor(col(e.A, i * D, D), col(e.A, i * D, D), col(e.B, i * D, D), ALU.add
                                  ).then_inc(x1, 1)

            def stats(it, k):
                i = it * G7 + k
                dve.wait_ge(x1, i + 1)
                dve.bn_stats(col(bf, 6 * i, 6), col(e.A, i * D, D)).then_inc(bs, 1)

            tile_steps(dve, (mixed, 0), (added, 2), (stats, 3))
            dve.wait_ge(bs, NT)
            row_moments(link, dve, bst, mean, var, th)
            link(dve.tensor_scalar(rstd, var, EPS, None, ALU.add))
            dve.wait_ge(a, 5)
            link(dve.reciprocal(rstd, rstd))
            link(dve.scalar_tensor_tensor(out=nmr, in0=mean, scalar=-1.0, in1=rstd, op0=ALU.mult, op1=ALU.mult))

            def normed(it, k):
                i = it * G7 + k
                free(dve, summed, i + 1 - G7)
                x = (col(e.A, i * D, D), col(mean, i), col(rstd, i), ALU.subtract, ALU.mult)
                if k not in BY_ACT:
                    dve.tensor_scalar(col(e.B, i * D, D), *x)
                dve.tensor_scalar(xs[:, k], *x).then_inc(x2, 1)

            tile_steps(dve, (normed, 0))
            dve.wait_ge(summed, NT)
            for c in range(2):
                link(dve.tensor_scalar(sums[:, c:c + 1], b_sum[c][:, 0:1], 1.0 / N, None, ALU.mult))
            lg, ex, t1, t2, rw, ii = (z[0:1] for z in eight)
            mx, sm, i1, i2, v1, v2, e2, w1 = (z[0:1] for z in one)
            dve.wait_ge(c_rdy, 1)
            link(dve.tensor_copy(ii, row[0:1].bitcast(I32)))
            dve.wait_ge(p, 1)
            link(dve.tensor_tensor(lg, e.banks[4][0:1, 0:NE], br[0:1], ALU.add))
            link(dve.tensor_reduce(mx, lg, AX.X, ALU.max))
            link(dve.tensor_scalar(lg, lg, mx, None, ALU.subtract))
            dve.wait_ge(a, 6)
            link(dve.reciprocal(sm, sm))
            link(dve.tensor_scalar(rw, ex, sm, None, ALU.mult))
            link(dve.tensor_scalar(t1, rw, float(N), None, ALU.mult))
            link(dve.tensor_scalar(t2, t1, CAPACITY, None, ALU.is_gt))
            link(dve.tensor_scalar(t1, t1, CAPACITY, None, ALU.max))
            link(dve.reciprocal(t1, t1))
            link(dve.tensor_scalar(t1, t1, CAPACITY, -1.0, ALU.mult, ALU.add))
            link(dve.tensor_tensor(t1, t1, t2, ALU.mult))
            link(dve.tensor_scalar(t1, t1, 1.0, None, ALU.add))
            link(dve.tensor_tensor(rw, rw, t1, ALU.mult))
            link(dve.tensor_reduce(mx, rw, AX.X, ALU.max))
            link(dve.tensor_scalar(rw, rw, mx, None, ALU.subtract))
            dve.wait_ge(a, 7)
            link(dve.reciprocal(sm, sm))
            link(dve.tensor_scalar(rw, ex, sm, None, ALU.mult))
            for n, (val, at) in enumerate(((v1, i1), (v2, i2))):
                link(dve.tensor_reduce(val, rw, AX.X, ALU.max))
                link(dve.tensor_scalar(t1, rw, val, -1000.0, ALU.is_equal, ALU.mult))
                link(dve.tensor_tensor(t1, t1, ii, ALU.add))
                link(dve.tensor_reduce(at, t1, AX.X, ALU.min))
                link(dve.tensor_scalar(at, at, 1000.0, None, ALU.add))
                if n == 0:
                    link(dve.tensor_scalar(t1, ii, at, -4.0, ALU.is_equal, ALU.mult))
                    link(dve.tensor_tensor(rw, rw, t1, ALU.add))
            link(dve.tensor_copy(e.pick[0:1, 0:1], i1))
            link(dve.tensor_copy(e.pick[0:1, 1:2], i2))
            link(dve.tensor_tensor(e2, v2, v1, ALU.subtract))
            dve.wait_ge(a, 8)
            link(dve.tensor_scalar(w1, e2, 1.0, None, ALU.add))
            link(dve.reciprocal(pair[0:1, 0:1], w1))
            link(dve.tensor_tensor(pair[0:1, 1:2], e2, pair[0:1, 0:1], ALU.mult))
            dve.wait_ge(p, 2)
            link(dve.tensor_copy(e.weight[:], e.banks[5][:, 0:2]))

        @block.scalar
        def _(act):
            ex, sm, lg, rw, e2 = eight[1][0:1], one[1][0:1], eight[0][0:1], eight[4][0:1], one[6][0:1]
            act.wait_ge(v, 2)
            act.activation(ss, ss, ACT.Sqrt).then_inc(a, 1)
            act.activation(sv, sv, ACT.Sqrt).then_inc(a, 1)
            act.activation(nf2, nf2, ACT.Sqrt).then_inc(a, 1)
            act.wait_ge(v, 5)
            act.activation(th, nf2, ACT.Tanh).then_inc(a, 1)
            act.wait_ge(v, 8)

            def scaled(it, k):
                i = it * G7 + k
                act.activation(col(e.B, i * D, 64), col(e.B, i * D, 64), ACT.Copy, scale=col(ss, i))
                act.activation(col(e.B, i * D + 64, 192), col(e.B, i * D + 64, 192), ACT.Copy, scale=col(sv_r, i)
                               ).then_inc(gs, 1)

            tile_steps(act, (scaled, 0))
            act.wait_ge(v, MOMENTS + 9)
            act.activation(rstd, rstd, ACT.Sqrt).then_inc(a, 1)
            act.wait_ge(v, MOMENTS + 11)
            xc = e.C[:, :].rearrange("p (c n) -> p c n", c=2)

            def out(it, k):
                i = it * G7 + k
                if k in BY_ACT:
                    act.activation(col(e.B, i * D, D), col(e.A, i * D, D), ACT.Identity, scale=col(rstd, i),
                                   bias=col(nmr, i))
                act.wait_ge(tt, i + 1)
                act.activation(xc[:, :, bass.ds(i * P, P)],
                               b_t[k][:, 0:D].rearrange("p (c n) -> p c n", c=2), ACT.Copy).then_inc(cT, 1)

            tile_steps(act, (out, 0))
            act.wait_ge(v, MOMENTS + 17)
            act.activation(ex, lg, ACT.Exp, accum_out=sm).then_inc(a, 1)
            act.wait_ge(v, MOMENTS + 29)
            act.activation(ex, rw, ACT.Exp, accum_out=sm).then_inc(a, 1)
            act.wait_ge(v, MOMENTS + 46)
            act.activation(e2, e2, ACT.Exp).then_inc(a, 1)

        @block.tensor
        def _(pe):
            def transposed(it, k):
                i = it * G7 + k
                pe.wait_ge(x2, i + 1)
                free(pe, cT, i + 1 - AGO[k])
                for c in range(2):
                    mm = pe.transpose(b_t[k][:, c * P:(c + 1) * P], xs[:, k, c * P:(c + 1) * P], ident[:])
                mm.then_inc(tt, 1)

            def summation(it, k):
                last = isinstance(it, int) and it * G7 + k == NT - 1
                rows = LAST if last else P
                for c in range(2):
                    mm = pe.matmul(b_sum[c][:, 0:1], xs[0:rows, k, c * P:(c + 1) * P], ones[0:rows, 0:1],
                                   start=isinstance(it, int) and it == 0 and k == 0, stop=last)
                mm.then_inc(summed, 1)

            pe.wait_ge(c_rdy, 1)
            tile_steps(pe, (transposed, 0), (summation, 1))
            pe.wait_ge(v, MOMENTS + 13)
            pe.wait_ge(w_ld, 16 * 6)
            for c in range(2):
                mm = pe.matmul(e.banks[4][0:1, 0:NE], sums[:, c:c + 1], wr[:, c], start=(c == 0), stop=(c == 1))
            mm.then_inc(p, 1)
            pe.wait_ge(v, MOMENTS + 49)
            pe.matmul(e.banks[5][:, 0:2], ones[0:1], pair[0:1], start=True, stop=True).then_inc(p, 1)


def phase_experts(nc, e):
    io, ar, S = e.io, e.arena, e.sem
    ar.reset()
    w1 = ar.take(2, 2, FF)
    w2 = ar.take(2, 4, D)
    hT = [ar.take(2, 4, 512) for _ in range(2)]
    b1 = ar.take(2, 4)
    b2 = ar.take(2, D)
    b2c = ar.take(D)
    lng, lnb = ar.take(D), ar.take(D)
    bst, mean, var, rstd, tmp = ar.take(6 * NT), ar.take(8), ar.take(8), ar.take(8), ar.take(8)
    xc = e.C[:, :].rearrange("p (c n) -> p c n", c=2)
    bank_h, bank_o = e.banks[0:4], e.banks[4:8]
    STEPS = NT // 8
    w_ld, w_rdy, v, a = S("ffn_w_ld"), S("ffn_w_ready"), S("ffn_vec"), S("ffn_act")
    h_done, h_rdy, o_done, z_rdy, bs = S("ffn_h"), S("ffn_gelu"), S("ffn_out"), S("z_ready"), S("z_stats")
    xb, n_rdy, g_rdy, o_rdy = S("x1_beta"), S("z_normed"), S("z_gamma"), S("out_ready")
    ST0 = 32 * (NT // G7)
    zb, w1_ld = S("x2_b2"), S("ffn_w1_ld")
    LINKS = MOMENTS + 2

    with nc.Block() as block:
        @block.sync
        def _(sp):
            chosen = [sp.value_load(e.pick[0:1, n:n + 1], min_val=0, max_val=NE - 1) for n in range(2)]
            for n, ex in enumerate(chosen):
                sp.dma_start(w1[:, n], io["ffn1"][bass.ds(ex, 1)].rearrange("o (k p) f -> p (o k) f", p=P)
                             ).then_inc(w1_ld, 16)
            for n, ex in enumerate(chosen):
                sp.dma_start(w2[:, n], io["ffn2"][bass.ds(ex, 1)].rearrange("o (f p) d -> p (o f) d", p=P)
                             ).then_inc(w_ld, 16)
                sp.dma_start(b1[:, n], io["ffb1"][bass.ds(ex, 1)].rearrange("o p f -> p (o f)")).then_inc(w_ld, 16)
                sp.dma_start(b2[:, n], io["ffb2"][bass.ds(ex, 1), :].broadcast_to([P, D])).then_inc(w_ld, 16)
            sp.dma_start(lng, io["ln_g"].broadcast_to([P, D])).then_inc(w_ld, 16)
            sp.dma_start(lnb, io["ln_b"].broadcast_to([P, D])).then_inc(w_ld, 16)
            def store(half, row, tiles):
                sp.dma_start(io["out"][bass.ds(row * P, tiles * P), :].rearrange("(t p) d -> p t d", p=P),
                             col(e.B, row * D, tiles * D).rearrange("p (t d) -> p t d", d=D)).then_inc(e.stored[half], 16)

            def each(s):
                for h in range(2):
                    sp.wait_ge(o_rdy, 2 * s + (h + 1))
                    store(h, 8 * s + 4 * h, 4)

            steps(sp, STEPS, each)
            sp.wait_ge(o_rdy, 2 * STEPS + 1)
            store(0, NT - 1, 1)
            sp.wait_ge(e.stored[0], ST0 + 16 * (STEPS + 1))
            sp.wait_ge(e.stored[1], ST0 + 16 * STEPS)

        @block.gpsimd
        def _(pool):
            pool.wait_ge(w_ld, 16 * 8)
            pool.wait_ge(w_rdy, 4)
            with pool.Fori(0, NT) as i:
                pool.tensor_tensor(col(e.B, i * D, D), col(e.B, i * D, D), b2c, ALU.add).then_inc(zb, 1)
                pool.tensor_tensor(col(e.A, i * D, D), col(e.A, i * D, D), lnb, ALU.add).then_inc(xb, 1)

        @block.vector
        def _(dve):
            dve.wait_ge(w_ld, 16 * 8)
            for n in range(2):
                dve.tensor_scalar(w2[:, n], w2[:, n], e.weight[:, n:n + 1], None, ALU.mult).then_inc(w_rdy, 1)
            dve.tensor_scalar(b2[:, 0], b2[:, 0], e.weight[:, 0:1], None, ALU.mult).then_inc(w_rdy, 1)
            dve.wait_ge(w_rdy, 3)
            dve.scalar_tensor_tensor(out=b2c, in0=b2[:, 1], scalar=e.weight[:, 1:2], in1=b2[:, 0], op0=ALU.mult,
                                     op1=ALU.add).then_inc(w_rdy, 1)

            def tile(i, j):
                z = col(e.B, i * D, D)
                dve.wait_ge(o_done, i + 1)
                dve.wait_ge(zb, i + 1)
                dve.tensor_tensor(z, bank_o[j % 4][:, 0:D], z, ALU.add).then_inc(z_rdy, 1)
                dve.wait_ge(z_rdy, i + 1)
                dve.bn_stats(col(bst, 6 * i, 6), z).then_inc(bs, 1)

            def normed(s, tiles):
                m = [0]

                def link(ins):
                    m[0] += 1
                    ins.then_inc(v, 1)
                    dve.wait_ge(v, LINKS * s + m[0])

                dve.wait_ge(bs, 8 * s + tiles)
                group = col(bst, s * 48, 6 * tiles).rearrange("p (t c) -> p t c", c=6)
                row_moments(link, dve, group, mean[:, 0:tiles], var[:, 0:tiles], tmp[:, 0:tiles])
                link(dve.tensor_scalar(rstd[:, 0:tiles], var[:, 0:tiles], EPS, None, ALU.add))
                dve.wait_ge(a, s + 1)
                link(dve.reciprocal(rstd[:, 0:tiles], rstd[:, 0:tiles]))
                for k in range(tiles):
                    z = col(e.B, s * (8 * D) + k * D, D)
                    dve.tensor_scalar(z, z, mean[:, k:k + 1], rstd[:, k:k + 1], ALU.subtract, ALU.mult).then_inc(n_rdy, 1)
                dve.wait_ge(n_rdy, 8 * s + tiles)
                z = col(e.B, s * (8 * D), tiles * D)
                zt = z.rearrange("p (t d) -> p t d", d=D)
                dve.tensor_tensor(zt, zt, lng.rearrange("p (o d) -> p o d", o=1).broadcast_to([P, tiles, D]), ALU.mult
                                  ).then_inc(g_rdy, 1)
                dve.wait_ge(g_rdy, s + 1)
                dve.wait_ge(xb, 8 * s + tiles)
                part = min(tiles, 4)
                for h in range(tiles // part):
                    z, x = (col(r, s * (8 * D) + h * part * D, part * D) for r in (e.B, e.A))
                    dve.tensor_tensor(z, z, x, ALU.add).then_inc(o_rdy, 1)

            def each(s):
                for j in range(8):
                    tile(8 * s + j, j)
                normed(s, 8)

            steps(dve, STEPS, each)
            tile(NT - 1, 0)
            normed(STEPS, 1)

        @block.scalar
        def _(act):
            act.wait_ge(w_ld, 16 * 8)

            def gelu(n, s, w, used):
                free(act, o_done, used)
                for m in range(8):
                    x, f = m // 4, m % 4
                    act.wait_ge(h_done, 8 * n + (m + 1))
                    act.activation(hT[s][:, x, f, 0:w], bank_h[m % 4][:, 0:w], ACT.Gelu, bias=b1[:, x, f:f + 1]
                                   ).then_inc(h_rdy, 1)

            def root(s):
                act.wait_ge(v, LINKS * s + (MOMENTS + 1))
                act.activation(rstd, rstd, ACT.Sqrt).then_inc(a, 1)

            gelu(0, 0, 512, 0)
            def each(s):
                for c in range(2):
                    gelu(2 * s + (c + 1), 1 - c, 512, 8 * s + 4 * c)
                root(s)

            steps(act, STEPS - 1, each)
            gelu(2 * STEPS - 1, 1, 512, 8 * (STEPS - 1))
            gelu(2 * STEPS, 0, P, 8 * (STEPS - 1) + 4)
            root(STEPS - 1)
            root(STEPS)

        @block.tensor
        def _(pe):
            def up(n, w):
                for m in range(8):
                    x, f = m // 4, m % 4
                    free(pe, h_rdy, 8 * n + (m - 3) if m > 3 else 8 * n)
                    for k in range(2):
                        mm = pe.matmul(bank_h[m % 4][:, 0:w], w1[:, x, k, f * P:(f + 1) * P],
                                       xc[:, k, bass.ds(n * 512, w)], start=(k == 0), stop=(k == 1))
                    mm.then_inc(h_done, 1)

            def down(n, s, tiles):
                pe.wait_ge(h_rdy, 8 * n + 8)
                free(pe, z_rdy, 4 * n)
                for t in range(tiles):
                    for m in range(8):
                        mm = pe.matmul(bank_o[t][:, 0:D], hT[s][:, m // 4, m % 4, t * P:(t + 1) * P],
                                       w2[:, m // 4, m % 4], start=(m == 0), stop=(m == 7))
                    mm.then_inc(o_done, 1)

            pe.wait_ge(w1_ld, 32)
            up(0, 512)
            pe.wait_ge(w_rdy, 4)
            def each(s):
                for c in range(2):
                    up(2 * s + (c + 1), 512)
                    down(2 * s + c, c, 4)

            steps(pe, STEPS - 1, each)
            up(2 * STEPS - 1, 512)
            down(2 * STEPS - 2, 0, 4)
            up(2 * STEPS, P)
            down(2 * STEPS - 1, 1, 4)
            down(2 * STEPS, 0, 1)


def build(nc, io, upto=99):
    with ExitStack() as ctx:
        e = setup(nc, ctx, io)
        for n, phase in enumerate(PHASES):
            if n < upto:
                phase(nc, e)


PHASES = [phase_nodes, phase_convolve, phase_edges, phase_combine, phase_residual,
          phase_experts]


def _layout(inputs):
    import numpy as _np
    g = {k: _np.asarray(v) for k, v in inputs.items()}

    def feat(a, axis):
        a = _np.moveaxis(a, axis, -1)
        s, v = a[..., :MUL], a[..., MUL:]
        v = v.reshape(v.shape[:-1] + (MUL, 3)).swapaxes(-1, -2).reshape(v.shape)
        return _np.ascontiguousarray(_np.moveaxis(_np.concatenate([s, v], -1), -1, axis))

    def edges(a, pad):
        full = _np.full((NH * HALF * P,) + a.shape[1:], pad, a.dtype)
        full[:E] = a
        return _np.ascontiguousarray(full.reshape((NH, HALF, P) + a.shape[1:]).swapaxes(1, 2))

    x = _np.zeros((NP, D), g["x"].dtype)
    x[:N] = feat(g["x"], 1)
    a8 = edges(g["edge_attr_8"], 0)
    qkv = feat(g["L0_mix_w_qkv"], 1)
    row = lambda a: _np.ascontiguousarray(a.reshape(1, -1))
    zeros = lambda *shape: _np.zeros((P,) + shape, x.dtype)
    w_nodes = zeros(2, D)
    for c, top in enumerate("sv"):
        for h, name in enumerate(("w1", "wsc")):
            w_nodes[:MUL, c, h * P:h * P + MUL] = g[f"L0_gnn_{name}_{top}"]
            w_nodes[MUL:, c, h * P + MUL:(h + 1) * P] = g[f"L0_gnn_{name}_v"]
    w_fc1, w_fc2, w_fc3 = zeros(HALF, P), zeros(P), zeros(2, D)
    for t in range(2):
        half = slice(MUL * t, MUL * (t + 1))
        for q in range(HALF):
            w_fc1[16 * q + 8 * t:16 * q + 8 * t + 8, q, half] = g["L0_gnn_fc_w1"]
        w_fc2[half, half] = g["L0_gnn_fc_w2"]
        w_fc3[half, t] = g["L0_gnn_fc_w3"]
    w_node2 = zeros(4, P)
    for c, r, k, kind, top in ((0, 0, 0, "s", 0), (0, 1, 1, "v", 1), (1, 0, 0, "v", 1), (1, 1, 1, "v", 1),
                               (2, 0, 0, "v", 0), (2, 1, 1, "v", 0), (3, 0, 1, "v", 0), (3, 1, 0, "s", 1)):
        w_node2[MUL * r:MUL * (r + 1), c, MUL * k:MUL * (k + 1)] = \
            g[f"L0_gnn_w2_{kind}"][MUL * top:MUL * (top + 1)]
    w_point = zeros(NCH, P)
    pw = g["L0_mix_w_pw"].reshape(NCH, 4, DIM, DIM).transpose(1, 3, 0, 2)
    for b in range(4):
        w_point[DIM * b:DIM * (b + 1), :, DIM * b:DIM * (b + 1)] = pw[b]
    out = {
        "x": x,
        "src": edges(g["src"], N),
        "dst": edges(g["dst"], 0),
        "sh": edges(g["edge_attr_4"], 0),
        "a8": _np.ascontiguousarray(a8.transpose(0, 2, 3, 1).reshape(NI, P, P)),
        "w_nodes": w_nodes, "w_fc1": w_fc1, "w_fc2": w_fc2, "w_fc3": w_fc3, "w_node2": w_node2, "w_point": w_point,
        "g_s": row(g["L0_gnn_g_s"]), "g_v": row(g["L0_gnn_g_v"]),
        "w_qkv": _np.ascontiguousarray(qkv.transpose(2, 1, 0)),
        "bn_g": _np.ascontiguousarray(g["L0_mix_bn_gamma"].reshape(NCH, P).T),
        "bn_b": _np.ascontiguousarray(g["L0_mix_bn_beta"].reshape(NCH, P).T),
        "w_dw": _np.ascontiguousarray(g["L0_mix_w_dw"].reshape(NCH, P, 5).transpose(2, 1, 0)),
        "w_res": _np.ascontiguousarray(feat(g["L0_mix_w_res"], 0).reshape(D, GROUPS * DIM).T),
        "b_res": row(feat(g["L0_mix_b_res"], 0)),
        "wr": feat(g["L0_ffn_Wr"], 0), "br": row(g["L0_ffn_br"]),
        "ffn1": feat(g["L0_ffn_W1"], 1),
        "ffb1": _np.ascontiguousarray(g["L0_ffn_b1"].reshape(NE, 4, P).swapaxes(1, 2)),
        "ffn2": feat(g["L0_ffn_W2"], 2), "ffb2": feat(g["L0_ffn_b2"], 1),
        "ln_g": row(feat(g["L0_ffn_gamma"], 0)), "ln_b": row(feat(g["L0_ffn_beta"], 0)),
    }
    return out


def _result(out):
    import numpy as _np
    s, v = out[:N, :MUL], out[:N, MUL:]
    v = v.reshape(N, 3, MUL).swapaxes(1, 2).reshape(N, 3 * MUL)
    return _np.ascontiguousarray(_np.concatenate([s, v], 1))


def kernel(**inputs):
    import concourse.bacc as _bacc
    from concourse import mybir as _mybir
    from concourse.bass_utils import run_bass_kernel_spmd as _run

    nc = _bacc.Bacc("TRN2", target_bir_lowering=False, num_devices=1)
    arrays, io = {}, {}
    for name, a in _layout(inputs).items():
        arrays[f"in_{name}_dram"] = a
        io[name] = nc.dram_tensor(f"in_{name}_dram", a.shape, _mybir.dt.from_np(a.dtype), kind="ExternalInput").ap()
    io["out"] = nc.dram_tensor("out_0_dram", (NP, D), _mybir.dt.float32, kind="ExternalOutput").ap()
    build(nc, io)
    r = _run(nc, [arrays], core_ids=[0])
    return _result(r.results[0]["out_0_dram"])
```
